# Optimizing a Trainium2 kernel written in Bass

```python
import numpy as np
import jax
import jax.numpy as jnp

def _softmax(x, axis=-1):
    return jax.nn.softmax(x, axis=axis)

def _gelu(x):
    return jax.nn.gelu(x, approximate=True)

def _silu(x):
    return jax.nn.silu(x)

def _sigmoid(x):
    return jax.nn.sigmoid(x)

def _layernorm(x, axis=-1, eps=1e-05):
    m = jnp.mean(x, axis=axis, keepdims=True)
    v = jnp.var(x, axis=axis, keepdims=True)
    return (x - m) / jnp.sqrt(v + eps)

def _scatter_add(tgt, idx, src, axis=0):
    return tgt.at[idx].add(src)

def _segment_sum(src, seg, n):
    return jax.ops.segment_sum(src, seg, n)
kernel_name = 'mk_prb_d2_jaxref_r4_67f8dc'

def setup_inputs(seed: int=0):
    np.random.seed(seed)
    _w = jnp.asarray

    def _L0_attn_setup():
        import jax, jax.numpy as jnp
        import numpy as np
        import math
        B, SEQ, DIM, HEADS = (1, 512, 512, 8)
        L_INIT = 0.8 - 0.6 * math.exp(-0.3 * 1)
        EPS = 1e-06
        key = jax.random.key(seed)
        ks = jax.random.split(key, 9)
        x = jax.random.normal(ks[0], (B, SEQ, DIM), jnp.float32)
        l_q1 = jax.random.normal(ks[1], (HEADS,), jnp.float32) * 0.1
        l_k1 = jax.random.normal(ks[2], (HEADS,), jnp.float32) * 0.1
        l_q2 = jax.random.normal(ks[3], (HEADS,), jnp.float32) * 0.1
        l_k2 = jax.random.normal(ks[4], (HEADS,), jnp.float32) * 0.1
        s = 1.0 / math.sqrt(DIM)
        wq = jax.random.normal(ks[5], (2 * DIM, DIM), jnp.float32) * s
        wk = jax.random.normal(ks[6], (2 * DIM, DIM), jnp.float32) * s
        wv = jax.random.normal(ks[7], (DIM, DIM), jnp.float32) * s
        wo = jax.random.normal(ks[8], (DIM, DIM), jnp.float32) * s
        return {'x': x, 'l_q1': l_q1, 'l_k1': l_k1, 'l_q2': l_q2, 'l_k2': l_k2, 'wq': wq, 'wk': wk, 'wv': wv, 'wo': wo}
    _L0_attn_in = _L0_attn_setup()

    def _L0_ffn_setup():
        import jax, jax.numpy as jnp
        import numpy as np
        B, S, D, H = (4, 512, 512, 2048)

        def fwht(x):
            orig_shape = x.shape
            n = orig_shape[-1]
            x = x.reshape(-1, n)
            h = 1
            while h < n:
                xb = x.reshape(-1, n // (2 * h), 2, h)
                a = xb[:, :, 0, :]
                b = xb[:, :, 1, :]
                x = jnp.stack([a + b, a - b], axis=2).reshape(-1, n)
                h *= 2
            scale = jnp.asarray(1.0 / np.sqrt(n), dtype=x.dtype)
            return (x * scale).reshape(orig_shape)
        key = jax.random.key(seed)
        kx, k1, k2, k3 = jax.random.split(key, 4)
        x = jax.random.normal(kx, (B, S, D), dtype=jnp.float32)
        W1 = jax.random.normal(k1, (H, D), dtype=jnp.float32) * (1.0 / np.sqrt(D))
        W2 = jax.random.normal(k2, (D, H), dtype=jnp.float32) * (1.0 / np.sqrt(H))
        W3 = jax.random.normal(k3, (H, D), dtype=jnp.float32) * (1.0 / np.sqrt(D))
        return {'x': x, 'W1': W1, 'W2': W2, 'W3': W3}
    _L0_ffn_in = _L0_ffn_setup()

    def _L1_attn_setup():
        import jax, jax.numpy as jnp
        import numpy as np
        B, S, D = (2, 1024, 512)
        EPS = 1e-05

        def rmsnorm(h, scale, eps=EPS):
            hf = h.astype(jnp.float32)
            hf = hf * jax.lax.rsqrt(jnp.mean(hf * hf, axis=-1, keepdims=True) + eps)
            return hf.astype(h.dtype) * scale
        key = jax.random.key(seed)
        kx, kr, kf, kc, ko = jax.random.split(key, 5)
        sc = 1.0 / np.sqrt(D).astype(np.float32)
        return {'x': jax.random.normal(kx, (B, S, D), jnp.float32), 'Wr': jax.random.normal(kr, (D, D), jnp.float32) * sc, 'Wf': jax.random.normal(kf, (D, D), jnp.float32) * sc, 'Wc': jax.random.normal(kc, (D, D), jnp.float32) * sc, 'Wo': jax.random.normal(ko, (D, D), jnp.float32) * sc, 'ln_scale': jnp.ones((D,), jnp.float32)}
    _L1_attn_in = _L1_attn_setup()

    def _L1_ffn_setup():
        import jax, jax.numpy as jnp
        import numpy as np
        B, S, H = (2, 256, 512)
        E, K, F = (64, 8, 192)
        CAP = 128
        key = jax.random.key(seed)
        k1, k2, k3, k4, k5 = jax.random.split(key, 5)
        scale_h = 1.0 / np.sqrt(H)
        scale_f = 1.0 / np.sqrt(F)
        return {'hidden_states': jax.random.normal(k1, (B, S, H), jnp.float32), 'router_w': jax.random.normal(k2, (E, H), jnp.float32) * scale_h, 'w_gate': jax.random.normal(k3, (E, H, F), jnp.float32) * scale_h, 'w_up': jax.random.normal(k4, (E, H, F), jnp.float32) * scale_h, 'w_down': jax.random.normal(k5, (E, F, H), jnp.float32) * scale_f}
    _L1_ffn_in = _L1_ffn_setup()
    _d = {'L0_attn_x': _L0_attn_in['x'], 'L0_attn_l_q1': _L0_attn_in['l_q1'], 'L0_attn_l_k1': _L0_attn_in['l_k1'], 'L0_attn_l_q2': _L0_attn_in['l_q2'], 'L0_attn_l_k2': _L0_attn_in['l_k2'], 'L0_attn_wq': _L0_attn_in['wq'], 'L0_attn_wk': _L0_attn_in['wk'], 'L0_attn_wv': _L0_attn_in['wv'], 'L0_attn_wo': _L0_attn_in['wo'], 'L0_ffn_W1': _L0_ffn_in['W1'], 'L0_ffn_W2': _L0_ffn_in['W2'], 'L0_ffn_W3': _L0_ffn_in['W3'], 'L1_attn_Wr': _L1_attn_in['Wr'], 'L1_attn_Wf': _L1_attn_in['Wf'], 'L1_attn_Wc': _L1_attn_in['Wc'], 'L1_attn_Wo': _L1_attn_in['Wo'], 'L1_attn_ln_scale': _L1_attn_in['ln_scale'], 'L1_ffn_router_w': _L1_ffn_in['router_w'], 'L1_ffn_w_gate': _L1_ffn_in['w_gate'], 'L1_ffn_w_up': _L1_ffn_in['w_up'], 'L1_ffn_w_down': _L1_ffn_in['w_down']}
    _x0 = _d['L0_attn_x']
    _d['L0_attn_x'] = jax.random.normal(jax.random.fold_in(jax.random.key(seed), 1), (4, 1024, 512), dtype=_x0.dtype)
    del _x0
    return _d

def reference(L0_attn_x, L0_attn_l_q1, L0_attn_l_k1, L0_attn_l_q2, L0_attn_l_k2, L0_attn_wq, L0_attn_wk, L0_attn_wv, L0_attn_wo, L0_ffn_W1, L0_ffn_W2, L0_ffn_W3, L1_attn_Wr, L1_attn_Wf, L1_attn_Wc, L1_attn_Wo, L1_attn_ln_scale, L1_ffn_router_w, L1_ffn_w_gate, L1_ffn_w_up, L1_ffn_w_down):

    def _L0_attn_ref(x, l_q1, l_k1, l_q2, l_k2, wq, wk, wv, wo):
        import jax, jax.numpy as jnp
        import numpy as np
        import math
        B, SEQ, DIM, HEADS = (1, 512, 512, 8)
        L_INIT = 0.8 - 0.6 * math.exp(-0.3 * 1)
        EPS = 1e-06
        b, s, d = x.shape
        nh = HEADS
        lmbda = jnp.exp(jnp.sum(l_q1 * l_k1)) - jnp.exp(jnp.sum(l_q2 * l_k2)) + L_INIT
        q = jnp.einsum('bsd,od->bso', x, wq)
        k = jnp.einsum('bsd,od->bso', x, wk)
        v = jnp.einsum('bsd,od->bso', x, wv)

        def split_heads(t):
            return t.reshape(b, s, nh, -1).transpose(0, 2, 1, 3)
        q, k, v = map(split_heads, (q, k, v))

        def prep(t):
            dh = t.shape[-1] // 2
            t = t.reshape(b, nh, s, 2, dh)
            return t.transpose(0, 1, 3, 2, 4).reshape(b, nh * 2, s, dh)
        q, k = (prep(q), prep(k))
        dh = q.shape[-1]
        scores = jnp.einsum('bhqd,bhkd->bhqk', q, k) / math.sqrt(dh)
        causal = jnp.triu(jnp.full((s, s), -jnp.inf, dtype=scores.dtype), 1)
        attn = jax.nn.softmax((scores + causal[None, None]).astype(jnp.float32), axis=-1).astype(scores.dtype)
        attn = attn[:, :nh] - attn[:, nh:] * lmbda
        out = jnp.einsum('bhqk,bhkd->bhqd', attn, v)
        dv = out.shape[-1]
        o = out.reshape(b, nh, s, nh, dv // nh)
        o32 = o.astype(jnp.float32)
        o = (o32 * jax.lax.rsqrt(jnp.mean(o32 * o32, axis=-1, keepdims=True) + EPS)).astype(o.dtype)
        o = o.reshape(b, nh, s, dv) * (1.0 - L_INIT)
        o = o.transpose(0, 2, 1, 3).reshape(b, s, nh * dv)
        return jnp.einsum('bsd,od->bso', o, wo)

    def _L0_ffn_ref(x, W1, W2, W3):
        import jax, jax.numpy as jnp
        import numpy as np
        B, S, D, H = (4, 512, 512, 2048)

        def fwht(x):
            orig_shape = x.shape
            n = orig_shape[-1]
            x = x.reshape(-1, n)
            h = 1
            while h < n:
                xb = x.reshape(-1, n // (2 * h), 2, h)
                a = xb[:, :, 0, :]
                b = xb[:, :, 1, :]
                x = jnp.stack([a + b, a - b], axis=2).reshape(-1, n)
                h *= 2
            scale = jnp.asarray(1.0 / np.sqrt(n), dtype=x.dtype)
            return (x * scale).reshape(orig_shape)
        up_gate = jnp.einsum('bsd,hd->bsh', x, W1)
        up_lin = jnp.einsum('bsd,hd->bsh', x, W3)
        hidden = jax.nn.silu(up_gate) * up_lin
        hidden = fwht(hidden)
        out = jnp.einsum('bsh,dh->bsd', hidden, W2)
        return out

    def _L1_attn_ref(x, Wr, Wf, Wc, Wo, ln_scale):
        import jax, jax.numpy as jnp
        import numpy as np
        B, S, D = (2, 1024, 512)
        EPS = 1e-05

        def rmsnorm(h, scale, eps=EPS):
            hf = h.astype(jnp.float32)
            hf = hf * jax.lax.rsqrt(jnp.mean(hf * hf, axis=-1, keepdims=True) + eps)
            return hf.astype(h.dtype) * scale
        r = jax.nn.silu(x @ Wr)
        f = jax.nn.sigmoid(x @ Wf)
        c = jax.nn.silu(x @ Wc)

        def combine(a, b):
            fa, ca = a
            fb, cb = b
            return (fa * fb, fb * ca + (1.0 - fb) * cb)
        _, h = jax.lax.associative_scan(combine, (f, c), axis=1)
        y = r * rmsnorm(h, ln_scale) @ Wo
        return y

    def _L1_ffn_ref(hidden_states, router_w, w_gate, w_up, w_down):
        import jax, jax.numpy as jnp
        import numpy as np
        B, S, H = (2, 256, 512)
        E, K, F = (64, 8, 192)
        CAP = 128
        b, s, h = hidden_states.shape
        T = b * s
        xf = hidden_states.reshape(T, h)
        logits = xf @ router_w.T
        scores = jax.nn.softmax(logits.astype(jnp.float32), axis=-1)
        topk_w, topk_idx = jax.lax.top_k(scores, K)
        topk_w = topk_w / (topk_w.sum(axis=-1, keepdims=True) + 1e-20)
        slot_expert = topk_idx.reshape(-1)
        slot_token = jnp.repeat(jnp.arange(T), K)
        onehot = jax.nn.one_hot(slot_expert, E, dtype=jnp.int32)
        pos = (jnp.cumsum(onehot, axis=0) * onehot).sum(-1) - 1
        valid = pos < CAP
        dest = jnp.where(valid, slot_expert * CAP + pos, E * CAP)
        buf = jnp.zeros((E * CAP + 1, h), xf.dtype).at[dest].set(xf[slot_token])
        xb = buf[:E * CAP].reshape(E, CAP, h)
        gate = jnp.einsum('ech,ehf->ecf', xb, w_gate)
        up = jnp.einsum('ech,ehf->ecf', xb, w_up)
        hmid = jax.nn.silu(gate) * up
        yb = jnp.einsum('ecf,efh->ech', hmid, w_down).reshape(E * CAP, h)
        yb = jnp.concatenate([yb, jnp.zeros((1, h), yb.dtype)], axis=0)
        slot_out = yb[dest] * topk_w.reshape(-1)[:, None].astype(yb.dtype)
        out = jnp.zeros((T, h), yb.dtype).at[slot_token].add(slot_out)
        return out.reshape(b, s, h)
    x = L0_attn_x
    xn = _layernorm(x, axis=-1)
    x = x + _L0_attn_ref(xn, L0_attn_l_q1, L0_attn_l_k1, L0_attn_l_q2, L0_attn_l_k2, L0_attn_wq, L0_attn_wk, L0_attn_wv, L0_attn_wo) + _L0_ffn_ref(xn, L0_ffn_W1, L0_ffn_W2, L0_ffn_W3)
    xn = _layernorm(x, axis=-1)
    x = x + _L1_attn_ref(xn, L1_attn_Wr, L1_attn_Wf, L1_attn_Wc, L1_attn_Wo, L1_attn_ln_scale) + _L1_ffn_ref(xn, L1_ffn_router_w, L1_ffn_w_gate, L1_ffn_w_up, L1_ffn_w_down)
    return x

_drawn_inputs = setup_inputs


def setup_inputs(seed=0):
    import zlib

    import numpy as np

    out = dict(_drawn_inputs(seed))
    spreads = {'L1_attn_ln_scale': (1.0, 0.2)}
    factors = {'L0_attn_l_k2': 8.0}
    for name, (base, spread) in spreads.items():
        noise = np.random.default_rng([zlib.crc32(name.encode()), seed]).standard_normal(out[name].shape)
        drawn = base * np.exp(spread * noise) if base else spread * noise
        out[name] = jnp.asarray(drawn.astype(out[name].dtype))
    for name, factor in factors.items():
        out[name] = (out[name] * factor).astype(out[name].dtype)
    return out
```

```python
import concourse.bass as bass
from concourse import mybir
from contextlib import ExitStack
import math
import numpy as np

F32 = mybir.dt.float32
F32R = mybir.dt.float32r
BF16 = mybir.dt.bfloat16
I32 = mybir.dt.int32
ALU = mybir.AluOpType
ACT = mybir.ActivationFunctionType
AX = mybir.AxisListType

P = 128
D = 512
KT = D // P
S = 1024
NT = S // P
HEADS = 8
DH = D // HEADS
HID = 2048
E = 64
TOPK = 8
CAP = 128
FE = 192
L_INIT = 0.8 - 0.6 * math.exp(-0.3 * 1)
LN_EPS = 1e-5
ATT_EPS = 1e-6
RMS_EPS = 1e-5
MASKED = -1e30
ROW = D + E


class Links:

    def __init__(self, eng, sem, per_turn, turn, passed=None):
        self.eng, self.sem, self.per_turn, self.turn, self.n = eng, sem, per_turn, turn, 0
        self.passed = passed

    def __call__(self, ins):
        self.n += 1
        ins.then_inc(self.sem, 1)
        self.eng.wait_ge(self.sem, self.turn * self.per_turn + self.n)
        if self.passed:
            self.eng.sem_inc(self.passed, 1)

    def close(self):
        assert self.n == self.per_turn, (self.n, self.per_turn)


def three_products(pe, out, w, x, first, last):
    pe.matmul(out, w[0], x[0], start=first, stop=False)
    pe.matmul(out, w[0], x[1], start=False, stop=False)
    return pe.matmul(out, w[1], x[0], start=False, stop=last)


def hadamard_w2(nc, W2T, had, w2p):
    NC = HID // P
    with ExitStack() as ctx:
        def sb(name, shape, dt=F32):
            return ctx.enter_context(nc.sbuf_tensor(name, shape, dt))

        def sem(name):
            return ctx.enter_context(nc.semaphore(name))

        ping = sb("had_ping", [P, NC, D])
        pong = sb("had_pong", [P, NC, D])
        h_f = sb("had_f", [P, P])
        h_r = sb("had_r", [P, P], F32R)
        hi = sb("had_hi", [P, 2, D], F32R)
        lo = sb("had_lo", [P, 2, D], F32R)
        out = sb("had_out", [P, 2, D])
        ps = ctx.enter_context(nc.psum_tensor("had_ps", [P, 2, D], F32))
        s_in, s_h, s_sum, s_dif = sem("had_in"), sem("had_hr"), sem("had_sum"), sem("had_dif")
        s_hi, s_lo, s_mm, s_out = sem("had_hi_done"), sem("had_lo_done"), sem("had_mm"), sem("had_scaled")
        s_st = [sem("had_store0"), sem("had_store1")]
        bufs = [ping, pong]
        src_v = W2T.rearrange("(c p) n -> p c n", p=P)
        dst_v = w2p.rearrange("(c p) n -> c p n", p=P)

        with nc.Block() as block:
            @block.sync
            def _(sp):
                sp.dma_start(ping[:, :, :], src_v).then_inc(s_in, 16)
                sp.dma_start(h_f[:, :], had).then_inc(s_in, 16)
                for c in range(NC):
                    sp.wait_ge(s_out, c + 1)
                    sp.dma_start(dst_v[c], out[:, c % 2, :]).then_inc(s_st[c % 2], 16)
                sp.wait_ge(s_st[0], 16 * NC // 2)
                sp.wait_ge(s_st[1], 16 * NC // 2)

            def halves(level):
                h = 1 << level
                a, b = (x[:, :, :].rearrange("p (g two h) n -> p g two (h n)", two=2, h=h)
                        for x in (bufs[level % 2], bufs[(level + 1) % 2]))
                return a, b

            @block.vector
            def _(dve):
                dve.wait_ge(s_in, 32)
                for level in range(4):
                    a, b = halves(level)
                    if level:
                        dve.wait_ge(s_dif, level)
                        dve.wait_ge(s_sum, level)
                    dve.tensor_tensor(b[:, :, 0], a[:, :, 0], a[:, :, 1], ALU.add).then_inc(s_sum, 1)
                for c in range(NC):
                    dve.wait_ge(s_hi, c + 1)
                    dve.tensor_tensor(lo[:, c % 2, :], ping[:, c, :], hi[:, c % 2, :].bitcast(F32), ALU.subtract)\
                       .then_inc(s_lo, 1)

            @block.gpsimd
            def _(pool):
                pool.wait_ge(s_in, 32)
                for level in range(4):
                    a, b = halves(level)
                    if level:
                        pool.wait_ge(s_sum, level)
                        pool.wait_ge(s_dif, level)
                    pool.tensor_tensor(b[:, :, 1], a[:, :, 0], a[:, :, 1], ALU.subtract).then_inc(s_dif, 1)

            @block.scalar
            def _(act):
                act.wait_ge(s_in, 32)
                act.activation(h_r[:, :], h_f[:, :], ACT.Copy).then_inc(s_h, 1)
                act.wait_ge(s_sum, 4)
                act.wait_ge(s_dif, 4)

                def scaled(c):
                    act.wait_ge(s_mm, c + 1)
                    if c >= 2:
                        act.wait_ge(s_st[c % 2], 16 * (c // 2))
                    act.activation(out[:, c % 2, :], ps[:, c % 2, :], ACT.Copy, scale=1.0 / math.sqrt(HID))\
                       .then_inc(s_out, 1)

                for c in range(NC):
                    if c >= 2:
                        scaled(c - 2)
                    act.activation(hi[:, c % 2, :], ping[:, c, :], ACT.Copy).then_inc(s_hi, 1)
                scaled(NC - 2)
                scaled(NC - 1)

            @block.tensor
            def _(pe):
                pe.wait_ge(s_h, 1)
                for c in range(NC):
                    pe.wait_ge(s_lo, c + 1)
                    if c >= 2:
                        pe.wait_ge(s_out, c - 1)
                    pe.matmul(ps[:, c % 2, :], h_r[:, :], hi[:, c % 2, :], start=True, stop=False)
                    pe.matmul(ps[:, c % 2, :], h_r[:, :], lo[:, c % 2, :], start=False, stop=True).then_inc(s_mm, 1)


def attention(nc, x, wqk, wvT, woT, lam, ident_d, mask_d, xth_d, xtl_d, x1, batches):
    SUBS = 2
    GQ = 2 * P
    NG = S // GQ
    STEPS = HEADS * NT
    LAG = 2
    U = NT * SUBS
    TH = sum(-(-2 * (g + 1) // 4) for g in range(NG)) * 2
    TTK = 2 * NT + HEADS * TH + 2 * NT
    TTH = TTK - NT
    LOADS = HEADS + 2
    QUARTERS = [(1, 0), (0, 0), (1, 1), (0, 1)]
    with ExitStack() as ctx:
        def sb(name, shape, dt=F32):
            return ctx.enter_context(nc.sbuf_tensor(name, shape, dt))

        def pb(name, shape):
            return ctx.enter_context(nc.psum_tensor(name, shape, F32))

        def sem(name):
            return nc.alloc_semaphore(name)

        SC = pb("score_ps", [P, 4, D])
        TT = pb("turn_ps", [P, 2, D])
        PV = pb("pv_ps", [P, D])
        PJ = pb("qk_ps", [P, D])

        xT = [sb("xT_hi", [P, KT, S], F32R), sb("xT_lo", [P, KT, S], F32R)]
        W = [sb("wvo_hi", [P, KT, D], F32R), sb("wvo_lo", [P, KT, D], F32R)]
        V = sb("values", [P, NT, HEADS, 2 * DH], F32R)
        Q = [[sb(f"q_{s}{r}", [P, S], F32R) for s in "ab"] for r in range(2)]
        K = sb("k_all", [P, 2, 4, S], F32R)
        w_in = sb("weight_in", [P, KT * 2 * P])
        w_in_qk = w_in[:, :].rearrange("p (k n) -> p k n", k=KT)
        w_in_wo = w_in[:, :].rearrange("p (k n) -> p k n", n=D)
        wq = [sb("wqk_hi", [P, KT, 2 * P], F32R), sb("wqk_lo", [P, KT, 2 * P], F32R)]
        AT = [sb("attT_hi", [P, NT, GQ], F32R), sb("attT_lo", [P, NT, GQ], F32R)]
        PR = sb("probs", [P, 3, SUBS, S])
        xn = PR[:, 0, 0, :].rearrange("p (t n) -> p t n", t=2)
        sq = PR[:, 0:2, :, :].rearrange("p a s (t n) -> p (a s t) n", n=D)
        wv_in = PR[:, 1, :, :].rearrange("p s (t n) -> p (s t) n", n=D)
        x1_sb = PR[:, 2, 0, :].rearrange("p (t n) -> p t n", t=2)
        grp = PR[:, 2, 1, 0:D].rearrange("p (t n) -> p t n", n=D // 8)
        inv = PR[:, 2, 1, D:2 * D].rearrange("p (t n) -> p t n", n=D // 8)
        O = sb("heads_out", [P, NT, D])
        x_in = sb("x_in", [P, 2, D])
        OT = sb("outT", [P, GQ])
        ident = sb("ident_sb", [P, P])
        fold = sb("fold", [P, DH])
        identb = sb("identb", [P, P], BF16)
        maskf = O[:, 0, :]
        mask = sb("maskb", [P, 2, GQ], BF16)
        lam_sb = sb("lam_sb", [P, 4, HEADS])
        lam_p = sb("lam_prod", [P, 2, HEADS])
        lam_s = sb("lam_sum", [P, 4])
        stats = sb("ln_stats", [P, 6])
        mv = sb("ln_mv", [P, 2, 2])
        rstd = sb("ln_rstd", [P, 2])
        nmax = sb("neg_max", [P, U])
        sums = sb("exp_sums", [P, NT, HEADS, SUBS])
        rsum = sb("sum_recip", [P, NT, HEADS, SUBS])
        comb = sb("comb", [P, 4])
        neg_half = sb("neg_half", [P, 1])
        newton = sb("newton", [P, NT // 2, D // 8])

        s_wv, s_c, s_fold = sem("a_wv_in"), sem("a_const"), sem("a_fold")
        s_wvh, s_wvl, s_wfree, s_cast = sem("a_wv_high"), sem("a_wv_low"), sem("a_wvo_free"), sem("a_cast")
        s_x = [sem("a_x0"), sem("a_x1")]
        s_xfree, s_xn, s_prime = sem("a_xfree"), sem("a_xn"), sem("a_prime")
        s_xts = sem("a_xt_stored")
        s_ttf, s_tth, s_ttfree = sem("a_tt_filled"), sem("a_tt_high"), sem("a_tt_free")
        s_win, s_wqh, s_wql = sem("a_win"), sem("a_wq_high"), sem("a_wq_low")
        s_pjf, s_pjh, s_pjfree, s_kdup = sem("a_pj_filled"), sem("a_pj_high"), sem("a_pj_free"), sem("a_kdup")
        s_scf, s_scfree = sem("a_sc_filled"), sem("a_sc_free")
        s_max, s_rs, s_cc = sem("a_max"), sem("a_recip"), sem("a_comb_factor")
        s_comb, s_scaled = sem("a_comb"), sem("a_scaled")
        s_pv, s_ot, s_ox, s_oxf = sem("a_pv"), sem("a_ot"), sem("a_ox"), sem("a_ox_free")
        s_var, s_root, s_half_set = sem("a_var"), sem("a_root"), sem("a_half_set")
        s_passed = sem("a_passed")
        s_dv, s_sq, s_ms, s_sqrt = sem("a_dve_chain"), sem("a_squares"), sem("a_mean_sq"), sem("a_sqrt")
        s_xn2 = sem("a_heads_normed")
        s_x1, s_st = sem("a_x1_ready"), [sem("a_st0"), sem("a_st1")]

        def width(i):
            return GQ * (i % NT // 2 + 1)

        def bank(u):
            return u % 4 if u < NT else 2 * (u % 2)

        def score_tile(u):
            n = width(u // SUBS)
            return SC[:, bank(u), 0:n] if u < NT else \
                SC[:, bank(u):bank(u) + 2, :].rearrange("p b n -> p (b n)")[:, 0:n]

        def bank_before(u):
            mine = {bank(u % U)} | ({bank(u % U) + 1} if u % U >= NT else set())
            for v in range(u - 1, -1, -1):
                if mine & ({bank(v % U)} | ({bank(v % U) + 1} if v % U >= NT else set())):
                    return v

        def blocks(i):
            n = width(i) // P
            return [(k, min(4, n - k)) for k in range(0, n, 4)]

        def turn_use(i):
            return 2 * NT + i // NT * TH + sum(len(blocks(j)) for j in range(i % NT))

        def pair_use(base, t, second):
            return base + (0 if t == 0 and not second else (2 * t + 2 if second and t < NT - 1 else
                           2 * t + 1 if second else 2 * t - 1))

        def x_use(t):
            return pair_use(0, t, False)

        def v_use(t):
            return pair_use(0, t, True)

        def o_use(t):
            return pair_use(2 * NT + HEADS * TH, t, False)

        def wo_use(t):
            return pair_use(2 * NT + HEADS * TH, t, True)

        def group_at(i, lag):
            return (i - lag) // 2 if i >= lag and (i - lag) % 2 == 0 and (i - lag) // 2 < HEADS * NG else None

        FIRST_QUARTERS = {3: (0,), 4: (1,), 7: (2, 3)}
        lo64, hi64 = slice(0, DH), slice(DH, P)

        with nc.Block() as block:
            @block.sync
            def _(sp):
                sp.dma_start(ident[:, :], ident_d).then_inc(s_c, 16)
                sp.dma_start(maskf, mask_d).then_inc(s_c, 16)
                sp.dma_start(lam_sb[:, :, :], lam).then_inc(s_c, 16)
                sp.dma_start(w_in_qk, wqk[0]).then_inc(s_win, 16)
                sp.dma_start(wv_in, wvT).then_inc(s_wv, 16)
                with sp.Fori(0, batches) as b:
                    def load_x(n):
                        t = n % NT
                        sp.wait_ge(s_xfree, b * 2 * NT + n + 1)
                        sp.dma_start(x_in[:, t % 2, :], x[bass.ds(b * S + t * P, P), :]).then_inc(s_x[t % 2], 16)

                    def load_wqk(h):
                        sp.wait_ge(s_wql, b * LOADS + h)
                        sp.dma_start(w_in_qk, wqk[h % HEADS]).then_inc(s_win, 16)

                    def double_keys(h, half):
                        sp.wait_ge(s_pjfree, b * 4 * HEADS + 4 * h + 2 * half + 1 + 1)
                        c = slice(half * D, (half + 1) * D)
                        for s, src, dst in ((0, lo64, hi64), (1, hi64, lo64)):
                            for part in range(2):
                                v = K[:, h % 2, 2 * s + part, c].bitcast(F32)
                                sp.dma_start(v[dst, :], v[src, :]).then_inc(s_kdup, 16)

                    for t in range(2):
                        load_x(t)
                    load_wqk(1)
                    for t in range(2, NT):
                        load_x(t)
                    double_keys(0, 0)
                    sp.wait_ge(s_ttfree, b * TTK + 2 + x_use(NT - 1) + 1)
                    for part, dram in ((0, xth_d), (1, xtl_d)):
                        for half in range(2):
                            sp.dma_start(dram[bass.ds(b * 2 + half, 1)].rearrange("o p k n -> (o p) k n"),
                                         xT[part][:, :, half * D:(half + 1) * D].bitcast(F32)).then_inc(s_xts, 16)
                    double_keys(0, 1)
                    for hd in range(HEADS - 1):
                        load_wqk(hd + 2)
                        double_keys(hd + 1, 0)
                        double_keys(hd + 1, 1)
                    for n in range(NT, NT + 2):
                        load_x(n)
                    for half in range(2):
                        sp.wait_ge(s_wql, b * LOADS + HEADS + 1 + half)
                        sp.dma_start(w_in_wo, woT[:, 2 * half:2 * half + 2, :]).then_inc(s_win, 16)
                    sp.wait_ge(s_ms, 2 * b + 2)
                    sp.dma_start(wv_in, wvT).then_inc(s_wv, 16)
                    for t in range(NT):
                        if t + 2 < NT:
                            load_x(NT + t + 2)
                        sp.wait_ge(s_x1, b * NT + t + 1)
                        sp.dma_start(x1[bass.ds(b * S + t * P, P), :], x1_sb[:, t % 2, :]).then_inc(s_st[t % 2], 16)
                sp.wait_ge(s_xts, 64 * batches)
                for i in range(2):
                    sp.wait_ge(s_st[i], 16 * NT // 2 * batches)
                sp.wait_ge(s_wv, 16 * (batches + 1))
                sp.wait_ge(s_win, 16 * (1 + LOADS * batches))

            @block.vector
            def _(dve):
                for _i in range(2):
                    dve.sem_inc(s_xfree, 1)
                    dve.sem_inc(s_ttfree, 1)
                dve.sem_inc(s_oxf, 1)
                dve.sem_inc(s_pjfree, 1)
                dve.sem_inc(s_wfree, 1)
                dve.wait_ge(s_c, 48)
                dve.tensor_tensor(fold[:, :], ident[:, 0:DH], ident[:, DH:P], ALU.add).then_inc(s_fold, 1)
                link = Links(dve, s_prime, 4, 0)
                link(dve.tensor_tensor(lam_p[:, :, :], lam_sb[:, 0:4:2, :], lam_sb[:, 1:4:2, :], ALU.mult))
                link(dve.tensor_reduce(lam_s[:, 0:2], lam_p[:, :, :], AX.X, ALU.add))
                dve.wait_ge(s_cast, 3)
                link(dve.tensor_tensor(lam_s[:, 2:3], lam_s[:, 1:2], lam_s[:, 0:1], ALU.subtract))
                link(dve.tensor_scalar(lam_s[:, 3:4], lam_s[:, 2:3], L_INIT, None, ALU.subtract))
                link.close()

                with dve.Fori(0, batches) as b:
                    link = Links(dve, s_dv, 2 * NT + NT + 2 * 5, b, passed=s_passed)

                    def low(use, high_use, out, in_, hi):
                        dve.wait_ge(s_tth, b * TTH + high_use + 1)
                        dve.tensor_tensor(out, in_, hi.bitcast(F32), ALU.subtract).then_inc(s_ttfree, 1)

                    def ln_stats(t):
                        dve.wait_ge(s_x[t % 2], 16 * (b * NT + t // 2 + 1))
                        link(dve.bn_stats(stats[:, :], x_in[:, t % 2, :]))
                        link(dve.bn_aggr(mv[:, t % 2, :], stats[:, :]))
                        dve.tensor_scalar(rstd[:, t % 2:t % 2 + 1], mv[:, t % 2, 1:2], LN_EPS, None, ALU.add)\
                           .then_inc(s_var, 1)

                    def ln(t):
                        dve.wait_ge(s_root, b * NT + t + 1)
                        if t >= 2:
                            dve.wait_ge(s_ttf, b * TTK + x_use(t - 2) + 1)
                        dve.tensor_scalar(xn[:, t % 2, :], x_in[:, t % 2, :], mv[:, t % 2, 0:1],
                                          rstd[:, t % 2:t % 2 + 1], ALU.subtract, ALU.mult).then_inc(s_xn, 1)
                        dve.wait_ge(s_xn, b * NT + t + 1)
                        dve.sem_inc(s_xfree, 1)

                    def proj_low(h, quarter):
                        m, half = QUARTERS[quarter]
                        c, r = slice(half * D, (half + 1) * D), h % 2
                        dve.wait_ge(s_pjh, b * 4 * HEADS + 4 * h + quarter + 1)
                        if m == 0:
                            dve.scalar_tensor_tensor(Q[r][0][hi64, c], PJ[lo64, :], 0.125,
                                                     Q[r][0][lo64, c].bitcast(F32), ALU.mult, ALU.subtract)
                            ins = dve.scalar_tensor_tensor(Q[r][1][lo64, c], PJ[hi64, :], 0.125,
                                                           Q[r][1][hi64, c].bitcast(F32), ALU.mult, ALU.subtract)
                        else:
                            for s, rows in ((0, lo64), (1, hi64)):
                                ins = dve.tensor_tensor(K[rows, r, 2 * s + 1, c], PJ[rows, :],
                                                        K[rows, r, 2 * s, c].bitcast(F32), ALU.subtract)
                        ins.then_inc(s_pjfree, 1)

                    dve.wait_ge(s_wvh, b + 1)
                    dve.tensor_tensor(W[1][:, :, :], wv_in, W[0][:, :, :].bitcast(F32), ALU.subtract)\
                       .then_inc(s_wvl, 1)
                    ln_stats(0)
                    ln_stats(1)
                    ln(0)
                    for t in range(NT):
                        if t + 2 < NT:
                            ln_stats(t + 2)
                        if t + 1 < NT:
                            ln(t + 1)
                        low(x_use(t), x_use(t), xT[1][:, :, t * P:(t + 1) * P],
                            TT[:, x_use(t) % 2, :].rearrange("p (k n) -> p k n", k=KT),
                            xT[0][:, :, t * P:(t + 1) * P])
                        for v in ([t - 1] if t else []) + ([t] if t == NT - 1 else []):
                            low(v_use(v), v_use(v), V[:, v, :, DH:2 * DH],
                                TT[:, v_use(v) % 2, :].rearrange("p (h n) -> p h n", h=HEADS), V[:, v, :, 0:DH])
                            for quarter in FIRST_QUARTERS.get(v, ()):
                                proj_low(0, quarter)

                    for i in range(STEPS + LAG + 2):
                        hd, j = divmod(i, NT)

                        def maximum(s):
                            u = hd * U + 2 * j + s
                            dve.wait_ge(s_scf, b * HEADS * U + u + 1)
                            sc = score_tile(u % U)
                            dve.tensor_reduce(nmax[:, u % U:u % U + 1], sc, AX.X, ALU.max, negate=True)\
                               .then_inc(s_max, 1)

                        def map_low(part):
                            if LAG <= i < STEPS + LAG and part < len(blocks(i - LAG)):
                                use, t = turn_use(i - LAG) + part, i % 2
                                k, nb = blocks(i - LAG)[part]
                                low(use, use, AT[1][:, k:k + nb, t * P:(t + 1) * P],
                                    TT[:, use % 2, 0:nb * P].rearrange("p (k n) -> p k n", k=nb),
                                    AT[0][:, k:k + nb, t * P:(t + 1) * P])

                        def reciprocals():
                            if 1 <= i <= STEPS:
                                dve.wait_ge(s_scfree, b * HEADS * U + 2 * i)
                                dve.reciprocal(rsum[:, (i - 1) % NT, (i - 1) // NT, :],
                                               sums[:, (i - 1) % NT, (i - 1) // NT, :]).then_inc(s_rs, 1)

                        def factor():
                            if 1 <= i <= STEPS:
                                h1, j1 = divmod(i - 1, NT)
                                dve.wait_ge(s_rs, b * STEPS + i)
                                dve.scalar_tensor_tensor(comb[:, j1 % 4:j1 % 4 + 1], sums[:, j1, h1, 0:1],
                                                         lam_s[:, 3:4], rsum[:, j1, h1, 1:2], ALU.mult, ALU.mult)\
                                   .then_inc(s_cc, 1)

                        def output():
                            g = group_at(i, LAG + 3)
                            if g is not None:
                                dve.wait_ge(s_ox, b * HEADS * NG + g + 1)
                                for t in range(2):
                                    tile, h = g % NG * 2 + t, g // NG
                                    ins = dve.tensor_scalar(O[:, tile, h * DH:(h + 1) * DH],
                                                            PV[:, GQ + t * DH:GQ + (t + 1) * DH],
                                                            rsum[:, tile, h, 0:1], None, ALU.mult)
                                ins.then_inc(s_oxf, 1)

                        def project_low():
                            q = j - 1
                            if 0 <= q < 4 and hd + 1 < HEADS:
                                proj_low(hd + 1, q)
                        if i < STEPS:
                            maximum(0)
                        reciprocals()
                        project_low()
                        factor()
                        output()
                        map_low(0)
                        if i < STEPS:
                            maximum(1)
                        map_low(1)

                    def mean_square(half):
                        for t in range(4 * half, 4 * half + 4):
                            dve.wait_ge(s_sq, b * NT + t + 1)
                            link(dve.tensor_reduce(grp[:, t, :], sq[:, t, :].rearrange("p (g n) -> p g n", n=8),
                                                   AX.X, ALU.add))
                        g = grp[:, 4 * half:4 * half + 4, :]
                        dve.tensor_scalar(g, g, 1.0 / 8, ATT_EPS, ALU.mult, ALU.add).then_inc(s_ms, 1)

                    def inverse_root(half):
                        g, r, n = grp[:, 4 * half:4 * half + 4, :], inv[:, 4 * half:4 * half + 4, :], newton[:, :, :]
                        dve.wait_ge(s_sqrt, 2 * b + half + 1)
                        link(dve.reciprocal(r, r))
                        link(dve.tensor_tensor(n, r, r, ALU.mult))
                        link(dve.tensor_tensor(n, n, g, ALU.mult))
                        link(dve.tensor_scalar(n, n, -0.5, 1.5, ALU.mult, ALU.add))
                        link(dve.tensor_tensor(r, r, n, ALU.mult))

                    def normalise(t):
                        o_g = O[:, t, :].rearrange("p (g n) -> p g n", n=8)
                        dve.scalar_tensor_tensor(o_g, o_g, 1.0 - L_INIT,
                                                 inv[:, t, :].unsqueeze(2).to_broadcast([P, D // 8, 8]),
                                                 ALU.mult, ALU.mult).then_inc(s_xn2, 1)

                    def ot_low(t):
                        half = slice(4 * (t % 2), 4 * (t % 2) + 4)
                        low(o_use(t), 2 * NT + HEADS * TH + t, AT[1][:, half, 0:P],
                            TT[:, o_use(t) % 2, :].rearrange("p (k n) -> p k n", k=KT), AT[0][:, half, 0:P])

                    def add_x(t):
                        dve.wait_ge(s_ttf, b * TTK + wo_use(t) + 1)
                        dve.wait_ge(s_x[t % 2], 16 * (b * NT + NT // 2 + t // 2 + 1))
                        if t >= 2:
                            dve.wait_ge(s_st[t % 2], 16 * (b * (NT // 2) + t // 2))
                        dve.tensor_tensor(x1_sb[:, t % 2, :], TT[:, wo_use(t) % 2, :], x_in[:, t % 2, :], ALU.add)\
                           .then_inc(s_x1, 1)
                        dve.wait_ge(s_x1, b * NT + t + 1)
                        dve.sem_inc(s_xfree, 1)
                        dve.sem_inc(s_ttfree, 1)

                    mean_square(0)
                    mean_square(1)
                    inverse_root(0)
                    normalise(0)
                    normalise(1)
                    ot_low(0)
                    inverse_root(1)
                    for t in range(NT):
                        if t + 2 < NT:
                            normalise(t + 2)
                        if t + 1 < NT:
                            ot_low(t + 1)
                        add_x(t)
                    for i in range(2):
                        dve.wait_ge(s_st[i], 16 * (b * (NT // 2) + NT // 2))
                    dve.sem_inc(s_wfree, 1)
                    link.close()

            @block.gpsimd
            def _(pool):
                pool.memset(neg_half[:, :], -0.5).then_inc(s_half_set, 1)
                pool.wait_ge(s_half_set, 1)

                def split_w(n, low, raw, high):
                    pool.wait_ge(s_wqh, n + 1)
                    pool.tensor_tensor(low, raw, high.bitcast(F32), ALU.subtract).then_inc(s_wql, 1)

                def split_wqk(n):
                    split_w(n, wq[1][:, :, :], w_in_qk, wq[0][:, :, :])

                split_wqk(0)
                with pool.Fori(0, batches) as b:
                    link = Links(pool, s_scaled, TH * HEADS, b, passed=s_passed)
                    for t in range(NT):
                        v = rstd[:, t % 2:t % 2 + 1]
                        pool.wait_ge(s_var, b * NT + t + 1)
                        pool.tensor_tensor(v, v, neg_half[:, :], ALU.pow).then_inc(s_root, 1)
                    split_wqk(b * LOADS + 1)
                    for i in range(STEPS):
                        hd, j = divmod(i, NT)
                        pool.wait_ge(s_cc, b * STEPS + i + 1)
                        pool.sem_inc(s_passed, 1)
                        for k, nb in blocks(i):
                            c = slice(k * P, (k + nb) * P)
                            p0, p1 = PR[:, i % 3, 0, c], PR[:, i % 3, 1, c]
                            link(pool.tensor_scalar(p1, p1, comb[:, j % 4:j % 4 + 1], 1.0, ALU.mult, ALU.mult))
                            pool.tensor_tensor(p0, p0, p1, ALU.add).then_inc(s_comb, 1)
                        if j == 4 and hd + 2 <= HEADS:
                            split_wqk(b * LOADS + hd + 2)
                        if hd == HEADS - 1 and j in (1, 3):
                            k = slice(j - 1, j + 1)
                            split_w(b * LOADS + HEADS + 1 + j // 2, W[1][:, k, :], w_in_wo, W[0][:, k, :])
                    link.close()

            @block.scalar
            def _(act):
                def high_w(n, high, raw):
                    act.wait_ge(s_win, n * 16 + 16)
                    act.activation(high, raw, ACT.Copy).then_inc(s_wqh, 1)

                def high_wqk(n):
                    high_w(n, wq[0][:, :, :], w_in_qk)

                act.wait_ge(s_c, 48)
                act.activation(identb[:, :], ident[:, :], ACT.Copy).then_inc(s_cast, 1)
                act.activation(mask[:, :, :], maskf.rearrange("p (t n) -> p t n", t=2), ACT.Copy).then_inc(s_cast, 1)
                act.wait_ge(s_prime, 2)
                act.activation(lam_s[:, 0:2], lam_s[:, 0:2], ACT.Exp).then_inc(s_cast, 1)
                high_wqk(0)
                with act.Fori(0, batches) as b:
                    def high(use, out, in_):
                        act.wait_ge(s_ttf, b * TTK + use + 1)
                        act.activation(out, in_, ACT.Copy).then_inc(s_tth, 1)

                    def proj_high(h, quarter):
                        m, half = QUARTERS[quarter]
                        c, r = slice(half * D, (half + 1) * D), h % 2
                        act.wait_ge(s_pjf, b * 4 * HEADS + 4 * h + quarter + 1)
                        if m == 0:
                            act.activation(Q[r][0][lo64, c], PJ[lo64, :], ACT.Copy, scale=0.125)
                            ins = act.activation(Q[r][1][hi64, c], PJ[hi64, :], ACT.Copy, scale=0.125)
                        else:
                            act.activation(K[lo64, r, 0, c], PJ[lo64, :], ACT.Copy)
                            ins = act.activation(K[hi64, r, 2, c], PJ[hi64, :], ACT.Copy)
                        ins.then_inc(s_pjh, 1)

                    act.wait_ge(s_wv, 16 * b + 16)
                    act.wait_ge(s_wfree, b + 1)
                    act.activation(W[0][:, :, :], wv_in, ACT.Copy).then_inc(s_wvh, 1)
                    for t in range(NT):
                        high(x_use(t), xT[0][:, :, t * P:(t + 1) * P],
                             TT[:, x_use(t) % 2, :].rearrange("p (k n) -> p k n", k=KT))
                        for v in ([t - 1] if t else []) + ([t] if t == NT - 1 else []):
                            high(v_use(v), V[:, v, :, 0:DH],
                                 TT[:, v_use(v) % 2, :].rearrange("p (h n) -> p h n", h=HEADS))
                            for quarter in FIRST_QUARTERS.get(v, ()):
                                proj_high(0, quarter)
                    high_wqk(b * LOADS + 1)

                    for i in range(STEPS + LAG + 2):
                        hd, j = divmod(i, NT)

                        def exponential(s):
                            u = hd * U + 2 * j + s
                            act.wait_ge(s_max, b * HEADS * U + u + 1)
                            sc = score_tile(u % U)
                            act.activation(PR[:, i % 3, s, 0:width(i)], sc, ACT.Exp, bias=nmax[:, u % U:u % U + 1],
                                           accum_out=sums[:, j, hd, s:s + 1]).then_inc(s_scfree, 1)

                        def map_high(part):
                            if LAG <= i < STEPS + LAG and part < len(blocks(i - LAG)):
                                use, t = turn_use(i - LAG) + part, i % 2
                                k, nb = blocks(i - LAG)[part]
                                high(use, AT[0][:, k:k + nb, t * P:(t + 1) * P],
                                     TT[:, use % 2, 0:nb * P].rearrange("p (k n) -> p k n", k=nb))

                        def turn_out():
                            g = group_at(i, LAG + 2)
                            if g is not None:
                                act.wait_ge(s_pv, b * HEADS * NG + g + 1)
                                act.activation(OT[:, :], PV[:, 0:GQ], ACT.Copy).then_inc(s_ot, 1)

                        def project_high():
                            q = j - 1
                            if 0 <= q < 4 and hd + 1 < HEADS:
                                proj_high(hd + 1, q)
                            if q == 3 and hd + 2 <= HEADS:
                                high_wqk(b * LOADS + hd + 2)
                        project_high()
                        map_high(0)
                        if i < STEPS:
                            exponential(0)
                        turn_out()
                        map_high(1)
                        if i < STEPS:
                            exponential(1)
                        if hd == HEADS - 1 and j in (1, 3):
                            high_w(b * LOADS + HEADS + 1 + j // 2, W[0][:, j - 1:j + 1, :], w_in_wo)
                    for t in range(NT):
                        if t % 2 == 0:
                            act.wait_ge(s_oxf, b * HEADS * NG + (HEADS - 1) * NG + t // 2 + 2)
                        act.activation(sq[:, t, :], O[:, t, :], ACT.Square).then_inc(s_sq, 1)
                    for half in range(2):
                        act.wait_ge(s_ms, 2 * b + half + 1)
                        act.activation(inv[:, 4 * half:4 * half + 4, :], grp[:, 4 * half:4 * half + 4, :], ACT.Sqrt)\
                           .then_inc(s_sqrt, 1)
                    for t in range(NT):
                        high(o_use(t), AT[0][:, 4 * (t % 2):4 * (t % 2) + 4, 0:P],
                             TT[:, o_use(t) % 2, :].rearrange("p (k n) -> p k n", k=KT))
                    act.wait_ge(s_xts, b * 64 + 64)

            @block.tensor
            def _(pe):
                pe.wait_ge(s_c, 48)
                pe.wait_ge(s_cast, 2)
                pe.wait_ge(s_fold, 1)
                with pe.Fori(0, batches) as b:
                    def turn(use, blocks_in):
                        pe.wait_ge(s_ttfree, b * TTK + use + 1)
                        for i, v in enumerate(blocks_in):
                            ins = pe.transpose(TT[:, use % 2, i * P:(i + 1) * P], v, ident[:, :])
                        ins.then_inc(s_ttf, 1)

                    def project(h, quarter):
                        m, half = QUARTERS[quarter]
                        if quarter == 0:
                            pe.wait_ge(s_wql, b * LOADS + h + 1)
                        pe.wait_ge(s_pjfree, b * 4 * HEADS + 4 * h + quarter + 1)
                        for k in range(KT):
                            ins = three_products(pe, PJ[:, :], [w[:, k, m * P:(m + 1) * P] for w in wq],
                                                 [w[:, k, half * D:(half + 1) * D] for w in xT], k == 0, k == KT - 1)
                        ins.then_inc(s_pjf, 1)

                    for t in range(NT):
                        for n in ([0, 1] if t == 0 else [t + 1] if t + 1 < NT else []):
                            pe.wait_ge(s_xn, b * NT + n + 1)
                            turn(x_use(n), [xn[:, n % 2, k * P:(k + 1) * P] for k in range(KT)])
                        if t == 0:
                            pe.wait_ge(s_wvl, b + 1)
                        use = v_use(t)
                        pe.wait_ge(s_ttfree, b * TTK + max(use, x_use(t) + 2) + 1)
                        for k in range(KT):
                            ins = three_products(pe, TT[:, use % 2, :], [w[:, k, t * P:(t + 1) * P] for w in xT],
                                                 [w[:, k, :] for w in W], k == 0, k == KT - 1)
                        ins.then_inc(s_ttf, 1)
                        for quarter in FIRST_QUARTERS.get(t, ()):
                            project(0, quarter)

                    for i in range(STEPS + LAG + 2):
                        hd, j = divmod(i, NT)

                        def scores(s):
                            n = width(i)
                            u = hd * U + 2 * j + s
                            if j == 0 and s == 0:
                                pe.wait_ge(s_pjfree, b * 4 * HEADS + 4 * hd + 4 + 1)
                                pe.wait_ge(s_kdup, (b * HEADS + hd + 1) * 8 * 16)
                            v = bank_before(u)
                            if v is not None:
                                pe.wait_ge(s_scfree, b * HEADS * U + v + 1)
                            first = bank(u % U)
                            qs = Q[hd % 2][s][:, j * P:(j + 1) * P]
                            for c0 in range(0, n, D):
                                w = min(D, n - c0)
                                end = c0 + w == n
                                out = SC[:, first + c0 // D, :]
                                pe.matmul(out[:, 0:w], qs, K[:, hd % 2, 2 * s, c0:c0 + w], start=True, stop=False)
                                pe.matmul(out[:, 0:w], qs, K[:, hd % 2, 2 * s + 1, c0:c0 + w], start=False,
                                          stop=not end)
                                if end:
                                    ins = pe.matmul(out[:, w - GQ:w], identb[:, :], mask[:, j % 2, :],
                                                    start=False, stop=True)
                            ins.then_inc(s_scf, 1)

                        def turn_maps(part):
                            if LAG <= i < STEPS + LAG and part < len(blocks(i - LAG)):
                                use = turn_use(i - LAG) + part
                                k, nb = blocks(i - LAG)[part]
                                pe.wait_ge(s_comb, b * HEADS * TH + use - 2 * NT + 1)
                                turn(use, [PR[:, (i - LAG) % 3, 0, (k + q) * P:(k + q + 1) * P] for q in range(nb)])

                        def values():
                            g = group_at(i, LAG + 2)
                            if g is not None:
                                pe.wait_ge(s_ttfree, b * TTK + turn_use(i - LAG - 1) + len(blocks(i - LAG - 1)) + 2)
                                pe.wait_ge(s_oxf, b * HEADS * NG + g + 1)
                                n = 2 * (g % NG + 1)
                                for k in range(n):
                                    for part in range(2):
                                        ins = pe.matmul(PV[:, 0:GQ], V[:, k, g // NG, :], AT[part][:, k, :],
                                                        start=(k + part == 0), stop=(k == n - 1 and part == 1))
                                ins.then_inc(s_pv, 1)

                        def output():
                            g = group_at(i, LAG + 3)
                            if g is not None:
                                pe.wait_ge(s_ot, b * HEADS * NG + g + 1)
                                for t in range(2):
                                    ins = pe.matmul(PV[:, GQ + t * DH:GQ + (t + 1) * DH], OT[:, t * P:(t + 1) * P],
                                                    fold[:, :], start=True, stop=True)
                                ins.then_inc(s_ox, 1)

                        def project_next():
                            if j < 4 and hd + 1 < HEADS:
                                project(hd + 1, j)
                        if i < STEPS:
                            scores(0)
                        values()
                        output()
                        turn_maps(0)
                        if i < STEPS:
                            scores(1)
                        turn_maps(1)
                        project_next()

                    def o_t(t):
                        pe.wait_ge(s_xn2, b * NT + t + 1)
                        turn(o_use(t), [O[:, t, k * P:(k + 1) * P] for k in range(KT)])

                    o_t(0)
                    pe.wait_ge(s_wql, (b + 1) * LOADS + 1)
                    for t in range(NT):
                        if t + 1 < NT:
                            o_t(t + 1)
                        use = wo_use(t)
                        pe.wait_ge(s_ttfree, b * TTK + max(use, o_use(t) + 2) + 1)
                        for k in range(KT):
                            ins = three_products(pe, TT[:, use % 2, :], [w[:, 4 * (t % 2) + k, 0:P] for w in AT],
                                                 [w[:, k, :] for w in W], k == 0, k == KT - 1)
                        ins.then_inc(s_ttf, 1)


def dense_ffn(nc, w1T, w3T, w2p, xth_d, xtl_d, x1, x1b, x2, chunks):
    HH = HID // 2
    M = HH // P
    RING = 4
    TK = D // P
    NP = 12
    with ExitStack() as ctx:
        def sb(name, shape, dt=F32):
            return ctx.enter_context(nc.sbuf_tensor(name, shape, dt))

        def pb(name, shape):
            return ctx.enter_context(nc.psum_tensor(name, shape, F32))

        def sem(name):
            return ctx.enter_context(nc.semaphore(name))

        G = pb("gate_ps", [P, 2, D])
        Up = pb("up_ps", [P, 2, D])
        Y = pb("ffn_ps", [P, TK, D])
        w1 = [sb("w1_hi", [P, KT, HH], F32R), sb("w1_lo", [P, KT, HH], F32R)]
        w3 = [sb("w3_hi", [P, KT, HH], F32R), sb("w3_lo", [P, KT, HH], F32R)]
        w2 = [sb("w2_hi", [P, M, D], F32R), sb("w2_lo", [P, M, D], F32R)]
        stage = sb("w_stage", [P, 3, 2 * D])
        X = [sb("ffn_x_hi", [P, 2, KT, D], F32R), sb("ffn_x_lo", [P, 2, KT, D], F32R)]
        sg = sb("silu_gate", [P, 2, D])
        hf = sb("hidden", [P, 2, D])
        H = [sb("hidden_hi", [P, RING, D], F32R), sb("hidden_lo", [P, RING, D], F32R)]
        res = sb("residual", [P, 2, TK, D])

        s_st = [sem(f"f_stage{i}") for i in range(3)]
        s_wh, s_wl, s_wl2 = sem("f_w_high"), sem("f_w_low"), sem("f_w_low2")
        s_x = [sem("f_x0"), sem("f_x1")]
        s_r = [sem("f_res0"), sem("f_res1")]
        s_out = [sem("f_out0"), sem("f_out1")]
        s_g, s_sg, s_u, s_hh, s_hl = sem("f_gate_up"), sem("f_silu"), sem("f_hidden"), sem("f_h_high"), sem("f_h_low")
        s_passed = sem("f_passed")
        s_y, s_sum = sem("f_product"), sem("f_sum")

        def piece(n):
            if n < 8:
                return (w1T, w3T)[n // 4], (w1, w3)[n // 4], n % 4
            return w2p, w2, n - 8

        def pieces(parts, i):
            n = i % NP
            _, w, k = piece(n)
            if n < 8:
                return w[parts][:, k, :]
            return w[parts][:, 2 * k:2 * k + 2, :].rearrange("p a n -> p (a n)")

        def over_chunks(eng, body, half):
            with eng.Fori(0, chunks // 2 - 1) as i:
                for par in range(2):
                    body(2 * i + (half * chunks + par), 2 * i + par, par, False)
            for par in range(2):
                c = chunks - 2 + par
                body(half * chunks + c, c, par, par == 1)

        with nc.Block() as block:
            @block.sync
            def _(sp):
                for half in range(2):
                    if half:
                        sp.wait_ge(s_g, M * chunks)
                    def load_x(cg, c, par):
                        for part, dram in ((0, xth_d), (1, xtl_d)):
                            sp.dma_start(X[part][:, par, :, :].bitcast(F32),
                                         dram[bass.ds(c, 1)].rearrange("o p k n -> (o p) k n")).then_inc(s_x[par], 16)

                    def tokens(d, c):
                        return d[bass.ds(c * D, D), :].rearrange("(t p) n -> p t n", p=P)

                    for n in range(NP):
                        i = half * NP + n
                        if i >= 3:
                            sp.wait_ge(s_wl if (i - 3) % 2 == 0 else s_wl2, (i - 3) // 2 + 1)
                        d, _, k = piece(n)
                        src = (d[k * P:(k + 1) * P, half * HH:(half + 1) * HH] if n < 8 else
                               d[half * HH + 2 * k * P:half * HH + 2 * (k + 1) * P, :].rearrange(
                                   "(a p) n -> p a n", p=P))
                        dst = stage[:, i % 3, :] if n < 8 else stage[:, i % 3, :].rearrange("p (a n) -> p a n", a=2)
                        sp.dma_start(dst, src).then_inc(s_st[i % 3], 16)
                        if n == 3:
                            load_x(0, 0, 0)
                    source, dest = (x1, x1b) if half == 0 else (x1b, x2)

                    def body(cg, c, par, last):
                        sp.dma_start(res[:, par, :, :], tokens(source, c)).then_inc(s_r[par], 16)
                        if not last:
                            sp.wait_ge(s_g, cg * M + 1)
                            load_x(cg + 1, c + 1, 1 - par)
                        sp.wait_ge(s_sum, cg * TK + 2 * TK)
                        sp.dma_start(tokens(dest, c), res[:, par, :, :]).then_inc(s_out[par], 16)
                        sp.wait_ge(s_out[par], 16 * half * (chunks // 2) + (c - par) * 8 + 16)
                        sp.sem_inc(s_passed, 1)

                    over_chunks(sp, body, half)

            @block.scalar
            def _(act):
                for half in range(2):
                    if half:
                        act.wait_ge(s_y, chunks * M)
                    for n in range(NP):
                        i = half * NP + n
                        act.wait_ge(s_st[i % 3], 16 * (i // 3 + 1))
                        act.activation(pieces(0, i), stage[:, i % 3, :], ACT.Copy).then_inc(s_wh, 1)

                    def body(cg, c, par, last):
                        for m in range(M):
                            n = cg * M + m
                            act.wait_ge(s_g, n + 1)
                            act.activation(sg[:, m % 2, :], G[:, m % 2, :], ACT.Silu).then_inc(s_sg, 1)
                            act.wait_ge(s_u, n + 1)
                            act.activation(H[0][:, m % RING, :], hf[:, m % 2, :], ACT.Copy).then_inc(s_hh, 1)

                    over_chunks(act, body, half)

            @block.gpsimd
            def _(pool):
                for half in range(2):
                    for n in range(0, NP, 2):
                        i = half * NP + n
                        pool.wait_ge(s_wh, i + 1)
                        pool.tensor_tensor(pieces(1, i), stage[:, i % 3, :], pieces(0, i).bitcast(F32),
                                           ALU.subtract).then_inc(s_wl, 1)

                    def body(cg, c, par, last):
                        for m in range(M):
                            n = cg * M + m
                            pool.wait_ge(s_hh, n + 1)
                            pool.tensor_tensor(H[1][:, m % RING, :], hf[:, m % 2, :],
                                               H[0][:, m % RING, :].bitcast(F32), ALU.subtract).then_inc(s_hl, 1)

                    over_chunks(pool, body, half)

            @block.vector
            def _(dve):
                dve.sem_inc(s_sum, TK)
                for half in range(2):
                    for n in range(1, NP, 2):
                        i = half * NP + n
                        dve.wait_ge(s_wh, i + 1)
                        dve.tensor_tensor(pieces(1, i), stage[:, i % 3, :], pieces(0, i).bitcast(F32),
                                          ALU.subtract).then_inc(s_wl2, 1)

                    def sums(cg, c, par):
                        dve.wait_ge(s_r[par], 16 * half * (chunks // 2) + (c - par) * 8 + 16)
                        for t in range(TK):
                            if t == 0:
                                dve.wait_ge(s_y, cg * M + M)
                            dve.tensor_tensor(res[:, par, t, :], Y[:, t, :], res[:, par, t, :], ALU.add)\
                               .then_inc(s_sum, 1)

                    def gated(cg, m, first=False):
                        n = cg * M + m
                        dve.wait_ge(s_sg, n + 1)
                        if not first:
                            dve.wait_ge(s_hl, n - 1)
                        dve.tensor_tensor(hf[:, m % 2, :], sg[:, m % 2, :], Up[:, m % 2, :], ALU.mult)\
                           .then_inc(s_u, 1)

                    for m in range(2):
                        gated(half * chunks, m, first=True)

                    def body(cg, c, par, last):
                        for m in range(2, M + (0 if last else 2)):
                            gated(cg + m // M, m % M)
                        sums(cg, c, par)

                    over_chunks(dve, body, half)

            @block.tensor
            def _(pe):
                for half in range(2):
                    pe.wait_ge(s_wl, (half + 1) * NP // 2)
                    pe.wait_ge(s_wl2, (half + 1) * NP // 2)

                    def gate_up(cg, c, par, m):
                        n = cg * M + m
                        if m == 0:
                            pe.wait_ge(s_x[par], 32 * half * (chunks // 2) + (c - par) * 16 + 32)
                        for out, w in ((G, w1), (Up, w3)):
                            for k in range(KT):
                                ins = three_products(pe, out[:, m % 2, :], [v[:, k, m * P:(m + 1) * P] for v in w],
                                                     [v[:, par, k, :] for v in X], k == 0, k == KT - 1)
                        ins.then_inc(s_g, 1)

                    def down(cg, m):
                        n = cg * M + m
                        pe.wait_ge(s_hl, n + 1)
                        for t in range(TK):
                            ts = slice(t * P, (t + 1) * P)
                            out = Y[:, t, :]
                            pe.matmul(out, H[0][:, m % RING, ts], w2[0][:, m, :], start=(m == 0), stop=False)
                            pe.matmul(out, H[0][:, m % RING, ts], w2[1][:, m, :], start=False, stop=False)
                            ins = pe.matmul(out, H[1][:, m % RING, ts], w2[0][:, m, :], start=False, stop=(m == M - 1))
                        ins.then_inc(s_y, 1)

                    for m in range(2):
                        gate_up(half * chunks, 0, 0, m)

                    def body(cg, c, par, last):
                        for m in range(M):
                            if m + 2 < M:
                                pe.wait_ge(s_hl, cg * M + m + 1)
                                gate_up(cg, c, par, m + 2)
                            elif not last:
                                pe.wait_ge(s_hl, cg * M + m + 1)
                                gate_up(cg + 1, c + 1, 1 - par, m + 2 - M)
                            if m == 0:
                                pe.wait_ge(s_sum, cg * TK + TK)
                            down(cg, m)

                    over_chunks(pe, body, half)


def recurrence(nc, wr, wf, wc, wo_d, ln_scale, rwT, ident_d, x2, table, logits_d, acc, batches):
    LV = int(math.log2(S))
    GC = 2
    NG = KT // GC
    PU = 3 * GC * 2
    RING = 6
    HU = 2 * GC * 2
    BU = NG * PU
    with ExitStack() as ctx:
        def sb(name, shape, dt=F32):
            return ctx.enter_context(nc.sbuf_tensor(name, shape, dt))

        def pb(name, shape):
            return ctx.enter_context(nc.psum_tensor(name, shape, F32))

        def sem(name):
            return ctx.enter_context(nc.semaphore(name))

        TT = pb("r_turn_ps", [P, 2, D])
        RT = pb("router_ps", [P, D])
        CO = pb("cols_ps", [P, D])
        PP = pb("proj_ps", [P, 2, D])
        MS = pb("sumsq_ps", [P, D])
        W = [[sb(f"w_{n}_{p}", [P, KT, D], F32R) for p in ("hi", "lo")] for n in ("f", "c", "r", "o")]
        rw = [sb("router_hi", [P, KT, P], F32R), sb("router_lo", [P, KT, P], F32R)]
        xT = [sb("r_xT_hi", [P, KT, S], F32R), sb("r_xT_lo", [P, KT, S], F32R)]
        F0 = sb("forget", [P, 2, GC, S])
        C0 = sb("cell_in", [P, 2, GC, S])
        R0 = sb("read_gate", [P, 2, GC, S])
        FU = sb("forget_up", [P, GC, S])
        CU = sb("cell_up", [P, GC, S])
        H = sb("state", [P, GC, S])
        diff = sb("scan_diff", [P, GC, S // 2])
        Z = [sb("gated_hi", [P, 2, KT, P], F32R), sb("gated_lo", [P, 2, KT, P], F32R)]
        x_in = sb("r_x_in", [P, 2, D])
        io = sb("r_tiles", [P, RING, D])
        rows = sb("r_rows", [E, S])
        lg = sb("logits", [P, NT * E])
        rw_in = lg[:, :].rearrange("p (k e) -> p k e", k=KT)
        ident = sb("r_ident", [P, P])
        ones = sb("r_ones", [P, 1])
        neg_half = sb("r_neg_half", [P, NT])
        scale = sb("ln_scale_sb", [P, KT])
        stats = sb("r_stats", [P, NT, 6])
        mv = sb("r_mv", [P, NT, 2])
        rstd = sb("r_rstd", [P, NT])
        minus_mean = sb("r_minus_mean", [P, NT])
        shift = sb("r_shift", [P, NT])
        rms = sb("r_rms", [P, NT])

        s_id, s_wh, s_wl, s_sc = sem("r_ident"), sem("r_wh"), sem("r_wl"), sem("r_scaled")
        s_w = [sem("r_w_" + n) for n in ("router", "forget", "cell", "read", "out")]
        s_x = [sem("r_x0"), sem("r_x1")]
        s_xa, s_xst, s_res, s_ost = ([sem(f"r_{n}{i}") for i in range(RING)]
                                     for n in ("x_to_norm", "xn_stored", "x_again", "out_stored"))
        s_bs, s_ag, s_xn, s_var, s_root = sem("r_bn"), sem("r_bn_joined"), sem("r_xn"), sem("r_var"), sem("r_root")
        s_ttf, s_tth, s_ttfree = sem("r_tt_filled"), sem("r_tt_high"), sem("r_tt_free")
        s_rt, s_rtc, s_co, s_lg, s_lgs = sem("r_router"), sem("r_router_c"), sem("r_cols"), sem("r_lg"), sem("r_lg_st")
        s_ppf, s_ppa, s_pof, s_ppd = sem("r_pp_filled"), sem("r_pp_act"), sem("r_pp_product"), sem("r_pp_dve")
        s_dv, s_lvl, s_fl, s_cp = sem("r_dve_chain"), sem("r_level"), sem("r_flevel"), sem("r_firsts")
        s_h, s_z, s_sq, s_zh, s_zl = sem("r_h"), sem("r_z"), sem("r_sq"), sem("r_zh"), sem("r_zl")
        s_sqs, s_ms, s_mean, s_msq, s_rroot = sem("r_sq_sum"), sem("r_ms"), sem("r_ms_half"), sem("r_ms_mean"), sem("r_rms_root")
        s_shift, s_passed, s_out, s_one = sem("r_shift"), sem("r_passed"), sem("r_out"), sem("r_ones_set")

        def level(arr0, up, par, k):
            if k == 0:
                return arr0[:, par, :, :]
            at = S - (S >> (k - 1))
            return up[:, :, at:at + (S >> k)]

        def tile(t):
            return io[:, t % RING, :]

        def uses(b, t):
            return b * (NT // RING + 1) + t // RING + 1 if t % RING < NT % RING else b + 1

        def product_bank(t):
            return (PP if t % 4 < 2 else TT)[:, t % 2, :]

        def over_batches(eng, head, turn):
            head(0, True)
            with eng.Fori(0, batches - 1) as b:
                turn(b, True)
            turn(batches - 1, False)

        def tile_of(d, b, t):
            return d[bass.ds(b * S + t * P, P), :]

        def gated(t):
            return R0[:, :, :, t * P:(t + 1) * P].rearrange("p g c n -> p (g c) n")

        stages = [F0[:, 1], C0[:, 1], R0[:, 0], R0[:, 1]]

        def weight(i):
            if i == 0:
                return rw[0][:, :, :], rw[1][:, :, :], rw_in
            return (*(flat(v[:, :, :]) for v in W[i - 1]), flat(stages[i - 1]))

        def flat(v):
            return v.rearrange("p a n -> p (a n)")

        with nc.Block() as block:
            @block.sync
            def _(sp):
                sp.dma_start(ident[:, :], ident_d).then_inc(s_id, 16)

                def load_weight(i):
                    sp.dma_start(flat(stages[i]), (wf, wc, wr, wo_d)[i].rearrange("p k n -> p (k n)"))\
                      .then_inc(s_w[1 + i], 16)
                def again(b, t, arrived):
                    sp.dma_start(tile(t), tile_of(x2, b, t)).then_inc(arrived[t % RING], 16)

                def head(b, first=False):
                    for t in range(NT):
                        if t >= 2:
                            sp.wait_ge(s_bs, b * NT + t - 1)
                        elif not first:
                            sp.wait_ge(s_bs, b * NT)
                        sp.dma_start(x_in[:, t % 2, :], tile_of(x2, b, t)).then_inc(s_x[t % 2], 16)
                        if first and t == 1:
                            sp.dma_start(rw_in, rwT).then_inc(s_w[0], 16)
                            load_weight(0)
                        if t == 3:
                            for i in range(RING):
                                again(b, i, s_xa)
                    if first:
                        sp.dma_start(scale[:, :], ln_scale).then_inc(s_w[4], 16)
                        for i in range(1, 4):
                            load_weight(i)
                    for t in range(NT):
                        sp.wait_ge(s_xn, b * NT + t + 1)
                        sp.dma_start(table[bass.ds(b * S + t * P, P), 0:D], tile(t)).then_inc(s_xst[t % RING], 16)
                        if 2 <= t < 2 + NT - RING:
                            sp.wait_ge(s_xst[t - 2], 16 * uses(b, t - 2))
                            sp.wait_ge(s_ttf, b * NT + t - 1)
                            again(b, t - 2 + RING, s_xa)
                    sp.wait_ge(s_lg, b + 1)
                    sp.dma_start(logits_d[bass.ds(b, 1)].rearrange("o p n -> (o p) n"), lg[:, :]).then_inc(s_lgs, 16)

                def turn(b, more):
                    if more:
                        head(b + 1)
                        sp.wait_ge(s_ttf, (b + 2) * NT)
                        sp.sem_inc(s_passed, 1)
                        for t in range(NT - RING, NT):
                            sp.wait_ge(s_xst[t % RING], 16 * uses(b + 1, t))
                        sp.sem_inc(s_passed, 1)
                    for t in range(RING):
                        again(b, t, s_res)
                    for t in range(NT):
                        sp.wait_ge(s_out, b * NT + t + 1)
                        sp.dma_start(tile_of(acc, b, t), tile(t)).then_inc(s_ost[t % RING], 16)
                        if 2 <= t < 2 + NT - RING:
                            sp.wait_ge(s_ost[t - 2], 16 * uses(b, t - 2))
                            again(b, t - 2 + RING, s_res)
                    for t in range(NT - RING, NT):
                        sp.wait_ge(s_ost[t % RING], 16 * uses(b, t))
                    sp.sem_inc(s_passed, 1)

                over_batches(sp, head, turn)
                sp.wait_ge(s_lgs, 16 * batches)
                for t in range(NT - RING, NT):
                    sp.wait_ge(s_xst[t % RING], 16 * uses(batches - 1, t))

            @block.vector
            def _(dve):
                dve.sem_inc(s_ttfree, 2)
                dve.sem_inc(s_ppd, 1)
                dve.sem_inc(s_z, 1)
                dve.sem_inc(s_sq, 1)
                dve.memset(ones[:, :], 1.0).then_inc(s_one, 1)

                def split(i):
                    high, low, raw = weight(i)
                    dve.wait_ge(s_wh, i + 1)
                    dve.tensor_tensor(low, raw, high.bitcast(F32), ALU.subtract).then_inc(s_wl, 1)

                def copy_logits(b, first):
                    dve.wait_ge(s_co, b + 1)
                    if not first:
                        dve.wait_ge(s_lgs, 16 * b)
                    dve.tensor_copy(lg[:, :], CO[:, :]).then_inc(s_lg, 1)

                def statistics(b, t):
                    dve.wait_ge(s_x[t % 2], 16 * (b * (NT // 2) + t // 2 + 1))
                    dve.bn_stats(stats[:, t, :], x_in[:, t % 2, :]).then_inc(s_bs, 1)

                def join_statistics(b):
                    dve.wait_ge(s_bs, b * NT + NT)
                    dve.sem_inc(s_passed, 1)
                    for t in range(NT):
                        dve.bn_aggr(mv[:, t, :], stats[:, t, :]).then_inc(s_ag, 1)
                    dve.wait_ge(s_ag, b * NT + NT)
                    dve.tensor_scalar(rstd[:, :], mv[:, :, 1], LN_EPS, None, ALU.add).then_inc(s_var, 1)
                    dve.tensor_scalar(minus_mean[:, :], mv[:, :, 0], -1.0, None, ALU.mult).then_inc(s_var, 1)

                def head(b, first=False):
                    if first:
                        for t in range(NT):
                            statistics(b, t)
                        join_statistics(b)
                    if first:
                        split(0)
                        split(1)
                        dve.wait_ge(s_w[4], 32)
                        for c in range(KT):
                            v = flat(stages[3])[:, c * D:(c + 1) * D]
                            dve.tensor_scalar(v, v, scale[:, c:c + 1], None, ALU.mult).then_inc(s_sc, 1)
                    for t in range(NT):
                        dve.wait_ge(s_tth, b * NT + t + 1)
                        dve.tensor_tensor(xT[1][:, :, t * P:(t + 1) * P],
                                          TT[:, t % 2, :].rearrange("p (k n) -> p k n", k=KT),
                                          xT[0][:, :, t * P:(t + 1) * P].bitcast(F32), ALU.subtract).then_inc(s_ttfree, 1)
                    if first:
                        for i in range(2, 5):
                            split(i)
                        copy_logits(b, first)

                def scan(b, g, link, more=False):
                    dve.wait_ge(s_ppa, b * BU + g * PU + HU)
                    for k in range(LV):
                        f, c = level(F0, FU, g, k), level(C0, CU, g, k)
                        d = diff[:, :, 0:S >> (k + 1)]
                        link(dve.tensor_tensor(d, c[:, :, 0::2], c[:, :, 1::2], ALU.subtract))
                        if k:
                            dve.wait_ge(s_fl, b * NG * (LV - 1) + g * (LV - 1) + k)
                        link(dve.tensor_tensor(d, d, f[:, :, 1::2], ALU.mult))
                        dve.tensor_tensor(level(C0, CU, g, k + 1), d, c[:, :, 1::2], ALU.add).then_inc(s_lvl, 1)
                        if more and k < NT:
                            statistics(b + 1, k)
                        dve.wait_ge(s_lvl, b * NG * LV + g * LV + k + 1)
                    if more:
                        join_statistics(b + 1)
                    dve.wait_ge(s_cp, b * NG * (LV + 1) + (g + 1) * (LV + 1))
                    for k in range(LV - 2, -1, -1):
                        f, c = level(F0, FU, g, k), level(C0, CU, g, k)
                        h, m = 1 << k, (S >> (k + 1)) - 1
                        d = diff[:, :, 0:m]
                        before = H[:, :, 2 * h - 1:2 * h - 1 + 2 * h * (m - 1) + 1:2 * h]
                        here = H[:, :, 3 * h - 1:3 * h - 1 + 2 * h * (m - 1) + 1:2 * h]
                        cn, fn = c[:, :, 2:2 * m + 1:2], f[:, :, 2:2 * m + 1:2]
                        link(dve.tensor_tensor(d, before, cn, ALU.subtract))
                        link(dve.tensor_tensor(d, d, fn, ALU.mult))
                        ins = dve.tensor_tensor(here, d, cn, ALU.add)
                        if k:
                            link(ins)
                        else:
                            ins.then_inc(s_h, 1)
                    dve.wait_ge(s_h, b * NG + g + 1)
                    dve.wait_ge(s_ppa, b * BU + (g + 1) * PU)
                    dve.tensor_tensor(R0[:, g], R0[:, g], H[:, :, :], ALU.mult).then_inc(s_z, 1)

                def turn(b, more):
                    link = Links(dve, s_dv, NG * (2 * LV + 3 * (LV - 1) - 1), b, passed=s_passed)
                    scan(b, 0, link, more)
                    if more:
                        head(b + 1)
                    scan(b, 1, link)
                    if more:
                        copy_logits(b + 1, False)
                    dve.wait_ge(s_ms, NG * b + NG)
                    dve.tensor_scalar(rms[:, :], MS[:, 0:NT], 1.0 / D, RMS_EPS, ALU.mult, ALU.add).then_inc(s_mean, 1)
                    dve.wait_ge(s_mean, b + 1)
                    dve.scalar_tensor_tensor(rms[:, :], MS[:, NT:2 * NT], 1.0 / D, rms[:, :], ALU.mult, ALU.add)\
                       .then_inc(s_msq, 1)
                    dve.wait_ge(s_rroot, b + 1)
                    for t in range(NT):
                        dve.wait_ge(s_pof, b * NT + t + 1)
                        dve.wait_ge(s_res[t % RING], 16 * uses(b, t))
                        dve.scalar_tensor_tensor(tile(t), product_bank(t), rms[:, t:t + 1], tile(t), ALU.mult, ALU.add).then_inc(s_out, 1)
                        dve.wait_ge(s_out, b * NT + t + 1)
                        dve.sem_inc(s_ppd, 1)
                    link.close()

                over_batches(dve, head, turn)

            @block.gpsimd
            def _(pool):
                pool.memset(neg_half[:, :], -0.5).then_inc(s_one, 1)
                pool.wait_ge(s_one, 2)

                def head_root(b):
                    pool.wait_ge(s_var, 2 * b + 2)
                    pool.tensor_tensor(rstd[:, :], rstd[:, :], neg_half[:, :], ALU.pow).then_inc(s_root, 1)
                    pool.wait_ge(s_root, b + 1)
                    pool.tensor_tensor(shift[:, :], minus_mean[:, :], rstd[:, :], ALU.mult).then_inc(s_shift, 1)

                def head(b, first=False):
                    head_root(b)

                def gates(b, g):
                    pool.wait_ge(s_z, b * NG + g + 1)
                    pool.wait_ge(s_ppa, b * BU + g * PU + HU // 2)
                    for k in range(LV - 1):
                        f = level(F0, FU, g, k)
                        pool.tensor_tensor(level(F0, FU, g, k + 1), f[:, :, 0::2], f[:, :, 1::2], ALU.mult)\
                            .then_inc(s_fl, 1)
                        pool.wait_ge(s_fl, b * NG * (LV - 1) + g * (LV - 1) + k + 1)

                def add_squares(b, g):
                    pool.wait_ge(s_sq, b * NG + g + 2)
                    pool.tensor_tensor(F0[:, g, 0, :], F0[:, g, 0, :], F0[:, g, 1, :], ALU.add).then_inc(s_sqs, 1)

                def firsts(b, g):
                    pool.wait_ge(s_sq, b * NG + g + 1)
                    pool.wait_ge(s_ppa, b * BU + g * PU + HU)
                    pool.sem_inc(s_passed, 1)
                    pool.tensor_copy(H[:, :, 0:1], C0[:, g, :, 0:1]).then_inc(s_cp, 1)
                    for k in range(LV):
                        pool.wait_ge(s_lvl, b * NG * LV + g * LV + k + 1)
                        pool.sem_inc(s_passed, 1)
                        at = (2 << k) - 1
                        pool.tensor_copy(H[:, :, at:at + 1], level(C0, CU, g, k + 1)[:, :, 0:1]).then_inc(s_cp, 1)

                def turn(b, more):
                    gates(b, 0)
                    firsts(b, 0)
                    if more:
                        head_root(b + 1)
                    gates(b, 1)
                    add_squares(b, 0)
                    firsts(b, 1)
                    add_squares(b, 1)
                    for t in range(NT):
                        if t == 2:
                            pool.wait_ge(s_msq, b + 1)
                            pool.tensor_tensor(rms[:, :], rms[:, :], neg_half[:, :], ALU.pow).then_inc(s_rroot, 1)
                        pool.wait_ge(s_zh, b * NT + t + 1)
                        pool.tensor_tensor(Z[1][:, t % 2, :, :], gated(t), Z[0][:, t % 2, :, :].bitcast(F32),
                                           ALU.subtract).then_inc(s_zl, 1)

                over_batches(pool, head, turn)

            @block.scalar
            def _(act):
                def high(i):
                    act.wait_ge(s_w[i], 32 if i == 4 else 16)
                    if i == 4:
                        act.wait_ge(s_sc, KT)
                    act.activation(weight(i)[0], weight(i)[2], ACT.Copy).then_inc(s_wh, 1)

                def projection(b, n):
                    g, i = n // PU, n % PU
                    w, ch, half = i // 4, (i // 2) % 2, i % 2
                    dst = (F0, C0, R0)[w][:, g, ch, half * D:(half + 1) * D]
                    act.wait_ge(s_ppf, b * BU + n + 1)
                    act.activation(dst, PP[:, n % 2, :], ACT.Sigmoid if w == 0 else ACT.Silu).then_inc(s_ppa, 1)

                def head(b, first=False):
                    def normalise(t):
                        act.wait_ge(s_xa[t % RING], 16 * uses(b, t))
                        act.activation(tile(t), tile(t), ACT.Identity, bias=shift[:, t:t + 1],
                                       scale=rstd[:, t:t + 1]).then_inc(s_xn, 1)

                    if first:
                        high(0)
                        high(1)
                    act.wait_ge(s_shift, b + 1)
                    normalise(0)
                    normalise(1)
                    for t in range(NT):
                        act.wait_ge(s_ttf, b * NT + t + 1)
                        act.activation(xT[0][:, :, t * P:(t + 1) * P],
                                       TT[:, t % 2, :].rearrange("p (k n) -> p k n", k=KT), ACT.Copy).then_inc(s_tth, 1)
                        if t + 2 < NT:
                            normalise(t + 2)
                    if first:
                        for i in range(2, 5):
                            high(i)
                    for half in range(2):
                        act.wait_ge(s_rt, b * 2 + half + 1)
                        act.activation(rows[:, half * D:(half + 1) * D], RT[0:E, :], ACT.Copy).then_inc(s_rtc, 1)
                    for n in range(HU):
                        projection(b, n)

                def squares(b, g):
                    act.wait_ge(s_h, b * NG + g + 1)
                    act.activation(F0[:, g], H[:, :, :], ACT.Square).then_inc(s_sq, 1)

                def turn(b, more):
                    for n in range(HU, BU):
                        projection(b, n)
                        if n == BU - 3:
                            squares(b, 0)
                    if more:
                        head(b + 1, False)
                    squares(b, 1)
                    act.wait_ge(s_z, b * NG + NG + 1)
                    for t in range(NT):
                        if t >= 2:
                            act.wait_ge(s_pof, b * NT + t - 1)
                        act.activation(Z[0][:, t % 2, :, :], gated(t), ACT.Copy).then_inc(s_zh, 1)

                over_batches(act, head, turn)

            @block.tensor
            def _(pe):
                pe.wait_ge(s_id, 16)
                pe.wait_ge(s_one, 2)

                def projection(b, n, first):
                    g, i = n // PU, n % PU
                    w, ch, half = i // 4, g * GC + (i // 2) % 2, i % 2
                    if n >= 2 or not first:
                        pe.wait_ge(s_ppa, b * BU + n - 1)
                    if n == HU:
                        pe.wait_ge(s_ppd, b * NT + 1)
                    if first and i % 4 == 0:
                        pe.wait_ge(s_wl, 2 + w)
                    for k in range(KT):
                        ins = three_products(pe, PP[:, n % 2, :], [v[:, k, ch * P:(ch + 1) * P] for v in W[w]],
                                             [v[:, k, half * D:(half + 1) * D] for v in xT], k == 0, k == KT - 1)
                    ins.then_inc(s_ppf, 1)

                def head(b, first=False):
                    for t in range(NT):
                        pe.wait_ge(s_xn, b * NT + t + 1)
                        pe.wait_ge(s_ttfree, b * NT + t + 1)
                        for k in range(KT):
                            ins = pe.transpose(TT[:, t % 2, k * P:(k + 1) * P], tile(t)[:, k * P:(k + 1) * P],
                                               ident[:, :])
                        ins.then_inc(s_ttf, 1)
                    for half in range(2):
                        c = slice(half * D, (half + 1) * D)
                        if half == 0:
                            pe.wait_ge(s_ttfree, b * NT + NT + 2)
                            if first:
                                pe.wait_ge(s_wl, 1)
                        else:
                            pe.wait_ge(s_rtc, b * 2 + 1)
                        for k in range(KT):
                            ins = three_products(pe, RT[:, :], [v[:, k, :] for v in rw], [v[:, k, c] for v in xT],
                                                 k == 0, k == KT - 1)
                        ins.then_inc(s_rt, 1)
                    if not first:
                        sum_squares(b - 1, 0)
                    for n in range(HU):
                        projection(b, n, first)
                        if n == 1:
                            pe.wait_ge(s_rtc, b * 2 + 2)
                            if not first:
                                pe.wait_ge(s_lg, b)
                            pe.sem_inc(s_passed, 1)
                            for t in range(NT):
                                ins = pe.transpose(CO[:, t * E:(t + 1) * E], rows[:, t * P:(t + 1) * P],
                                                   ident[0:E, 0:E])
                            ins.then_inc(s_co, 1)

                def sum_squares(b, g):
                    pe.wait_ge(s_sqs, b * NG + g + 1)
                    for t in range(NT):
                        ins = pe.matmul(MS[:, g * NT + t:g * NT + t + 1], F0[:, g, 0, t * P:(t + 1) * P], ones[:, :],
                                        start=True, stop=True)
                    ins.then_inc(s_ms, 1)

                def turn(b, more):
                    for n in range(HU, BU):
                        if n == HU:
                            pe.wait_ge(s_wl, 5)
                        projection(b, n, False)
                    if more:
                        head(b + 1)
                    else:
                        sum_squares(b, 0)
                    pe.wait_ge(s_ppa, (b + 1) * BU + (HU if more else 0))
                    for t in range(NT):
                        pe.wait_ge(s_zl, b * NT + t + 1)
                        if t >= 4:
                            pe.wait_ge(s_ppd, b * NT + t - 2)
                        for k in range(KT):
                            ins = three_products(pe, product_bank(t), [v[:, t % 2, k, :] for v in Z],
                                                 [v[:, k, :] for v in W[3]], k == 0, k == KT - 1)
                        ins.then_inc(s_pof, 1)
                        if t == 1:
                            sum_squares(b, 1)

                over_batches(pe, head, turn)


def routing(nc, logits_d, rev_d, pcol_d, ident_d, table, out, slots, batches):
    T = batches * S
    NTT = T // P
    HT = NTT // 2
    ROUNDS = CAP // 8
    with ExitStack() as ctx:
        def sb(name, shape, dt=F32):
            return ctx.enter_context(nc.sbuf_tensor(name, shape, dt))

        def sem(name):
            return ctx.enter_context(nc.semaphore(name))

        L = sb("all_logits", [P, NTT, E])
        rest = sb("without_top", [P, NTT, E])
        ex = sb("route_exp", [P, NTT, E])
        sel = sb("selected", [P, HT, 2, E])
        top = sb("top_values", [P, NTT, TOPK])
        zsum = sb("z_sum", [P, NTT])
        den = sb("top_sum", [P, NTT])
        key = sb("keys", [P, 2, T // 2])
        rev = sb("rev_sb", [P, T // 2])
        pcol = sb("pcol_sb", [P, 1])
        ident = sb("m_ident", [P, P])
        drawn = sb("drawn", [P, CAP])
        both = sb("both_halves", [E, 2, 2 * CAP])
        first = sb("first_tokens", [E, CAP])
        vt = sb("slot_keys", [P, E])
        tmp = sb("slot_tmp", [P, E])
        zero = sb("zero_rows", [P, ROW])
        MT = ctx.enter_context(nc.psum_tensor("mask_ps", [P, 2, D], F32))
        VT = ctx.enter_context(nc.psum_tensor("slot_ps", [P, E], F32))

        s_in, s_dv, s_exp, s_sel, s_zero = sem("m_in"), sem("m_chain"), sem("m_exp"), sem("m_sel"), sem("m_zero")
        s_mt, s_key, s_gate, s_st, s_mv = sem("m_turned"), sem("m_key"), sem("m_gate"), sem("m_stored"), sem("m_moved")
        s_drawn, s_first, s_vt, s_shift = sem("m_drawn"), sem("m_first"), sem("m_vt"), sem("m_shift")

        def bcast(v):
            return v.unsqueeze(2).to_broadcast([P, NTT, E])

        with nc.Block() as block:
            @block.sync
            def _(sp):
                sp.dma_start(L[:, :, :].rearrange("p (b n) e -> p b (n e)", b=batches),
                             logits_d.rearrange("b p n -> p b n")).then_inc(s_in, 16)
                sp.dma_start(rev[:, :], rev_d).then_inc(s_in, 16)
                sp.dma_start(pcol[:, :], pcol_d).then_inc(s_in, 16)
                sp.dma_start(ident[:, :], ident_d).then_inc(s_in, 16)
                sp.wait_ge(s_zero, 1)
                sp.dma_start(table[T:T + P, :], zero[:, :]).then_inc(s_st, 16)
                sp.dma_start(out[T:T + P, :], zero[:, 0:D]).then_inc(s_st, 16)
                sp.wait_ge(s_gate, 1)
                sp.dma_start(table[0:T, D:ROW].rearrange("(n p) e -> p n e", p=P), ex[:, :, :]).then_inc(s_st, 16)
                sp.wait_ge(s_drawn, ROUNDS)
                sp.dma_start(both[:, 0, 0:CAP], drawn[0:E, :]).then_inc(s_mv, 16)
                sp.dma_start(both[:, 0, CAP:2 * CAP], drawn[E:2 * E, :]).then_inc(s_mv, 16)
                sp.wait_ge(s_st, 48)

            @block.gpsimd
            def _(pool):
                pool.memset(zero[:, :], 0.0).then_inc(s_zero, 1)

            @block.scalar
            def _(act):
                act.wait_ge(s_shift, 1)
                act.activation(ex[:, :, :], ex[:, :, :], ACT.Exp).then_inc(s_exp, 1)

            @block.vector
            def _(dve):
                link = Links(dve, s_dv, 7 + NTT, 0)
                dve.wait_ge(s_in, 64)
                for i in range(NTT):
                    link(dve.max(top[:, i, :], L[:, i, :]))
                    ins = dve.match_replace(rest[:, i, :], top[:, i, :], L[:, i, :], -3.0e38)
                link(ins)
                dve.tensor_tensor(sel[:, :, :, :].rearrange("p i h e -> p h i e"),
                                  rest[:, :, :].rearrange("p (h i) e -> p h i e", h=2),
                                  L[:, :, :].rearrange("p (h i) e -> p h i e", h=2), ALU.not_equal).then_inc(s_sel, 1)
                dve.tensor_tensor(ex[:, :, :], L[:, :, :], bcast(top[:, :, 0]), ALU.subtract).then_inc(s_shift, 1)
                for n in range(HT // 4):
                    dve.wait_ge(s_mt, n + 1)
                    dve.tensor_tensor(key[:, 0, n * D:(n + 1) * D], MT[:, n % 2, :], rev[:, n * D:(n + 1) * D],
                                      ALU.mult).then_inc(s_key, 1)
                dve.wait_ge(s_exp, 1)
                link(dve.tensor_reduce(zsum[:, :], ex[:, :, :], AX.X, ALU.add))
                sel_t = sel[:, :, :, :].rearrange("p i h e -> p h i e")
                ex_t = ex[:, :, :].rearrange("p (h i) e -> p h i e", h=2)
                link(dve.tensor_tensor(ex_t, ex_t, sel_t, ALU.mult))
                link(dve.tensor_reduce(den[:, :], ex[:, :, :], AX.X, ALU.add))
                link(dve.scalar_tensor_tensor(den[:, :], zsum[:, :], 1e-20, den[:, :], ALU.mult, ALU.add))
                link(dve.reciprocal(den[:, :], den[:, :]))
                dve.tensor_tensor(ex[:, :, :], ex[:, :, :], bcast(den[:, :]), ALU.mult).then_inc(s_gate, 1)
                dve.wait_ge(s_key, HT // 4)
                for r in range(ROUNDS):
                    v = drawn[:, 8 * r:8 * r + 8]
                    dve.max(v, key[:, r % 2, :]).then_inc(s_drawn, 1)
                    dve.wait_ge(s_drawn, r + 1)
                    if r + 1 < ROUNDS:
                        dve.match_replace(key[:, (r + 1) % 2, :], v, key[:, r % 2, :], 0.0).then_inc(s_key, 1)
                        dve.wait_ge(s_key, HT // 4 + r + 1)
                dve.wait_ge(s_mv, 32)
                for r in range(ROUNDS):
                    v = first[:, 8 * r:8 * r + 8]
                    dve.max(v, both[:, r % 2, :]).then_inc(s_first, 1)
                    dve.wait_ge(s_first, r + 1)
                    if r + 1 < ROUNDS:
                        dve.match_replace(both[:, (r + 1) % 2, :], v, both[:, r % 2, :], 0.0).then_inc(s_key, 1)
                        dve.wait_ge(s_key, HT // 4 + ROUNDS + r)
                dve.wait_ge(s_vt, 1)
                link(dve.tensor_copy(vt[:, :], VT[:, :]))
                dve.tensor_scalar(tmp[:, :], vt[:, :], 0.0, pcol[:, 0:1], ALU.is_equal, ALU.mult).then_inc(s_shift, 1)
                dve.wait_ge(s_shift, 2)
                dve.tensor_tensor(tmp[:, :], tmp[:, :], vt[:, :], ALU.subtract).then_inc(s_shift, 1)
                dve.wait_ge(s_shift, 3)
                dve.tensor_scalar(slots[:, :], tmp[:, :], float(T), None, ALU.add).then_inc(s_shift, 1)
                link.close()

            @block.tensor
            def _(pe):
                pe.wait_ge(s_in, 64)
                pe.wait_ge(s_sel, 1)
                for n in range(HT // 4):
                    if n >= 2:
                        pe.wait_ge(s_key, n - 1)
                    for i in range(4):
                        ins = pe.transpose(MT[:, n % 2, i * P:(i + 1) * P],
                                           sel[:, 4 * n + i, :, :].rearrange("p h e -> p (h e)"), ident[:, :])
                    ins.then_inc(s_mt, 1)
                pe.wait_ge(s_first, ROUNDS)
                pe.transpose(VT[:, :], first[:, :], ident[0:E, 0:E]).then_inc(s_vt, 1)


def experts(nc, w_gate, w_up, w_down, ident_d, table, out, slots):
    RING = 4
    GROUPS = E // RING
    FJ = 2
    FP = FE // FJ
    with ExitStack() as ctx:
        def sb(name, shape, dt=F32):
            return ctx.enter_context(nc.sbuf_tensor(name, shape, dt))

        def pb(name, shape):
            return ctx.enter_context(nc.psum_tensor(name, shape, F32))

        def sem(name):
            return ctx.enter_context(nc.semaphore(name))

        XP = pb("xt_ps", [P, 2, D])
        GU = pb("gu_ps", [P, 2, D])
        HP = pb("ht_ps", [P, D])
        YP = pb("y_ps", [P, 2, D])
        ident = sb("e_ident", [P, P])
        wgu = sb("e_gate_up", [P, RING, 2, KT * FE])
        wd = sb("e_down", [FP, RING, FJ * D])
        xg = sb("e_rows", [P, RING, ROW])
        idx = sb("e_index", [P, RING], I32)
        xT = sb("e_xT", [P, 2, D])
        sg = sb("e_silu", [P, 2, FE])
        hm = sb("e_hidden", [P, 2, FE])
        hT = sb("e_hiddenT", [FP, 2, FJ * P])
        wt = sb("e_weight", [P, RING])
        ys = sb("e_y", [P, 2, D])

        s_w = [sem(f"e_w{q}") for q in range(RING)]
        s_xg = [sem(f"e_xg{q}") for q in range(RING)]
        s_passed = sem("e_passed")
        s_c, s_idx, s_sc = sem("e_const"), sem("e_idx"), sem("e_scattered")
        s_xp, s_xT, s_wt, s_gu, s_sg, s_hm = (sem("e_" + n) for n in ("xp", "xT", "wt", "gu", "sg", "hm"))
        s_hp, s_hT, s_y, s_ys = (sem("e_" + n) for n in ("hp", "hT", "y", "ys"))

        def over_groups(eng, group):
            group(0, True, False)
            with eng.Fori(1, GROUPS - 1) as i:
                group(i, False, False)
            group(GROUPS - 1, False, True)

        with nc.Block() as block:
            @block.sync
            def _(sp):
                sp.dma_start(ident[:, :], ident_d).then_inc(s_c, 16)

                def group(i, first, last):
                    for q in range(RING):
                        n = i * RING + q
                        if not first:
                            sp.wait_ge(s_y, n - RING + 1)
                        for m, d in enumerate((w_gate, w_up)):
                            sp.dma_start(wgu[:, q, m, :], d[bass.ds(n, 1)].rearrange(
                                "o (p k) f -> (o p) (k f)", k=KT)).then_inc(s_w[q], 16)
                        sp.dma_start(wd[:, q, :], w_down[bass.ds(n, 1)].rearrange(
                            "o (p j) n -> (o p) (j n)", j=FJ)).then_inc(s_w[q], 16)

                over_groups(sp, group)

            @block.gpsimd
            def _(pool):
                def gather(n, q, first):
                    if not first:
                        pool.wait_ge(s_ys, n - RING + 1)
                    pool.sem_inc(s_passed, 1)
                    pool.tensor_copy(idx[:, q:q + 1], slots[:, bass.ds(n, 1)]).then_inc(s_idx, 1)
                    pool.wait_ge(s_idx, n + 1)
                    pool.sem_inc(s_passed, 1)
                    pool.indirect_dma_start(xg[:, q, :], None, table, bass.IndirectOffsetOnAxis(idx[:, q:q + 1], 0))\
                        .then_inc(s_xg[q], 16)

                def scatter(n, q, first):
                    pool.wait_ge(s_ys, n + 1)
                    if not first:
                        pool.wait_ge(s_sc, 16 * n)
                    pool.sem_inc(s_passed, 1)
                    pool.indirect_dma_start(out, bass.IndirectOffsetOnAxis(idx[:, q:q + 1], 0), ys[:, q % 2, :], None,
                                            compute_op=ALU.add).then_inc(s_sc, 16)

                def group(i, first, last):
                    for q in range(RING):
                        n = i * RING + q
                        scatter(n, q, first and q == 0)
                        if not last:
                            pool.wait_ge(s_sc, 16 * (n + 1))
                            gather(n + RING, q, False)

                for q in range(RING):
                    gather(q, q, True)
                over_groups(pool, group)
                pool.wait_ge(s_sc, 16 * E)

            @block.scalar
            def _(act):
                def x_out(n, q):
                    act.wait_ge(s_xp, n + 1)
                    act.activation(xT[:, q % 2, :], XP[:, q % 2, :], ACT.Copy).then_inc(s_xT, 1)

                def y_out(n, q, first):
                    act.wait_ge(s_y, n + 1)
                    act.wait_ge(s_wt, n + 1)
                    if not first:
                        act.wait_ge(s_sc, 16 * (n - 1))
                    act.activation(ys[:, q % 2, :], YP[:, q % 2, :], ACT.Copy, scale=wt[:, q:q + 1]).then_inc(s_ys, 1)

                def group(i, first, last):
                    for q in range(RING):
                        n = i * RING + q
                        act.wait_ge(s_gu, n + 1)
                        act.activation(sg[:, q % 2, :], GU[:, q % 2, 0:FE], ACT.Silu).then_inc(s_sg, 1)
                        if not (last and q == RING - 1):
                            x_out(n + 1, (q + 1) % RING)
                        if not (first and q == 0):
                            y_out(n - 1, (q - 1) % RING, first and q <= 2)

                x_out(0, 0)
                over_groups(act, group)
                y_out(E - 1, RING - 1, False)

            @block.vector
            def _(dve):
                def group(i, first, last):
                    for q in range(RING):
                        n = i * RING + q
                        dve.wait_ge(s_xg[q], i * 16 + 16)
                        dve.tensor_copy(wt[:, q:q + 1], xg[:, q, bass.ds(n + D, 1)]).then_inc(s_wt, 1)
                        dve.wait_ge(s_sg, n + 1)
                        dve.tensor_tensor(hm[:, q % 2, :], sg[:, q % 2, :], GU[:, q % 2, FE:2 * FE], ALU.mult)\
                           .then_inc(s_hm, 1)
                        dve.wait_ge(s_hp, n + 1)
                        dve.tensor_copy(hT[:, q % 2, :], HP[0:FP, 0:FJ * P]).then_inc(s_hT, 1)

                over_groups(dve, group)

            @block.tensor
            def _(pe):
                pe.wait_ge(s_c, 16)

                def turn_x(n, q, turn):
                    pe.wait_ge(s_xg[q], turn * 16 + 16)
                    for k in range(KT):
                        ins = pe.transpose(XP[:, q % 2, k * P:(k + 1) * P], xg[:, q, k:D:KT], ident[:, :])
                    ins.then_inc(s_xp, 1)

                def down(n, q, first):
                    pe.wait_ge(s_hT, n + 1)
                    if not first:
                        pe.wait_ge(s_ys, n - 1)
                    for j in range(FJ):
                        ins = pe.matmul(YP[:, q % 2, :], hT[:, q % 2, j * P:(j + 1) * P],
                                        wd[:, q, j * D:(j + 1) * D], start=(j == 0), stop=(j == FJ - 1))
                    ins.then_inc(s_y, 1)

                def group(i, first, last):
                    for q in range(RING):
                        n = i * RING + q
                        pe.wait_ge(s_xT, n + 1)
                        pe.wait_ge(s_w[q], i * 48 + 48)
                        for k in range(KT):
                            ins = pe.matmul(GU[:, q % 2, 0:2 * FE].rearrange("p (m f) -> p m f", m=2),
                                            xT[:, q % 2, k * P:(k + 1) * P], wgu[:, q, :, k * FE:(k + 1) * FE],
                                            start=(k == 0), stop=(k == KT - 1))
                        ins.then_inc(s_gu, 1)
                        if not (last and q == RING - 1):
                            turn_x(n + 1, (q + 1) % RING, i + (q == RING - 1))
                        if not (first and q == 0):
                            down(n - 1, (q - 1) % RING, first and q <= 2)
                        pe.wait_ge(s_hm, n + 1)
                        for j in range(FJ):
                            ins = pe.transpose(HP[0:FP, j * P:(j + 1) * P], hm[:, q % 2, j:FE:FJ], ident[:, :])
                        ins.then_inc(s_hp, 1)

                turn_x(0, 0, 0)
                over_groups(pe, group)
                down(E - 1, RING - 1, False)


def transformer(nc, x, wqk, wvT, woT, lam, w1T, w3T, W2T, wr, wf, wc, wo, ln_scale, rwT, w_gate, w_up, w_down,
                ident, mask, had, rev, pcol, out):
    T = x.shape[0]
    batches = T // S
    chunks = T // D

    def scratch(name, shape):
        return nc.dram_tensor(name, shape, F32, kind="Internal").ap()

    w2p = scratch("w2_transformed", (HID, D))
    xt_hi, xt_lo = scratch("xt_hi", (chunks, P, KT, D)), scratch("xt_lo", (chunks, P, KT, D))
    x1, x1b, x2 = scratch("x_attn", (T, D)), scratch("x_half", (T, D)), scratch("x_layer0", (T, D))
    table = scratch("token_table", (T + P, ROW))
    logits = scratch("router_logits", (batches, P, NT * E))

    hadamard_w2(nc, W2T, had, w2p)
    with nc.cleanup_on_exit():
        attention(nc, x, wqk, wvT, woT, lam, ident, mask, xt_hi, xt_lo, x1, batches)
    dense_ffn(nc, w1T, w3T, w2p, xt_hi, xt_lo, x1, x1b, x2, chunks)
    recurrence(nc, wr, wf, wc, wo, ln_scale, rwT, ident, x2, table, logits, out, batches)
    with nc.sbuf_tensor("slots", [P, E], I32) as slots:
        routing(nc, logits, rev, pcol, ident, table, out, slots, batches)
        experts(nc, w_gate, w_up, w_down, ident, table, out, slots)


def by_partition(w):
    return np.ascontiguousarray(w.reshape(-1, P, w.shape[1]).transpose(1, 0, 2))


def kernel(**inputs):
    import concourse.bacc as _bacc
    from concourse.bass_utils import run_bass_kernel_spmd as _run

    a = {k: np.asarray(v) for k, v in inputs.items()}
    f32 = np.float32
    x = a["L0_attn_x"]
    B, _, _ = x.shape
    T = B * S
    wq, wk = a["L0_attn_wq"], a["L0_attn_wk"]

    def two(w, h):
        return [w[DH * h:DH * (h + 1)], w[DH * (h + HEADS):DH * (h + HEADS + 1)]]

    wqk = np.stack([by_partition(np.concatenate(two(wq, h) + two(wk, h), 0).T) for h in range(HEADS)])
    lam = np.stack([a["L0_attn_" + n] for n in ("l_q1", "l_k1", "l_q2", "l_k2")])
    rw = a["L1_ffn_router_w"]

    ident = np.eye(P, dtype=f32)
    query, key = np.arange(P)[:, None], np.arange(2 * P)[None]
    mask = np.concatenate([np.where(key > query + P * t, MASKED, 0.0) for t in range(2)], 1).astype(f32)
    had = np.ones((1, 1), f32)
    while had.shape[0] < P:
        had = np.block([[had, had], [had, -had]])
    rev = np.concatenate([np.tile(T - h * (T // 2) - np.arange(T // 2), (E, 1)) for h in range(2)], 0).astype(f32)
    pcol = np.arange(P, dtype=f32)[:, None]

    arrays = {
        "x": x.reshape(T, D),
        "wqk": wqk,
        "wvT": by_partition(a["L0_attn_wv"].T),
        "woT": by_partition(a["L0_attn_wo"].T),
        "lam": np.broadcast_to(lam, (P,) + lam.shape),
        "w1T": a["L0_ffn_W1"].T,
        "w3T": a["L0_ffn_W3"].T,
        "W2T": a["L0_ffn_W2"].T,
        "wr": by_partition(a["L1_attn_Wr"]),
        "wf": by_partition(a["L1_attn_Wf"]),
        "wc": by_partition(a["L1_attn_Wc"]),
        "wo": by_partition(a["L1_attn_Wo"]),
        "ln_scale": a["L1_attn_ln_scale"].reshape(KT, P).T,
        "rwT": by_partition(np.concatenate([rw, rw], 0).T),
        "w_gate": a["L1_ffn_w_gate"],
        "w_up": a["L1_ffn_w_up"],
        "w_down": a["L1_ffn_w_down"],
        "ident": ident, "mask": mask, "had": had, "rev": rev, "pcol": pcol,
    }
    nc = _bacc.Bacc("TRN2", target_bir_lowering=False, num_devices=1)
    sent, args = {}, {}
    for name, v in arrays.items():
        v = np.ascontiguousarray(v)
        sent[f"in_{name}_dram"] = v
        args[name] = nc.dram_tensor(f"in_{name}_dram", v.shape, mybir.dt.from_np(v.dtype), kind="ExternalInput").ap()
    out = nc.dram_tensor("out_0_dram", (T + P, D), F32, kind="ExternalOutput").ap()
    transformer(nc, out=out, **args)
    r = _run(nc, [sent], core_ids=[0])
    return r.results[0]["out_0_dram"][:T].reshape(B, S, D)
```

```python
import concourse.bass as bass
from concourse import mybir
from contextlib import ExitStack
import math
import numpy as np

F32 = mybir.dt.float32
F32R = mybir.dt.float32r
BF16 = mybir.dt.bfloat16
I32 = mybir.dt.int32
ALU = mybir.AluOpType
ACT = mybir.ActivationFunctionType
AX = mybir.AxisListType

P = 128
D = 512
KT = D // P
S = 1024
NT = S // P
HEADS = 8
DH = D // HEADS
HID = 2048
E = 64
TOPK = 8
CAP = 128
FE = 192
L_INIT = 0.8 - 0.6 * math.exp(-0.3 * 1)
LN_EPS = 1e-5
ATT_EPS = 1e-6
RMS_EPS = 1e-5
MASKED = -1e30
ROW = D + E


class Links:

    def __init__(self, eng, sem, per_turn, turn, passed=None):
        self.eng, self.sem, self.per_turn, self.turn, self.n = eng, sem, per_turn, turn, 0
        self.passed = passed

    def __call__(self, ins):
        self.n += 1
        ins.then_inc(self.sem, 1)
        self.eng.wait_ge(self.sem, self.turn * self.per_turn + self.n)
        if self.passed:
            self.eng.sem_inc(self.passed, 1)

    def close(self):
        assert self.n == self.per_turn, (self.n, self.per_turn)


def three_products(pe, out, w, x, first, last):
    pe.matmul(out, w[0], x[0], start=first, stop=False)
    pe.matmul(out, w[0], x[1], start=False, stop=False)
    return pe.matmul(out, w[1], x[0], start=False, stop=last)


def hadamard_w2(nc, W2T, had, w2p):
    NC = HID // P
    PIECES = 4
    ND = D // PIECES
    CB = 4
    NB = NC // CB
    LEVELS = int(math.log2(NC))
    with ExitStack() as ctx:
        def sb(name, shape, dt=F32):
            return ctx.enter_context(nc.sbuf_tensor(name, shape, dt))

        def sem(name):
            return ctx.enter_context(nc.semaphore(name))

        bufs = [sb("had_ping", [P, PIECES, NC, ND]), sb("had_pong", [P, PIECES, NC, ND])]
        h_f = sb("had_f", [P, P])
        h_r = sb("had_r", [P, P], F32R)
        hi = sb("had_hi", [P, 2, CB * ND], F32R)
        lo = sb("had_lo", [P, 2, CB * ND], F32R)
        out = sb("had_out", [P, 4, CB * ND])
        ps = ctx.enter_context(nc.psum_tensor("had_ps", [P, 2, CB * ND], F32))
        s_in, s_c, s_h = [sem(f"had_in{i}") for i in range(PIECES)], sem("had_const"), sem("had_hr")
        s_sum, s_dif, s_dif2 = sem("had_sum"), sem("had_dif"), sem("had_dif_pool")
        s_hi, s_lo, s_mm, s_out = sem("had_hi_done"), sem("had_lo_done"), sem("had_mm"), sem("had_scaled")
        s_st = [sem(f"had_store{i}") for i in range(4)]
        src_v = W2T.rearrange("(c p) n -> p c n", p=P)
        dst_v = w2p.rearrange("(c p) n -> p c n", p=P)

        def block_of(i):
            return i // NB, slice(i % NB * CB, (i % NB + 1) * CB)

        def chunk(i):
            q, c = block_of(i)
            return bufs[LEVELS % 2][:, q, c, :].rearrange("p c n -> p (c n)")

        with nc.Block() as block:
            @block.sync
            def _(sp):
                for q in range(PIECES):
                    sp.dma_start(bufs[0][:, q, :, :], src_v[:, :, q * ND:(q + 1) * ND]).then_inc(s_in[q], 16)
                    if q == 0:
                        sp.dma_start(h_f[:, :], had).then_inc(s_c, 16)
                for i in range(PIECES * NB):
                    q, c = block_of(i)
                    sp.wait_ge(s_out, i + 1)
                    sp.dma_start(dst_v[:, c, q * ND:(q + 1) * ND],
                                 out[:, i % 4, :].rearrange("p (c n) -> p c n", c=CB)).then_inc(s_st[i % 4], 16)
                for i in range(4):
                    sp.wait_ge(s_st[i], 16 * PIECES * NB // 4)

            def halves(level, q):
                h = 1 << level
                return [x[:, q, :, :].rearrange("p (g two h) n -> p g two (h n)", two=2, h=h)
                        for x in (bufs[level % 2], bufs[(level + 1) % 2])]

            def split(v):
                n = v.shape[1]
                if n > 1:
                    return v[:, 0:n // 2], v[:, n // 2:n]
                w = v.shape[2] // 2
                return v[:, :, 0:w], v[:, :, w:2 * w]

            @block.vector
            def _(dve):
                def low(i):
                    dve.wait_ge(s_hi, i + 1)
                    dve.tensor_tensor(lo[:, i % 2, :], chunk(i), hi[:, i % 2, :].bitcast(F32), ALU.subtract)\
                       .then_inc(s_lo, 1)

                for q in range(PIECES):
                    dve.wait_ge(s_in[q], 16)
                    for level in range(LEVELS):
                        a, b = halves(level, q)
                        if level:
                            n = q * LEVELS + level
                            dve.wait_ge(s_dif2, n)
                            dve.wait_ge(s_sum, n)
                            dve.wait_ge(s_dif, n)
                        dve.tensor_tensor(b[:, :, 0], a[:, :, 0], a[:, :, 1], ALU.add).then_inc(s_sum, 1)
                        dve.tensor_tensor(split(b[:, :, 1])[0], split(a[:, :, 0])[0], split(a[:, :, 1])[0], ALU.subtract)\
                           .then_inc(s_dif, 1)
                        if q:
                            low((q - 1) * NB + level)
                for k in range(NB):
                    low((PIECES - 1) * NB + k)

            @block.gpsimd
            def _(pool):
                for q in range(PIECES):
                    pool.wait_ge(s_in[q], 16)
                    for level in range(LEVELS):
                        a, b = halves(level, q)
                        if level:
                            n = q * LEVELS + level
                            pool.wait_ge(s_sum, n)
                            pool.wait_ge(s_dif, n)
                            pool.wait_ge(s_dif2, n)
                        pool.tensor_tensor(split(b[:, :, 1])[1], split(a[:, :, 0])[1], split(a[:, :, 1])[1], ALU.subtract)\
                            .then_inc(s_dif2, 1)

            @block.scalar
            def _(act):
                act.wait_ge(s_c, 16)
                act.activation(h_r[:, :], h_f[:, :], ACT.Copy).then_inc(s_h, 1)

                def scaled(i):
                    act.wait_ge(s_mm, i + 1)
                    if i >= 4:
                        act.wait_ge(s_st[i % 4], 16 * (i // 4))
                    act.activation(out[:, i % 4, :], ps[:, i % 2, :], ACT.Copy, scale=1.0 / math.sqrt(HID))\
                       .then_inc(s_out, 1)

                for i in range(PIECES * NB):
                    if i >= 2:
                        scaled(i - 2)
                    if i % NB == 0:
                        n = (i // NB + 1) * LEVELS
                        act.wait_ge(s_sum, n)
                        act.wait_ge(s_dif, n)
                        act.wait_ge(s_dif2, n)
                    act.activation(hi[:, i % 2, :], chunk(i), ACT.Copy).then_inc(s_hi, 1)
                scaled(PIECES * NB - 2)
                scaled(PIECES * NB - 1)

            @block.tensor
            def _(pe):
                pe.wait_ge(s_h, 1)
                for i in range(PIECES * NB):
                    pe.wait_ge(s_lo, i + 1)
                    if i >= 2:
                        pe.wait_ge(s_out, i - 1)
                    pe.matmul(ps[:, i % 2, :], h_r[:, :], hi[:, i % 2, :], start=True, stop=False)
                    pe.matmul(ps[:, i % 2, :], h_r[:, :], lo[:, i % 2, :], start=False, stop=True).then_inc(s_mm, 1)


def attention(nc, x, wqk, wvT, woT, lam, ident_d, mask_d, xth_d, xtl_d, x1, batches):
    SUBS = 2
    GQ = 2 * P
    NG = S // GQ
    STEPS = HEADS * NT
    LAG = 2
    U = NT * SUBS
    TH = sum(-(-2 * (g + 1) // 4) for g in range(NG)) * 2
    TTK = 2 * NT + HEADS * TH + 2 * NT
    TTH = TTK - NT
    LOADS = HEADS + 2
    QUARTERS = [(1, 0), (0, 0), (1, 1), (0, 1)]
    AT_STEPS = [0, 1, 3, 4]
    with ExitStack() as ctx:
        def sb(name, shape, dt=F32):
            return ctx.enter_context(nc.sbuf_tensor(name, shape, dt))

        def pb(name, shape):
            return ctx.enter_context(nc.psum_tensor(name, shape, F32))

        def sem(name):
            return nc.alloc_semaphore(name)

        SC = pb("score_ps", [P, 4, D])
        TT = pb("turn_ps", [P, 2, D])
        PV = pb("pv_ps", [P, D])
        PJ = pb("qk_ps", [P, D])

        xT = [sb("xT_hi", [P, KT, S], F32R), sb("xT_lo", [P, KT, S], F32R)]
        W = [sb("wvo_hi", [P, KT, D], F32R), sb("wvo_lo", [P, KT, D], F32R)]
        V = sb("values", [P, NT, HEADS, 2 * DH], F32R)
        Q = [[sb(f"q_{s}{r}", [P, S], F32R) for s in "ab"] for r in range(2)]
        K = sb("k_all", [P, 2, 4, S], F32R)
        w_in = sb("weight_in", [P, KT * 2 * P])
        w_in_qk = w_in[:, :].rearrange("p (k n) -> p k n", k=KT)
        w_in_wo = w_in[:, :].rearrange("p (k n) -> p k n", n=D)
        wq = [sb("wqk_hi", [P, KT, 2 * P], F32R), sb("wqk_lo", [P, KT, 2 * P], F32R)]
        AT = [sb("attT_hi", [P, NT, GQ], F32R), sb("attT_lo", [P, NT, GQ], F32R)]
        PR = sb("probs", [P, 3, SUBS, S])
        xn = PR[:, 0, 0, :].rearrange("p (t n) -> p t n", t=2)
        sq = [PR[:, 1 - h, :, :].rearrange("p s (t n) -> p (s t) n", n=D) for h in range(2)]
        wv_in = PR[:, 1, :, :].rearrange("p s (t n) -> p (s t) n", n=D)
        x1_sb = PR[:, 2, 0, :].rearrange("p (t n) -> p t n", t=2)
        grp = PR[:, 2, 1, 0:D].rearrange("p (t n) -> p t n", n=D // 8)
        inv = PR[:, 2, 1, D:2 * D].rearrange("p (t n) -> p t n", n=D // 8)
        O = sb("heads_out", [P, NT, D])
        x_in = sb("x_in", [P, 2, D])
        OT = sb("outT", [P, GQ])
        ident = sb("ident_sb", [P, P])
        fold = sb("fold", [P, DH])
        identb = sb("identb", [P, P], BF16)
        maskf = O[:, 0, :]
        mask = sb("maskb", [P, 2, GQ], BF16)
        lam_sb = sb("lam_sb", [P, 4, HEADS])
        lam_p = sb("lam_prod", [P, 2, HEADS])
        lam_s = sb("lam_sum", [P, 4])
        stats = sb("ln_stats", [P, 6])
        mv = sb("ln_mv", [P, 2, 2])
        rstd = sb("ln_rstd", [P, 2])
        nmax = sb("neg_max", [P, U])
        sums = sb("exp_sums", [P, NT, HEADS, SUBS])
        rsum = sb("sum_recip", [P, NT, HEADS, SUBS])
        comb = sb("comb", [P, 4])
        neg_half = sb("neg_half", [P, 1])
        newton = sb("newton", [P, NT // 2, D // 8])

        s_wv, s_c, s_fold = sem("a_wv_in"), sem("a_const"), sem("a_fold")
        s_wvh, s_wvl, s_wfree, s_cast = sem("a_wv_high"), sem("a_wv_low"), sem("a_wvo_free"), sem("a_cast")
        s_x = [sem("a_x0"), sem("a_x1")]
        s_xl = [sem(f"a_x_pair{i}") for i in range(NT // 2)]
        s_xfree, s_xn, s_prime = sem("a_xfree"), sem("a_xn"), sem("a_prime")
        s_xts = sem("a_xt_stored")
        s_ttf, s_tth, s_ttfree = sem("a_tt_filled"), sem("a_tt_high"), sem("a_tt_free")
        s_win, s_wqh, s_wql = sem("a_win"), sem("a_wq_high"), sem("a_wq_low")
        s_pjf, s_pjh, s_pjfree, s_kdup = sem("a_pj_filled"), sem("a_pj_high"), sem("a_pj_free"), sem("a_kdup")
        s_scf, s_scfree = sem("a_sc_filled"), sem("a_sc_free")
        s_max, s_rs, s_cc = sem("a_max"), sem("a_recip"), sem("a_comb_factor")
        s_comb, s_scaled = sem("a_comb"), sem("a_scaled")
        s_pv, s_ot, s_ox, s_oxf = sem("a_pv"), sem("a_ot"), sem("a_ox"), sem("a_ox_free")
        s_var, s_root, s_half_set = sem("a_var"), sem("a_root"), sem("a_half_set")
        s_passed = sem("a_passed")
        s_dv, s_sq, s_ms, s_sqrt = sem("a_dve_chain"), sem("a_squares"), sem("a_mean_sq"), sem("a_sqrt")
        s_xn2 = sem("a_heads_normed")
        s_x1, s_st = sem("a_x1_ready"), [sem("a_st0"), sem("a_st1")]

        def x_tile(t):
            return PR[:, 0, 1, t * D:(t + 1) * D] if t < 2 else x_in[:, t - 2, :] if t < 4 else \
                PR[:, 2, (t - 4) // 2, (t % 2) * D:(t % 2 + 1) * D]

        def width(i):
            return GQ * (i % NT // 2 + 1)

        def bank(u):
            return u % 4 if u < NT else 2 * (u % 2)

        def score_tile(u):
            n = width(u // SUBS)
            return SC[:, bank(u), 0:n] if u < NT else \
                SC[:, bank(u):bank(u) + 2, :].rearrange("p b n -> p (b n)")[:, 0:n]

        def bank_before(u):
            mine = {bank(u % U)} | ({bank(u % U) + 1} if u % U >= NT else set())
            for v in range(u - 1, -1, -1):
                if mine & ({bank(v % U)} | ({bank(v % U) + 1} if v % U >= NT else set())):
                    return v

        def blocks(i):
            n = width(i) // P
            return [(k, min(4, n - k)) for k in range(0, n, 4)]

        def turn_use(i):
            return 2 * NT + i // NT * TH + sum(len(blocks(j)) for j in range(i % NT))

        def pair_use(base, t, second):
            return base + (0 if t == 0 and not second else (2 * t + 2 if second and t < NT - 1 else
                           2 * t + 1 if second else 2 * t - 1))

        def x_use(t):
            return pair_use(0, t, False)

        def v_use(t):
            return pair_use(0, t, True)

        def o_use(t):
            return pair_use(2 * NT + HEADS * TH, t, False)

        def wo_use(t):
            return pair_use(2 * NT + HEADS * TH, t, True)

        def product_bank(t):
            return SC[:, 2 + t % 2, :]

        def group_at(i, lag):
            return (i - lag) // 2 if i >= lag and (i - lag) % 2 == 0 and (i - lag) // 2 < HEADS * NG else None

        FIRST_QUARTERS = {3: (0,), 4: (1,), 7: (2, 3)}
        lo64, hi64 = slice(0, DH), slice(DH, P)

        with nc.Block() as block:
            @block.sync
            def _(sp):
                sp.dma_start(ident[:, :], ident_d).then_inc(s_c, 16)
                sp.dma_start(maskf, mask_d).then_inc(s_c, 16)
                sp.dma_start(lam_sb[:, :, :], lam).then_inc(s_c, 16)
                sp.dma_start(w_in_qk, wqk[0]).then_inc(s_win, 16)
                sp.dma_start(wv_in, wvT).then_inc(s_wv, 16)
                for i in range(2):
                    sp.sem_inc(s_st[i], 16)
                with sp.Fori(0, batches) as b:
                    def load_x(dst, t, arrived):
                        sp.dma_start(dst, x[bass.ds(b * S + t * P, P), :]).then_inc(arrived, 16)

                    def load_again(t):
                        sp.wait_ge(s_xfree, b * (NT + 2) + 2 + t + 1)
                        load_x(x_in[:, t % 2, :], t, s_x[t % 2])

                    def load_wqk(h):
                        sp.wait_ge(s_wql, b * LOADS + h)
                        sp.dma_start(w_in_qk, wqk[h % HEADS]).then_inc(s_win, 16)

                    def double_keys(h, half):
                        sp.wait_ge(s_pjfree, b * 4 * HEADS + 4 * h + 2 * half + 1 + 1)
                        c = slice(half * D, (half + 1) * D)
                        for s, src, dst in ((0, lo64, hi64), (1, hi64, lo64)):
                            for part in range(2):
                                v = K[:, h % 2, 2 * s + part, c].bitcast(F32)
                                sp.dma_start(v[dst, :], v[src, :]).then_inc(s_kdup, 16)

                    for t in range(NT):
                        if t in (2, 3):
                            sp.wait_ge(s_xfree, b * (NT + 2) + t - 1)
                        if t == 4:
                            for i in range(2):
                                sp.wait_ge(s_st[i], 16 * (b * (NT // 2) + 1))
                        load_x(x_tile(t), t, s_xl[t // 2])
                    load_wqk(1)
                    double_keys(0, 0)
                    sp.wait_ge(s_ttfree, b * TTK + 2 + x_use(NT - 1) + 1)
                    for part, dram in ((0, xth_d), (1, xtl_d)):
                        for half in range(2):
                            sp.dma_start(dram[bass.ds(b * 2 + half, 1)].rearrange("o p k n -> (o p) k n"),
                                         xT[part][:, :, half * D:(half + 1) * D].bitcast(F32)).then_inc(s_xts, 16)
                    double_keys(0, 1)
                    for hd in range(HEADS - 1):
                        load_wqk(hd + 2)
                        double_keys(hd + 1, 0)
                        double_keys(hd + 1, 1)
                    for t in range(2):
                        load_again(t)
                    for half in range(2):
                        sp.wait_ge(s_wql, b * LOADS + HEADS + 1 + half)
                        sp.dma_start(w_in_wo, woT[:, 2 * half:2 * half + 2, :]).then_inc(s_win, 16)
                    sp.wait_ge(s_ms, 2 * b + 2)
                    sp.dma_start(wv_in, wvT).then_inc(s_wv, 16)
                    for t in range(NT):
                        if t + 2 < NT:
                            load_again(t + 2)
                        sp.wait_ge(s_x1, b * NT + t + 1)
                        sp.dma_start(x1[bass.ds(b * S + t * P, P), :], x1_sb[:, t % 2, :]).then_inc(s_st[t % 2], 16)
                sp.wait_ge(s_xts, 64 * batches)
                for i in range(2):
                    sp.wait_ge(s_st[i], 16 * (1 + batches * (NT // 2)))
                sp.wait_ge(s_wv, 16 * (batches + 1))
                sp.wait_ge(s_win, 16 * (1 + LOADS * batches))

            @block.vector
            def _(dve):
                for _i in range(2):
                    dve.sem_inc(s_xfree, 1)
                    dve.sem_inc(s_ttfree, 1)
                dve.sem_inc(s_oxf, 1)
                dve.sem_inc(s_pjfree, 1)
                dve.sem_inc(s_wfree, 1)
                dve.wait_ge(s_c, 48)
                dve.tensor_tensor(fold[:, :], ident[:, 0:DH], ident[:, DH:P], ALU.add).then_inc(s_fold, 1)
                link = Links(dve, s_prime, 4, 0)
                link(dve.tensor_tensor(lam_p[:, :, :], lam_sb[:, 0:4:2, :], lam_sb[:, 1:4:2, :], ALU.mult))
                link(dve.tensor_reduce(lam_s[:, 0:2], lam_p[:, :, :], AX.X, ALU.add))
                dve.wait_ge(s_cast, 3)
                link(dve.tensor_tensor(lam_s[:, 2:3], lam_s[:, 1:2], lam_s[:, 0:1], ALU.subtract))
                link(dve.tensor_scalar(lam_s[:, 3:4], lam_s[:, 2:3], L_INIT, None, ALU.subtract))
                link.close()

                with dve.Fori(0, batches) as b:
                    link = Links(dve, s_dv, 2 * NT + NT + 2 * 5, b, passed=s_passed)

                    def low(use, high_use, out, in_, hi):
                        dve.wait_ge(s_tth, b * TTH + high_use + 1)
                        dve.tensor_tensor(out, in_, hi.bitcast(F32), ALU.subtract).then_inc(s_ttfree, 1)

                    def ln_stats(t):
                        dve.wait_ge(s_xl[t // 2], 32 * (b + 1))
                        link(dve.bn_stats(stats[:, :], x_tile(t)))
                        link(dve.bn_aggr(mv[:, t % 2, :], stats[:, :]))
                        dve.tensor_scalar(rstd[:, t % 2:t % 2 + 1], mv[:, t % 2, 1:2], LN_EPS, None, ALU.add)\
                           .then_inc(s_var, 1)

                    def ln(t):
                        dve.wait_ge(s_root, b * NT + t + 1)
                        if t >= 2:
                            dve.wait_ge(s_ttf, b * TTK + x_use(t - 2) + 1)
                        dve.tensor_scalar(xn[:, t % 2, :], x_tile(t), mv[:, t % 2, 0:1],
                                          rstd[:, t % 2:t % 2 + 1], ALU.subtract, ALU.mult).then_inc(s_xn, 1)
                        if t in (2, 3):
                            dve.wait_ge(s_xn, b * NT + t + 1)
                            dve.sem_inc(s_xfree, 1)

                    def proj_low(h, quarter):
                        m, half = QUARTERS[quarter]
                        c, r = slice(half * D, (half + 1) * D), h % 2
                        dve.wait_ge(s_pjh, b * 4 * HEADS + 4 * h + quarter + 1)
                        if m == 0:
                            dve.scalar_tensor_tensor(Q[r][0][hi64, c], PJ[lo64, :], 0.125,
                                                     Q[r][0][lo64, c].bitcast(F32), ALU.mult, ALU.subtract)
                            ins = dve.scalar_tensor_tensor(Q[r][1][lo64, c], PJ[hi64, :], 0.125,
                                                           Q[r][1][hi64, c].bitcast(F32), ALU.mult, ALU.subtract)
                        else:
                            for s, rows in ((0, lo64), (1, hi64)):
                                ins = dve.tensor_tensor(K[rows, r, 2 * s + 1, c], PJ[rows, :],
                                                        K[rows, r, 2 * s, c].bitcast(F32), ALU.subtract)
                        ins.then_inc(s_pjfree, 1)

                    dve.wait_ge(s_wvh, b + 1)
                    dve.tensor_tensor(W[1][:, :, :], wv_in, W[0][:, :, :].bitcast(F32), ALU.subtract)\
                       .then_inc(s_wvl, 1)
                    ln_stats(0)
                    ln_stats(1)
                    ln(0)
                    for t in range(NT):
                        if t + 2 < NT:
                            ln_stats(t + 2)
                        if t + 1 < NT:
                            ln(t + 1)
                        low(x_use(t), x_use(t), xT[1][:, :, t * P:(t + 1) * P],
                            TT[:, t % 2, :].rearrange("p (k n) -> p k n", k=KT),
                            xT[0][:, :, t * P:(t + 1) * P])
                        for v in ([t - 1] if t else []) + ([t] if t == NT - 1 else []):
                            low(v_use(v), v_use(v), V[:, v, :, DH:2 * DH],
                                product_bank(v).rearrange("p (h n) -> p h n", h=HEADS), V[:, v, :, 0:DH])
                            for quarter in FIRST_QUARTERS.get(v, ()):
                                proj_low(0, quarter)

                    def mean_square(half):
                        for t in range(4 * half, 4 * half + 4):
                            dve.wait_ge(s_sq, b * NT + t + 1)
                            link(dve.tensor_reduce(grp[:, t, :], sq[half][:, t % 4, :].rearrange("p (g n) -> p g n", n=8),
                                                   AX.X, ALU.add))
                        g = grp[:, 4 * half:4 * half + 4, :]
                        dve.tensor_scalar(g, g, 1.0 / 8, ATT_EPS, ALU.mult, ALU.add).then_inc(s_ms, 1)

                    def inverse_root(half):
                        g, r, n = grp[:, 4 * half:4 * half + 4, :], inv[:, 4 * half:4 * half + 4, :], newton[:, :, :]
                        dve.wait_ge(s_sqrt, 2 * b + half + 1)
                        link(dve.reciprocal(r, r))
                        link(dve.tensor_tensor(n, r, r, ALU.mult))
                        link(dve.tensor_tensor(n, n, g, ALU.mult))
                        link(dve.tensor_scalar(n, n, -0.5, 1.5, ALU.mult, ALU.add))
                        link(dve.tensor_tensor(r, r, n, ALU.mult))

                    def normalise(t):
                        o_g = O[:, t, :].rearrange("p (g n) -> p g n", n=8)
                        dve.scalar_tensor_tensor(o_g, o_g, 1.0 - L_INIT,
                                                 inv[:, t, :].unsqueeze(2).to_broadcast([P, D // 8, 8]),
                                                 ALU.mult, ALU.mult).then_inc(s_xn2, 1)

                    for i in range(STEPS + LAG + 2):
                        hd, j = divmod(i, NT)

                        def maximum(s):
                            u = hd * U + 2 * j + s
                            dve.wait_ge(s_scf, b * HEADS * U + u + 1)
                            sc = score_tile(u % U)
                            dve.tensor_reduce(nmax[:, u % U:u % U + 1], sc, AX.X, ALU.max, negate=True)\
                               .then_inc(s_max, 1)

                        def map_low(part):
                            if LAG <= i < STEPS + LAG and part < len(blocks(i - LAG)):
                                use, t = turn_use(i - LAG) + part, i % 2
                                k, nb = blocks(i - LAG)[part]
                                low(use, use, AT[1][:, k:k + nb, t * P:(t + 1) * P],
                                    TT[:, use % 2, 0:nb * P].rearrange("p (k n) -> p k n", k=nb),
                                    AT[0][:, k:k + nb, t * P:(t + 1) * P])

                        def reciprocals():
                            if 1 <= i <= STEPS:
                                dve.wait_ge(s_scfree, b * HEADS * U + 2 * i)
                                dve.reciprocal(rsum[:, (i - 1) % NT, (i - 1) // NT, :],
                                               sums[:, (i - 1) % NT, (i - 1) // NT, :]).then_inc(s_rs, 1)

                        def factor():
                            if 1 <= i <= STEPS:
                                h1, j1 = divmod(i - 1, NT)
                                dve.wait_ge(s_rs, b * STEPS + i)
                                dve.scalar_tensor_tensor(comb[:, j1 % 4:j1 % 4 + 1], sums[:, j1, h1, 0:1],
                                                         lam_s[:, 3:4], rsum[:, j1, h1, 1:2], ALU.mult, ALU.mult)\
                                   .then_inc(s_cc, 1)

                        def output():
                            g = group_at(i, LAG + 3)
                            if g is not None:
                                dve.wait_ge(s_ox, b * HEADS * NG + g + 1)
                                for t in range(2):
                                    tile, h = g % NG * 2 + t, g // NG
                                    ins = dve.tensor_scalar(O[:, tile, h * DH:(h + 1) * DH],
                                                            PV[:, GQ + t * DH:GQ + (t + 1) * DH],
                                                            rsum[:, tile, h, 0:1], None, ALU.mult)
                                ins.then_inc(s_oxf, 1)

                        def project_low():
                            if j - 1 in AT_STEPS and hd + 1 < HEADS:
                                proj_low(hd + 1, AT_STEPS.index(j - 1))
                        if i < STEPS:
                            maximum(0)
                        reciprocals()
                        factor()
                        project_low()
                        output()
                        map_low(0)
                        if i < STEPS:
                            maximum(1)
                        map_low(1)
                        if i == STEPS + 1:
                            mean_square(0)
                        if i == STEPS + 2:
                            inverse_root(0)
                            normalise(0)
                            normalise(1)

                    def ot_low(t):
                        half = slice(4 * (t % 2), 4 * (t % 2) + 4)
                        low(o_use(t), 2 * NT + HEADS * TH + t, AT[1][:, half, 0:P],
                            TT[:, t % 2, :].rearrange("p (k n) -> p k n", k=KT), AT[0][:, half, 0:P])

                    def add_x(t):
                        dve.wait_ge(s_ttf, b * TTK + wo_use(t) + 1)
                        dve.wait_ge(s_x[t % 2], 16 * (b * (NT // 2) + t // 2 + 1))
                        if t >= 2:
                            dve.wait_ge(s_st[t % 2], 16 * (b * (NT // 2) + t // 2 + 1))
                        dve.tensor_tensor(x1_sb[:, t % 2, :], product_bank(t), x_in[:, t % 2, :], ALU.add)\
                           .then_inc(s_x1, 1)
                        dve.wait_ge(s_x1, b * NT + t + 1)
                        dve.sem_inc(s_xfree, 1)
                        dve.sem_inc(s_ttfree, 1)

                    ot_low(0)
                    mean_square(1)
                    inverse_root(1)
                    for t in range(NT):
                        if t + 2 < NT:
                            normalise(t + 2)
                        if t + 1 < NT:
                            ot_low(t + 1)
                        add_x(t)
                    dve.sem_inc(s_wfree, 1)
                    link.close()

            @block.gpsimd
            def _(pool):
                pool.memset(neg_half[:, :], -0.5).then_inc(s_half_set, 1)
                pool.wait_ge(s_half_set, 1)

                def split_w(n, low, raw, high):
                    pool.wait_ge(s_wqh, n + 1)
                    pool.tensor_tensor(low, raw, high.bitcast(F32), ALU.subtract).then_inc(s_wql, 1)

                def split_wqk(n):
                    split_w(n, wq[1][:, :, :], w_in_qk, wq[0][:, :, :])

                split_wqk(0)
                with pool.Fori(0, batches) as b:
                    link = Links(pool, s_scaled, TH * HEADS, b, passed=s_passed)
                    for t in range(NT):
                        v = rstd[:, t % 2:t % 2 + 1]
                        pool.wait_ge(s_var, b * NT + t + 1)
                        pool.tensor_tensor(v, v, neg_half[:, :], ALU.pow).then_inc(s_root, 1)
                    split_wqk(b * LOADS + 1)
                    for i in range(STEPS):
                        hd, j = divmod(i, NT)
                        pool.wait_ge(s_cc, b * STEPS + i + 1)
                        pool.sem_inc(s_passed, 1)
                        for k, nb in blocks(i):
                            c = slice(k * P, (k + nb) * P)
                            p0, p1 = PR[:, i % 3, 0, c], PR[:, i % 3, 1, c]
                            link(pool.tensor_scalar(p1, p1, comb[:, j % 4:j % 4 + 1], 1.0, ALU.mult, ALU.mult))
                            pool.tensor_tensor(p0, p0, p1, ALU.add).then_inc(s_comb, 1)
                        if j == 4 and hd + 2 <= HEADS:
                            split_wqk(b * LOADS + hd + 2)
                        if hd == HEADS - 1 and j in (1, 3):
                            k = slice(j - 1, j + 1)
                            split_w(b * LOADS + HEADS + 1 + j // 2, W[1][:, k, :], w_in_wo, W[0][:, k, :])
                    link.close()

            @block.scalar
            def _(act):
                def high_w(n, high, raw):
                    act.wait_ge(s_win, n * 16 + 16)
                    act.activation(high, raw, ACT.Copy).then_inc(s_wqh, 1)

                def high_wqk(n):
                    high_w(n, wq[0][:, :, :], w_in_qk)

                act.wait_ge(s_c, 48)
                act.activation(identb[:, :], ident[:, :], ACT.Copy).then_inc(s_cast, 1)
                act.activation(mask[:, :, :], maskf.rearrange("p (t n) -> p t n", t=2), ACT.Copy).then_inc(s_cast, 1)
                act.wait_ge(s_prime, 2)
                act.activation(lam_s[:, 0:2], lam_s[:, 0:2], ACT.Exp).then_inc(s_cast, 1)
                high_wqk(0)
                with act.Fori(0, batches) as b:
                    def high(use, out, in_):
                        act.wait_ge(s_ttf, b * TTK + use + 1)
                        act.activation(out, in_, ACT.Copy).then_inc(s_tth, 1)

                    def proj_high(h, quarter):
                        m, half = QUARTERS[quarter]
                        c, r = slice(half * D, (half + 1) * D), h % 2
                        act.wait_ge(s_pjf, b * 4 * HEADS + 4 * h + quarter + 1)
                        if m == 0:
                            act.activation(Q[r][0][lo64, c], PJ[lo64, :], ACT.Copy, scale=0.125)
                            ins = act.activation(Q[r][1][hi64, c], PJ[hi64, :], ACT.Copy, scale=0.125)
                        else:
                            act.activation(K[lo64, r, 0, c], PJ[lo64, :], ACT.Copy)
                            ins = act.activation(K[hi64, r, 2, c], PJ[hi64, :], ACT.Copy)
                        ins.then_inc(s_pjh, 1)

                    act.wait_ge(s_wv, 16 * b + 16)
                    act.wait_ge(s_wfree, b + 1)
                    act.activation(W[0][:, :, :], wv_in, ACT.Copy).then_inc(s_wvh, 1)
                    for t in range(NT):
                        high(x_use(t), xT[0][:, :, t * P:(t + 1) * P],
                             TT[:, t % 2, :].rearrange("p (k n) -> p k n", k=KT))
                        for v in ([t - 1] if t else []) + ([t] if t == NT - 1 else []):
                            high(v_use(v), V[:, v, :, 0:DH],
                                 product_bank(v).rearrange("p (h n) -> p h n", h=HEADS))
                            for quarter in FIRST_QUARTERS.get(v, ()):
                                proj_high(0, quarter)
                    high_wqk(b * LOADS + 1)

                    def squares(half):
                        for t in range(4 * half, 4 * half + 4):
                            if t % 2 == 0:
                                act.wait_ge(s_oxf, b * HEADS * NG + (HEADS - 1) * NG + t // 2 + 2)
                            act.activation(sq[half][:, t % 4, :], O[:, t, :], ACT.Square).then_inc(s_sq, 1)

                    def roots(half):
                        act.wait_ge(s_ms, 2 * b + half + 1)
                        act.activation(inv[:, 4 * half:4 * half + 4, :], grp[:, 4 * half:4 * half + 4, :], ACT.Sqrt)\
                           .then_inc(s_sqrt, 1)

                    for i in range(STEPS + LAG + 2):
                        hd, j = divmod(i, NT)

                        def exponential(s):
                            u = hd * U + 2 * j + s
                            act.wait_ge(s_max, b * HEADS * U + u + 1)
                            sc = score_tile(u % U)
                            act.activation(PR[:, i % 3, s, 0:width(i)], sc, ACT.Exp, bias=nmax[:, u % U:u % U + 1],
                                           accum_out=sums[:, j, hd, s:s + 1]).then_inc(s_scfree, 1)

                        def map_high(part):
                            if LAG <= i < STEPS + LAG and part < len(blocks(i - LAG)):
                                use, t = turn_use(i - LAG) + part, i % 2
                                k, nb = blocks(i - LAG)[part]
                                high(use, AT[0][:, k:k + nb, t * P:(t + 1) * P],
                                     TT[:, use % 2, 0:nb * P].rearrange("p (k n) -> p k n", k=nb))

                        def turn_out():
                            g = group_at(i, LAG + 2)
                            if g is not None:
                                act.wait_ge(s_pv, b * HEADS * NG + g + 1)
                                act.activation(OT[:, :], PV[:, 0:GQ], ACT.Copy).then_inc(s_ot, 1)

                        def project_high():
                            if j - 1 in AT_STEPS and hd + 1 < HEADS:
                                proj_high(hd + 1, AT_STEPS.index(j - 1))
                            if j == AT_STEPS[3] + 1 and hd + 2 <= HEADS:
                                high_wqk(b * LOADS + hd + 2)
                        project_high()
                        map_high(0)
                        if i < STEPS:
                            exponential(0)
                        turn_out()
                        map_high(1)
                        if i < STEPS:
                            exponential(1)
                        if i == STEPS:
                            squares(0)
                        if i == STEPS + 1:
                            roots(0)
                        if hd == HEADS - 1 and j in (1, 3):
                            high_w(b * LOADS + HEADS + 1 + j // 2, W[0][:, j - 1:j + 1, :], w_in_wo)
                    for t in range(NT):
                        if t == 1:
                            squares(1)
                            roots(1)
                        high(o_use(t), AT[0][:, 4 * (t % 2):4 * (t % 2) + 4, 0:P],
                             TT[:, t % 2, :].rearrange("p (k n) -> p k n", k=KT))
                    act.wait_ge(s_xts, b * 64 + 64)

            @block.tensor
            def _(pe):
                pe.wait_ge(s_c, 48)
                pe.wait_ge(s_cast, 2)
                pe.wait_ge(s_fold, 1)
                with pe.Fori(0, batches) as b:
                    def turn(bank, free, blocks_in):
                        pe.wait_ge(s_ttfree, b * TTK + free)
                        for i, v in enumerate(blocks_in):
                            ins = pe.transpose(TT[:, bank, i * P:(i + 1) * P], v, ident[:, :])
                        ins.then_inc(s_ttf, 1)

                    def project(h, quarter):
                        m, half = QUARTERS[quarter]
                        if quarter == 0:
                            pe.wait_ge(s_wql, b * LOADS + h + 1)
                        pe.wait_ge(s_pjfree, b * 4 * HEADS + 4 * h + quarter + 1)
                        for k in range(KT):
                            ins = three_products(pe, PJ[:, :], [w[:, k, m * P:(m + 1) * P] for w in wq],
                                                 [w[:, k, half * D:(half + 1) * D] for w in xT], k == 0, k == KT - 1)
                        ins.then_inc(s_pjf, 1)

                    for t in range(NT):
                        for n in ([0, 1] if t == 0 else [t + 1] if t + 1 < NT else []):
                            pe.wait_ge(s_xn, b * NT + n + 1)
                            turn(n % 2, n + 1 if n < 2 else x_use(n - 2) + 3, [xn[:, n % 2, k * P:(k + 1) * P] for k in range(KT)])
                        if t == 0:
                            pe.wait_ge(s_wvl, b + 1)
                        pe.wait_ge(s_ttfree, b * TTK + x_use(t) + 3)
                        for k in range(KT):
                            ins = three_products(pe, product_bank(t), [w[:, k, t * P:(t + 1) * P] for w in xT],
                                                 [w[:, k, :] for w in W], k == 0, k == KT - 1)
                        ins.then_inc(s_ttf, 1)
                        for quarter in FIRST_QUARTERS.get(t, ()):
                            project(0, quarter)

                    for i in range(STEPS + LAG + 2):
                        hd, j = divmod(i, NT)

                        def scores(s):
                            n = width(i)
                            u = hd * U + 2 * j + s
                            if j == 0 and s == 0:
                                pe.wait_ge(s_pjfree, b * 4 * HEADS + 4 * hd + 4 + 1)
                                pe.wait_ge(s_kdup, (b * HEADS + hd + 1) * 8 * 16)
                            if u == 2:
                                pe.wait_ge(s_ttfree, b * TTK + 2 * NT + 2)
                            v = bank_before(u)
                            if v is not None:
                                pe.wait_ge(s_scfree, b * HEADS * U + v + 1)
                            first = bank(u % U)
                            qs = Q[hd % 2][s][:, j * P:(j + 1) * P]
                            for c0 in range(0, n, D):
                                w = min(D, n - c0)
                                end = c0 + w == n
                                out = SC[:, first + c0 // D, :]
                                pe.matmul(out[:, 0:w], qs, K[:, hd % 2, 2 * s, c0:c0 + w], start=True, stop=False)
                                pe.matmul(out[:, 0:w], qs, K[:, hd % 2, 2 * s + 1, c0:c0 + w], start=False,
                                          stop=not end)
                                if end:
                                    ins = pe.matmul(out[:, w - GQ:w], identb[:, :], mask[:, j % 2, :],
                                                    start=False, stop=True)
                            ins.then_inc(s_scf, 1)

                        def turn_maps(part):
                            if LAG <= i < STEPS + LAG and part < len(blocks(i - LAG)):
                                use = turn_use(i - LAG) + part
                                k, nb = blocks(i - LAG)[part]
                                pe.wait_ge(s_comb, b * HEADS * TH + use - 2 * NT + 1)
                                turn(use % 2, use + 1, [PR[:, (i - LAG) % 3, 0, (k + q) * P:(k + q + 1) * P] for q in range(nb)])

                        def values():
                            g = group_at(i, LAG + 2)
                            if g is not None:
                                pe.wait_ge(s_ttfree, b * TTK + turn_use(i - LAG - 1) + len(blocks(i - LAG - 1)) + 2)
                                pe.wait_ge(s_oxf, b * HEADS * NG + g + 1)
                                n = 2 * (g % NG + 1)
                                for k in range(n):
                                    for part in range(2):
                                        ins = pe.matmul(PV[:, 0:GQ], V[:, k, g // NG, :], AT[part][:, k, :],
                                                        start=(k + part == 0), stop=(k == n - 1 and part == 1))
                                ins.then_inc(s_pv, 1)

                        def output():
                            g = group_at(i, LAG + 3)
                            if g is not None:
                                pe.wait_ge(s_ot, b * HEADS * NG + g + 1)
                                for t in range(2):
                                    ins = pe.matmul(PV[:, GQ + t * DH:GQ + (t + 1) * DH], OT[:, t * P:(t + 1) * P],
                                                    fold[:, :], start=True, stop=True)
                                ins.then_inc(s_ox, 1)

                        def project_next():
                            if j in AT_STEPS and hd + 1 < HEADS:
                                project(hd + 1, AT_STEPS.index(j))
                        if i < STEPS:
                            scores(0)
                        values()
                        output()
                        turn_maps(0)
                        if i < STEPS:
                            scores(1)
                        turn_maps(1)
                        project_next()

                    def o_t(t):
                        pe.wait_ge(s_xn2, b * NT + t + 1)
                        turn(t % 2, o_use(t) + 1 if t < 2 else o_use(t - 2) + 3, [O[:, t, k * P:(k + 1) * P] for k in range(KT)])

                    o_t(0)
                    pe.wait_ge(s_wql, (b + 1) * LOADS + 1)
                    for t in range(NT):
                        if t + 1 < NT:
                            o_t(t + 1)
                        pe.wait_ge(s_ttfree, b * TTK + o_use(t) + 3)
                        for k in range(KT):
                            ins = three_products(pe, product_bank(t), [w[:, 4 * (t % 2) + k, 0:P] for w in AT],
                                                 [w[:, k, :] for w in W], k == 0, k == KT - 1)
                        ins.then_inc(s_ttf, 1)


def dense_ffn(nc, w1T, w3T, w2p, xth_d, xtl_d, x1, x1b, x2, chunks):
    HH = HID // 2
    M = HH // P
    RING = 4
    TK = D // P
    NP = 3 * M // 2
    PLACED = {1: (0, 1), 3: (2, 3, 4), 5: (5, 6, 7), 7: (8, 9, 10), M: (11,)}
    with ExitStack() as ctx:
        def sb(name, shape, dt=F32):
            return ctx.enter_context(nc.sbuf_tensor(name, shape, dt))

        def pb(name, shape):
            return ctx.enter_context(nc.psum_tensor(name, shape, F32))

        def sem(name):
            return ctx.enter_context(nc.semaphore(name))

        G = pb("gate_ps", [P, 2, D])
        Up = pb("up_ps", [P, 2, D])
        Y = pb("ffn_ps", [P, TK, D])
        w1 = [sb("w1_hi", [P, KT, HH], F32R), sb("w1_lo", [P, KT, HH], F32R)]
        w3 = [sb("w3_hi", [P, KT, HH], F32R), sb("w3_lo", [P, KT, HH], F32R)]
        w2 = [sb("w2_hi", [P, M, D], F32R), sb("w2_lo", [P, M, D], F32R)]
        stage = sb("w_stage", [P, 3, 2 * D])
        X = [sb("ffn_x_hi", [P, 2, KT, D], F32R), sb("ffn_x_lo", [P, 2, KT, D], F32R)]
        sg = sb("silu_gate", [P, 2, D])
        hf = sb("hidden", [P, 2, D])
        H = [sb("hidden_hi", [P, RING, D], F32R), sb("hidden_lo", [P, RING, D], F32R)]
        res = sb("residual", [P, 2, TK, D])

        s_st = [sem(f"f_stage{i}") for i in range(3)]
        s_wh, s_wl, s_wl2 = sem("f_w_high"), sem("f_w_low"), sem("f_w_low2")
        s_x = [sem("f_x0"), sem("f_x1")]
        s_r = [sem("f_res0"), sem("f_res1")]
        s_out = [sem("f_out0"), sem("f_out1")]
        s_g, s_sg, s_u, s_hh, s_hl = sem("f_gate_up"), sem("f_silu"), sem("f_hidden"), sem("f_h_high"), sem("f_h_low")
        s_passed = sem("f_passed")
        s_y, s_sum = sem("f_product"), sem("f_sum")

        def source(i):
            half, g, kind = i // NP, i % NP // 3, i % 3
            h0 = half * HH + g * 2 * P
            if kind < 2:
                return (w1T, w3T)[kind][:, h0:h0 + 2 * P].rearrange("(k p) n -> p k n", p=P)
            return w2p[h0:h0 + 2 * P, :].rearrange("(a p) n -> p a n", p=P)

        def place(part, i):
            g, kind = i % NP // 3, i % 3
            if kind < 2:
                return (w1, w3)[kind][part][:, :, g * 2 * P:(g + 1) * 2 * P]
            return w2[part][:, 2 * g:2 * g + 2, :]

        def staged(i):
            return stage[:, i % 3, :].rearrange("p (k n) -> p k n", k=KT if i % 3 < 2 else 2)

        def split_done(i):
            return (s_wl, s_wl2)[i % 2], i // 2 + 1

        def over_chunks(eng, body, half):
            with eng.Fori(0, chunks // 2 - 1) as i:
                for par in range(2):
                    body(2 * i + (half * chunks + par), 2 * i + par, par, False)
            for par in range(2):
                c = chunks - 2 + par
                body(half * chunks + c, c, par, par == 1)

        with nc.Block() as block:
            @block.sync
            def _(sp):
                def load_x(c, par):
                    for part, dram in ((0, xth_d), (1, xtl_d)):
                        sp.dma_start(X[part][:, par, :, :].bitcast(F32),
                                     dram[bass.ds(c, 1)].rearrange("o p k n -> (o p) k n")).then_inc(s_x[par], 16)

                def load_piece(i):
                    if i >= 3:
                        sp.wait_ge(*split_done(i - 3))
                    sp.dma_start(staged(i), source(i)).then_inc(s_st[i % 3], 16)

                def tokens(d, c):
                    return d[bass.ds(c * D, D), :].rearrange("(t p) n -> p t n", p=P)

                for i in range(NP):
                    load_piece(i)
                    if i == 1:
                        load_x(0, 0)
                for half in range(2):
                    before, after = (x1, x1b) if half == 0 else (x1b, x2)

                    def body(cg, c, par, last):
                        sp.dma_start(res[:, par, :, :], tokens(before, c)).then_inc(s_r[par], 16)
                        if not last or half == 0:
                            sp.wait_ge(s_g, cg * M + 1)
                            load_x(0 if last else c + 1, 1 - par)
                        if last and half == 0:
                            for i in range(NP, 2 * NP):
                                load_piece(i)
                        sp.wait_ge(s_sum, cg * TK + 2 * TK)
                        sp.dma_start(tokens(after, c), res[:, par, :, :]).then_inc(s_out[par], 16)
                        sp.wait_ge(s_out[par], 16 * half * (chunks // 2) + (c - par) * 8 + 16)
                        sp.sem_inc(s_passed, 1)

                    over_chunks(sp, body, half)

            @block.scalar
            def _(act):
                def high(i):
                    act.wait_ge(s_st[i % 3], 16 * (i // 3 + 1))
                    act.activation(place(0, i), staged(i), ACT.Copy).then_inc(s_wh, 1)

                for i in range(NP):
                    high(i)
                for half in range(2):
                    def body(cg, c, par, last):
                        for m in range(M):
                            n = cg * M + m
                            act.wait_ge(s_g, n + 1)
                            act.activation(sg[:, m % 2, :], G[:, m % 2, :], ACT.Silu).then_inc(s_sg, 1)
                            act.wait_ge(s_u, n + 1)
                            act.activation(H[0][:, m % RING, :], hf[:, m % 2, :], ACT.Copy).then_inc(s_hh, 1)
                            if last and half == 0:
                                for i in PLACED.get(m, ()):
                                    if i % 3 == 2:
                                        act.wait_ge(s_y, cg * M + i // 3 * 2 + 2)
                                    high(NP + i)
                        if last and half == 0:
                            act.wait_ge(s_y, cg * M + M)
                            for i in PLACED[M]:
                                high(NP + i)

                    over_chunks(act, body, half)

            @block.gpsimd
            def _(pool):
                def low(i):
                    if i % 2 == 0:
                        pool.wait_ge(s_wh, i + 1)
                        pool.tensor_tensor(place(1, i), staged(i), place(0, i).bitcast(F32), ALU.subtract)\
                            .then_inc(s_wl, 1)

                for i in range(NP):
                    low(i)
                for half in range(2):
                    def body(cg, c, par, last):
                        for m in range(M):
                            n = cg * M + m
                            pool.wait_ge(s_hh, n + 1)
                            pool.tensor_tensor(H[1][:, m % RING, :], hf[:, m % 2, :],
                                               H[0][:, m % RING, :].bitcast(F32), ALU.subtract).then_inc(s_hl, 1)
                            if last and half == 0:
                                for i in PLACED.get(m, ()):
                                    low(NP + i)

                    over_chunks(pool, body, half)

            @block.vector
            def _(dve):
                dve.sem_inc(s_sum, TK)
                def low(i):
                    if i % 2:
                        dve.wait_ge(s_wh, i + 1)
                        dve.tensor_tensor(place(1, i), staged(i), place(0, i).bitcast(F32), ALU.subtract)\
                           .then_inc(s_wl2, 1)

                for i in range(NP):
                    low(i)
                for half in range(2):
                    def sums(cg, c, par):
                        dve.wait_ge(s_r[par], 16 * half * (chunks // 2) + (c - par) * 8 + 16)
                        for t in range(TK):
                            if t == 0:
                                dve.wait_ge(s_y, cg * M + M)
                            dve.tensor_tensor(res[:, par, t, :], Y[:, t, :], res[:, par, t, :], ALU.add)\
                               .then_inc(s_sum, 1)

                    def gated(cg, m, first=False):
                        n = cg * M + m
                        dve.wait_ge(s_sg, n + 1)
                        if not first:
                            dve.wait_ge(s_hl, n - 1)
                        dve.tensor_tensor(hf[:, m % 2, :], sg[:, m % 2, :], Up[:, m % 2, :], ALU.mult)\
                           .then_inc(s_u, 1)

                    for m in range(2):
                        gated(half * chunks, m, first=True)

                    def body(cg, c, par, last):
                        for m in range(2, M + (0 if last else 2)):
                            gated(cg + m // M, m % M)
                            if last and half == 0 and m % 2:
                                for i in (PLACED[1] if m == 3 else ()) + PLACED[m]:
                                    low(NP + i)
                        sums(cg, c, par)
                        if last and half == 0:
                            for i in PLACED[M]:
                                low(NP + i)

                    over_chunks(dve, body, half)

            @block.tensor
            def _(pe):
                for half in range(2):
                    def gate_up(cg, c, par, m):
                        n = cg * M + m
                        if m == 0:
                            pe.wait_ge(s_x[par], 32 * half * (chunks // 2) + (c - par) * 16 + 32)
                        for out, w in ((G, w1), (Up, w3)):
                            for k in range(KT):
                                ins = three_products(pe, out[:, m % 2, :], [v[:, k, m * P:(m + 1) * P] for v in w],
                                                     [v[:, par, k, :] for v in X], k == 0, k == KT - 1)
                        ins.then_inc(s_g, 1)

                    def down(cg, m):
                        n = cg * M + m
                        pe.wait_ge(s_hl, n + 1)
                        for t in range(TK):
                            ts = slice(t * P, (t + 1) * P)
                            out = Y[:, t, :]
                            pe.matmul(out, H[0][:, m % RING, ts], w2[0][:, m, :], start=(m == 0), stop=False)
                            pe.matmul(out, H[0][:, m % RING, ts], w2[1][:, m, :], start=False, stop=False)
                            ins = pe.matmul(out, H[1][:, m % RING, ts], w2[0][:, m, :], start=False, stop=(m == M - 1))
                        ins.then_inc(s_y, 1)

                    for i in range(2):
                        pe.wait_ge(*split_done(half * NP + i))
                    for m in range(2):
                        gate_up(half * chunks, 0, 0, m)
                    for i in (NP - 2, NP - 1):
                        pe.wait_ge(*split_done(half * NP + i))

                    def body(cg, c, par, last):
                        for m in range(M):
                            if m + 2 < M:
                                pe.wait_ge(s_hl, cg * M + m + 1)
                                gate_up(cg, c, par, m + 2)
                            elif not last:
                                pe.wait_ge(s_hl, cg * M + m + 1)
                                gate_up(cg + 1, c + 1, 1 - par, m + 2 - M)
                            if m == 0:
                                pe.wait_ge(s_sum, cg * TK + TK)
                            down(cg, m)

                    over_chunks(pe, body, half)


def recurrence(nc, wr, wf, wc, wo_d, ln_scale, rwT, ident_d, x2, table, logits_d, acc, batches):
    LV = int(math.log2(S))
    GC = 2
    NG = KT // GC
    PU = 3 * GC * 2
    RING = 6
    HU = 2 * GC * 2
    BU = NG * PU
    with ExitStack() as ctx:
        def sb(name, shape, dt=F32):
            return ctx.enter_context(nc.sbuf_tensor(name, shape, dt))

        def pb(name, shape):
            return ctx.enter_context(nc.psum_tensor(name, shape, F32))

        def sem(name):
            return ctx.enter_context(nc.semaphore(name))

        TT = pb("r_turn_ps", [P, 2, D])
        RT = pb("router_ps", [P, D])
        CO = pb("cols_ps", [P, D])
        PP = pb("proj_ps", [P, 2, D])
        MS = pb("sumsq_ps", [P, D])
        W = [[sb(f"w_{n}_{p}", [P, KT, D], F32R) for p in ("hi", "lo")] for n in ("f", "c", "r", "o")]
        rw = [sb("router_hi", [P, KT, P], F32R), sb("router_lo", [P, KT, P], F32R)]
        xT = [sb("r_xT_hi", [P, KT, S], F32R), sb("r_xT_lo", [P, KT, S], F32R)]
        F0 = sb("forget", [P, 2, GC, S])
        C0 = sb("cell_in", [P, 2, GC, S])
        R0 = sb("read_gate", [P, 2, GC, S])
        FU = sb("forget_up", [P, GC, S])
        CU = sb("cell_up", [P, GC, S])
        H = sb("state", [P, GC, S])
        diff = sb("scan_diff", [P, GC, S // 2])
        Z = [sb("gated_hi", [P, 2, KT, P], F32R), sb("gated_lo", [P, 2, KT, P], F32R)]
        x_in = sb("r_x_in", [P, 2, D])
        io = sb("r_tiles", [P, RING, D])
        rows = sb("r_rows", [E, S])
        lg = sb("logits", [P, NT * E])
        rw_in = lg[:, :].rearrange("p (k e) -> p k e", k=KT)
        ident = sb("r_ident", [P, P])
        ones = sb("r_ones", [P, 1])
        neg_half = sb("r_neg_half", [P, NT])
        scale = sb("ln_scale_sb", [P, KT])
        stats = sb("r_stats", [P, NT, 6])
        mv = sb("r_mv", [P, NT, 2])
        rstd = sb("r_rstd", [P, NT])
        minus_mean = sb("r_minus_mean", [P, NT])
        shift = sb("r_shift", [P, NT])
        rms = sb("r_rms", [P, NT])

        s_id, s_wh, s_wl, s_sc = sem("r_ident"), sem("r_wh"), sem("r_wl"), sem("r_scaled")
        s_w = [sem("r_w_" + n) for n in ("router", "forget", "cell", "read", "out")]
        s_x = sem("r_x_last")
        s_xa, s_xst, s_res, s_ost = ([sem(f"r_{n}{i}") for i in range(RING)]
                                     for n in ("x_to_norm", "xn_stored", "x_again", "out_stored"))
        s_bs, s_ag, s_xn, s_var, s_root = sem("r_bn"), sem("r_bn_joined"), sem("r_xn"), sem("r_var"), sem("r_root")
        s_ttf, s_tth, s_ttfree = sem("r_tt_filled"), sem("r_tt_high"), sem("r_tt_free")
        s_rt, s_rtc, s_co, s_lg, s_lgs = sem("r_router"), sem("r_router_c"), sem("r_cols"), sem("r_lg"), sem("r_lg_st")
        s_ppf, s_ppa, s_pof, s_ppd = sem("r_pp_filled"), sem("r_pp_act"), sem("r_pp_product"), sem("r_pp_dve")
        s_dv, s_lvl, s_fl, s_cp = sem("r_dve_chain"), sem("r_level"), sem("r_flevel"), sem("r_firsts")
        s_h, s_z, s_sq, s_zh, s_zl = sem("r_h"), sem("r_z"), sem("r_sq"), sem("r_zh"), sem("r_zl")
        s_sqs, s_ms, s_mean, s_msq, s_rroot = sem("r_sq_sum"), sem("r_ms"), sem("r_ms_half"), sem("r_ms_mean"), sem("r_rms_root")
        s_shift, s_passed, s_out, s_one = sem("r_shift"), sem("r_passed"), sem("r_out"), sem("r_ones_set")

        def level(arr0, up, par, k):
            if k == 0:
                return arr0[:, par, :, :]
            at = S - (S >> (k - 1))
            return up[:, :, at:at + (S >> k)]

        def tile(t):
            return io[:, t % RING, :]

        def uses(b, t):
            return b * (NT // RING + 1) + t // RING + 1 if t % RING < NT % RING else b + 1

        def product_bank(t):
            return (PP if t % 4 < 2 else TT)[:, t % 2, :]

        def over_batches(eng, head, turn):
            head(0, True)
            with eng.Fori(0, batches - 1) as b:
                turn(b, True)
            turn(batches - 1, False)

        def tile_of(d, b, t):
            return d[bass.ds(b * S + t * P, P), :]

        def gated(t):
            return R0[:, :, :, t * P:(t + 1) * P].rearrange("p g c n -> p (g c) n")

        stages = [F0[:, 1], C0[:, 1], R0[:, 0], R0[:, 1]]

        def weight(i):
            if i == 0:
                return rw[0][:, :, :], rw[1][:, :, :], rw_in
            return (*(flat(v[:, :, :]) for v in W[i - 1]), flat(stages[i - 1]))

        def flat(v):
            return v.rearrange("p a n -> p (a n)")

        with nc.Block() as block:
            @block.sync
            def _(sp):
                sp.dma_start(ident[:, :], ident_d).then_inc(s_id, 16)

                def load_weight(i):
                    sp.dma_start(flat(stages[i]), (wf, wc, wr, wo_d)[i].rearrange("p k n -> p (k n)"))\
                      .then_inc(s_w[1 + i], 16)
                def again(b, t, arrived):
                    sp.dma_start(tile(t), tile_of(x2, b, t)).then_inc(arrived[t % RING], 16)

                def head(b, first=False):
                    for t in range(NT):
                        if t < RING:
                            again(b, t, s_xa)
                        else:
                            if t == RING and not first:
                                sp.wait_ge(s_bs, b * NT)
                            sp.dma_start(x_in[:, t - RING, :], tile_of(x2, b, t)).then_inc(s_x, 16)
                        if first and t == 1:
                            sp.dma_start(rw_in, rwT).then_inc(s_w[0], 16)
                            load_weight(0)
                    if first:
                        sp.dma_start(scale[:, :], ln_scale).then_inc(s_w[4], 16)
                        for i in range(1, 4):
                            load_weight(i)
                    for t in range(NT):
                        sp.wait_ge(s_xn, b * NT + t + 1)
                        sp.dma_start(table[bass.ds(b * S + t * P, P), 0:D], tile(t)).then_inc(s_xst[t % RING], 16)
                        if 2 <= t < 2 + NT - RING:
                            sp.wait_ge(s_xst[t - 2], 16 * uses(b, t - 2))
                            sp.wait_ge(s_ttf, b * NT + t - 1)
                            again(b, t - 2 + RING, s_xa)
                    sp.wait_ge(s_lg, b + 1)
                    sp.dma_start(logits_d[bass.ds(b, 1)].rearrange("o p n -> (o p) n"), lg[:, :]).then_inc(s_lgs, 16)

                def turn(b, more):
                    if more:
                        head(b + 1)
                        sp.wait_ge(s_ttf, (b + 2) * NT)
                        sp.sem_inc(s_passed, 1)
                        for t in range(NT - RING, NT):
                            sp.wait_ge(s_xst[t % RING], 16 * uses(b + 1, t))
                        sp.sem_inc(s_passed, 1)
                    for t in range(RING):
                        again(b, t, s_res)
                    for t in range(NT):
                        sp.wait_ge(s_out, b * NT + t + 1)
                        sp.dma_start(tile_of(acc, b, t), tile(t)).then_inc(s_ost[t % RING], 16)
                        if 2 <= t < 2 + NT - RING:
                            sp.wait_ge(s_ost[t - 2], 16 * uses(b, t - 2))
                            again(b, t - 2 + RING, s_res)
                    for t in range(NT - RING, NT):
                        sp.wait_ge(s_ost[t % RING], 16 * uses(b, t))
                    sp.sem_inc(s_passed, 1)

                over_batches(sp, head, turn)
                sp.wait_ge(s_lgs, 16 * batches)
                for t in range(NT - RING, NT):
                    sp.wait_ge(s_xst[t % RING], 16 * uses(batches - 1, t))

            @block.vector
            def _(dve):
                dve.sem_inc(s_ttfree, 2)
                dve.sem_inc(s_ppd, 1)
                dve.sem_inc(s_z, 1)
                dve.sem_inc(s_sq, 1)
                dve.memset(ones[:, :], 1.0).then_inc(s_one, 1)

                def split(i):
                    high, low, raw = weight(i)
                    dve.wait_ge(s_wh, i + 1)
                    dve.tensor_tensor(low, raw, high.bitcast(F32), ALU.subtract).then_inc(s_wl, 1)

                def copy_logits(b, first):
                    dve.wait_ge(s_co, b + 1)
                    if not first:
                        dve.wait_ge(s_lgs, 16 * b)
                    dve.tensor_copy(lg[:, :], CO[:, :]).then_inc(s_lg, 1)

                def statistics(b, t):
                    if t < RING:
                        dve.wait_ge(s_xa[t], 16 * uses(b, t))
                    else:
                        dve.wait_ge(s_x, 16 * (b + 1) * (NT - RING))
                    dve.bn_stats(stats[:, t, :], tile(t) if t < RING else x_in[:, t - RING, :]).then_inc(s_bs, 1)

                def join_statistics(b):
                    dve.wait_ge(s_bs, b * NT + NT)
                    dve.sem_inc(s_passed, 1)
                    for t in range(NT):
                        dve.bn_aggr(mv[:, t, :], stats[:, t, :]).then_inc(s_ag, 1)
                    dve.wait_ge(s_ag, b * NT + NT)
                    dve.tensor_scalar(rstd[:, :], mv[:, :, 1], LN_EPS, None, ALU.add).then_inc(s_var, 1)
                    dve.tensor_scalar(minus_mean[:, :], mv[:, :, 0], -1.0, None, ALU.mult).then_inc(s_var, 1)

                def head(b, first=False):
                    if first:
                        for t in range(NT):
                            statistics(b, t)
                        join_statistics(b)
                    if first:
                        split(0)
                        split(1)
                        dve.wait_ge(s_w[4], 32)
                        for c in range(KT):
                            v = flat(stages[3])[:, c * D:(c + 1) * D]
                            dve.tensor_scalar(v, v, scale[:, c:c + 1], None, ALU.mult).then_inc(s_sc, 1)
                    for t in range(NT):
                        dve.wait_ge(s_tth, b * NT + t + 1)
                        dve.tensor_tensor(xT[1][:, :, t * P:(t + 1) * P],
                                          TT[:, t % 2, :].rearrange("p (k n) -> p k n", k=KT),
                                          xT[0][:, :, t * P:(t + 1) * P].bitcast(F32), ALU.subtract).then_inc(s_ttfree, 1)
                    if first:
                        for i in range(2, 5):
                            split(i)
                        copy_logits(b, first)

                def scan(b, g, link, more=False):
                    dve.wait_ge(s_ppa, b * BU + g * PU + HU)
                    for k in range(LV):
                        f, c = level(F0, FU, g, k), level(C0, CU, g, k)
                        d = diff[:, :, 0:S >> (k + 1)]
                        link(dve.tensor_tensor(d, c[:, :, 0::2], c[:, :, 1::2], ALU.subtract))
                        if k:
                            dve.wait_ge(s_fl, b * NG * (LV - 1) + g * (LV - 1) + k)
                        link(dve.tensor_tensor(d, d, f[:, :, 1::2], ALU.mult))
                        dve.tensor_tensor(level(C0, CU, g, k + 1), d, c[:, :, 1::2], ALU.add).then_inc(s_lvl, 1)
                        if more and k < NT:
                            statistics(b + 1, k)
                        dve.wait_ge(s_lvl, b * NG * LV + g * LV + k + 1)
                    if more:
                        join_statistics(b + 1)
                    dve.wait_ge(s_cp, b * NG * (LV + 1) + (g + 1) * (LV + 1))
                    for k in range(LV - 2, -1, -1):
                        f, c = level(F0, FU, g, k), level(C0, CU, g, k)
                        h, m = 1 << k, (S >> (k + 1)) - 1
                        d = diff[:, :, 0:m]
                        before = H[:, :, 2 * h - 1:2 * h - 1 + 2 * h * (m - 1) + 1:2 * h]
                        here = H[:, :, 3 * h - 1:3 * h - 1 + 2 * h * (m - 1) + 1:2 * h]
                        cn, fn = c[:, :, 2:2 * m + 1:2], f[:, :, 2:2 * m + 1:2]
                        link(dve.tensor_tensor(d, before, cn, ALU.subtract))
                        link(dve.tensor_tensor(d, d, fn, ALU.mult))
                        ins = dve.tensor_tensor(here, d, cn, ALU.add)
                        if k:
                            link(ins)
                        else:
                            ins.then_inc(s_h, 1)
                    dve.wait_ge(s_h, b * NG + g + 1)
                    dve.wait_ge(s_ppa, b * BU + (g + 1) * PU)
                    dve.tensor_tensor(R0[:, g], R0[:, g], H[:, :, :], ALU.mult).then_inc(s_z, 1)

                def turn(b, more):
                    link = Links(dve, s_dv, NG * (2 * LV + 3 * (LV - 1) - 1), b, passed=s_passed)
                    scan(b, 0, link, more)
                    if more:
                        head(b + 1)
                    scan(b, 1, link)
                    if more:
                        copy_logits(b + 1, False)
                    dve.wait_ge(s_ms, NG * b + NG)
                    dve.tensor_scalar(rms[:, :], MS[:, 0:NT], 1.0 / D, RMS_EPS, ALU.mult, ALU.add).then_inc(s_mean, 1)
                    dve.wait_ge(s_mean, b + 1)
                    dve.scalar_tensor_tensor(rms[:, :], MS[:, NT:2 * NT], 1.0 / D, rms[:, :], ALU.mult, ALU.add)\
                       .then_inc(s_msq, 1)
                    dve.wait_ge(s_rroot, b + 1)
                    for t in range(NT):
                        dve.wait_ge(s_pof, b * NT + t + 1)
                        dve.wait_ge(s_res[t % RING], 16 * uses(b, t))
                        dve.scalar_tensor_tensor(tile(t), product_bank(t), rms[:, t:t + 1], tile(t), ALU.mult, ALU.add).then_inc(s_out, 1)
                        dve.wait_ge(s_out, b * NT + t + 1)
                        dve.sem_inc(s_ppd, 1)
                    link.close()

                over_batches(dve, head, turn)

            @block.gpsimd
            def _(pool):
                pool.memset(neg_half[:, :], -0.5).then_inc(s_one, 1)
                pool.wait_ge(s_one, 2)

                def head_root(b):
                    pool.wait_ge(s_var, 2 * b + 2)
                    pool.tensor_tensor(rstd[:, :], rstd[:, :], neg_half[:, :], ALU.pow).then_inc(s_root, 1)
                    pool.wait_ge(s_root, b + 1)
                    pool.tensor_tensor(shift[:, :], minus_mean[:, :], rstd[:, :], ALU.mult).then_inc(s_shift, 1)

                def head(b, first=False):
                    head_root(b)

                def gates(b, g):
                    pool.wait_ge(s_z, b * NG + g + 1)
                    pool.wait_ge(s_ppa, b * BU + g * PU + HU // 2)
                    for k in range(LV - 1):
                        f = level(F0, FU, g, k)
                        pool.tensor_tensor(level(F0, FU, g, k + 1), f[:, :, 0::2], f[:, :, 1::2], ALU.mult)\
                            .then_inc(s_fl, 1)
                        pool.wait_ge(s_fl, b * NG * (LV - 1) + g * (LV - 1) + k + 1)

                def add_squares(b, g):
                    pool.wait_ge(s_sq, b * NG + g + 2)
                    pool.tensor_tensor(F0[:, g, 0, :], F0[:, g, 0, :], F0[:, g, 1, :], ALU.add).then_inc(s_sqs, 1)

                def firsts(b, g):
                    pool.wait_ge(s_sq, b * NG + g + 1)
                    pool.wait_ge(s_ppa, b * BU + g * PU + HU)
                    pool.sem_inc(s_passed, 1)
                    pool.tensor_copy(H[:, :, 0:1], C0[:, g, :, 0:1]).then_inc(s_cp, 1)
                    for k in range(LV):
                        pool.wait_ge(s_lvl, b * NG * LV + g * LV + k + 1)
                        pool.sem_inc(s_passed, 1)
                        at = (2 << k) - 1
                        pool.tensor_copy(H[:, :, at:at + 1], level(C0, CU, g, k + 1)[:, :, 0:1]).then_inc(s_cp, 1)

                def turn(b, more):
                    gates(b, 0)
                    firsts(b, 0)
                    if more:
                        head_root(b + 1)
                    gates(b, 1)
                    add_squares(b, 0)
                    firsts(b, 1)
                    add_squares(b, 1)
                    for t in range(NT):
                        if t == 2:
                            pool.wait_ge(s_msq, b + 1)
                            pool.tensor_tensor(rms[:, :], rms[:, :], neg_half[:, :], ALU.pow).then_inc(s_rroot, 1)
                        pool.wait_ge(s_zh, b * NT + t + 1)
                        pool.tensor_tensor(Z[1][:, t % 2, :, :], gated(t), Z[0][:, t % 2, :, :].bitcast(F32),
                                           ALU.subtract).then_inc(s_zl, 1)

                over_batches(pool, head, turn)

            @block.scalar
            def _(act):
                def high(i):
                    act.wait_ge(s_w[i], 32 if i == 4 else 16)
                    if i == 4:
                        act.wait_ge(s_sc, KT)
                    act.activation(weight(i)[0], weight(i)[2], ACT.Copy).then_inc(s_wh, 1)

                def projection(b, n):
                    g, i = n // PU, n % PU
                    w, ch, half = i // 4, (i // 2) % 2, i % 2
                    dst = (F0, C0, R0)[w][:, g, ch, half * D:(half + 1) * D]
                    act.wait_ge(s_ppf, b * BU + n + 1)
                    act.activation(dst, PP[:, n % 2, :], ACT.Sigmoid if w == 0 else ACT.Silu).then_inc(s_ppa, 1)

                def head(b, first=False):
                    def normalise(t):
                        act.wait_ge(s_xa[t % RING], 16 * uses(b, t))
                        act.activation(tile(t), tile(t), ACT.Identity, bias=shift[:, t:t + 1],
                                       scale=rstd[:, t:t + 1]).then_inc(s_xn, 1)

                    if first:
                        high(0)
                        high(1)
                    act.wait_ge(s_shift, b + 1)
                    normalise(0)
                    normalise(1)
                    for t in range(NT):
                        act.wait_ge(s_ttf, b * NT + t + 1)
                        act.activation(xT[0][:, :, t * P:(t + 1) * P],
                                       TT[:, t % 2, :].rearrange("p (k n) -> p k n", k=KT), ACT.Copy).then_inc(s_tth, 1)
                        if t + 2 < NT:
                            normalise(t + 2)
                    if first:
                        for i in range(2, 5):
                            high(i)
                    for half in range(2):
                        act.wait_ge(s_rt, b * 2 + half + 1)
                        act.activation(rows[:, half * D:(half + 1) * D], RT[0:E, :], ACT.Copy).then_inc(s_rtc, 1)
                    for n in range(HU):
                        projection(b, n)

                def squares(b, g):
                    act.wait_ge(s_h, b * NG + g + 1)
                    act.activation(F0[:, g], H[:, :, :], ACT.Square).then_inc(s_sq, 1)

                def turn(b, more):
                    for n in range(HU, BU):
                        projection(b, n)
                        if n == BU - 3:
                            squares(b, 0)
                    if more:
                        head(b + 1, False)
                    squares(b, 1)
                    act.wait_ge(s_z, b * NG + NG + 1)
                    for t in range(NT):
                        if t >= 2:
                            act.wait_ge(s_pof, b * NT + t - 1)
                        act.activation(Z[0][:, t % 2, :, :], gated(t), ACT.Copy).then_inc(s_zh, 1)

                over_batches(act, head, turn)

            @block.tensor
            def _(pe):
                pe.wait_ge(s_id, 16)
                pe.wait_ge(s_one, 2)

                def projection(b, n, first):
                    g, i = n // PU, n % PU
                    w, ch, half = i // 4, g * GC + (i // 2) % 2, i % 2
                    if n >= 2 or not first:
                        pe.wait_ge(s_ppa, b * BU + n - 1)
                    if n == HU:
                        pe.wait_ge(s_ppd, b * NT + 1)
                    if first and i % 4 == 0:
                        pe.wait_ge(s_wl, 2 + w)
                    for k in range(KT):
                        ins = three_products(pe, PP[:, n % 2, :], [v[:, k, ch * P:(ch + 1) * P] for v in W[w]],
                                             [v[:, k, half * D:(half + 1) * D] for v in xT], k == 0, k == KT - 1)
                    ins.then_inc(s_ppf, 1)

                def head(b, first=False):
                    for t in range(NT):
                        pe.wait_ge(s_xn, b * NT + t + 1)
                        pe.wait_ge(s_ttfree, b * NT + t + 1)
                        for k in range(KT):
                            ins = pe.transpose(TT[:, t % 2, k * P:(k + 1) * P], tile(t)[:, k * P:(k + 1) * P],
                                               ident[:, :])
                        ins.then_inc(s_ttf, 1)
                    for half in range(2):
                        c = slice(half * D, (half + 1) * D)
                        if half == 0:
                            pe.wait_ge(s_ttfree, b * NT + NT + 2)
                            if first:
                                pe.wait_ge(s_wl, 1)
                        else:
                            pe.wait_ge(s_rtc, b * 2 + 1)
                        for k in range(KT):
                            ins = three_products(pe, RT[:, :], [v[:, k, :] for v in rw], [v[:, k, c] for v in xT],
                                                 k == 0, k == KT - 1)
                        ins.then_inc(s_rt, 1)
                    if not first:
                        sum_squares(b - 1, 0)
                    for n in range(HU):
                        projection(b, n, first)
                        if n == 1:
                            pe.wait_ge(s_rtc, b * 2 + 2)
                            if not first:
                                pe.wait_ge(s_lg, b)
                            pe.sem_inc(s_passed, 1)
                            for t in range(NT):
                                ins = pe.transpose(CO[:, t * E:(t + 1) * E], rows[:, t * P:(t + 1) * P],
                                                   ident[0:E, 0:E])
                            ins.then_inc(s_co, 1)

                def sum_squares(b, g):
                    pe.wait_ge(s_sqs, b * NG + g + 1)
                    for t in range(NT):
                        ins = pe.matmul(MS[:, g * NT + t:g * NT + t + 1], F0[:, g, 0, t * P:(t + 1) * P], ones[:, :],
                                        start=True, stop=True)
                    ins.then_inc(s_ms, 1)

                def turn(b, more):
                    for n in range(HU, BU):
                        if n == HU:
                            pe.wait_ge(s_wl, 5)
                        projection(b, n, False)
                    if more:
                        head(b + 1)
                    else:
                        sum_squares(b, 0)
                    pe.wait_ge(s_ppa, (b + 1) * BU + (HU if more else 0))
                    for t in range(NT):
                        pe.wait_ge(s_zl, b * NT + t + 1)
                        if t >= 4:
                            pe.wait_ge(s_ppd, b * NT + t - 2)
                        for k in range(KT):
                            ins = three_products(pe, product_bank(t), [v[:, t % 2, k, :] for v in Z],
                                                 [v[:, k, :] for v in W[3]], k == 0, k == KT - 1)
                        ins.then_inc(s_pof, 1)
                        if t == 1:
                            sum_squares(b, 1)

                over_batches(pe, head, turn)


def routing(nc, logits_d, rev_d, pcol_d, ident_d, table, out, slots, batches):
    T = batches * S
    NTT = T // P
    HT = NTT // 2
    ROUNDS = CAP // 8
    with ExitStack() as ctx:
        def sb(name, shape, dt=F32):
            return ctx.enter_context(nc.sbuf_tensor(name, shape, dt))

        def sem(name):
            return ctx.enter_context(nc.semaphore(name))

        L = sb("all_logits", [P, NTT, E])
        rest = sb("without_top", [P, NTT, E])
        ex = sb("route_exp", [P, NTT, E])
        sel = sb("selected", [P, HT, 2, E])
        top = sb("top_values", [P, NTT, TOPK])
        zsum = sb("z_sum", [P, NTT])
        den = sb("top_sum", [P, NTT])
        key = sb("keys", [P, 2, T // 2])
        rev = sb("rev_sb", [P, T // 2])
        pcol = sb("pcol_sb", [P, 1])
        ident = sb("m_ident", [P, P])
        drawn = sb("drawn", [P, CAP])
        both = sb("both_halves", [E, 2, 2 * CAP])
        first = sb("first_tokens", [E, CAP])
        vt = sb("slot_keys", [P, E])
        tmp = sb("slot_tmp", [P, E])
        zero = sb("zero_rows", [P, ROW])
        MT = ctx.enter_context(nc.psum_tensor("mask_ps", [P, 2, D], F32))
        VT = ctx.enter_context(nc.psum_tensor("slot_ps", [P, E], F32))

        s_in, s_dv, s_exp, s_sel, s_zero = sem("m_in"), sem("m_chain"), sem("m_exp"), sem("m_sel"), sem("m_zero")
        s_mt, s_key, s_gate, s_st, s_mv = sem("m_turned"), sem("m_key"), sem("m_gate"), sem("m_stored"), sem("m_moved")
        s_top, s_drawn, s_first, s_vt, s_shift = sem("m_top"), sem("m_drawn"), sem("m_first"), sem("m_vt"), sem("m_shift")

        def bcast(v):
            return v.unsqueeze(2).to_broadcast([P, NTT, E])

        with nc.Block() as block:
            @block.sync
            def _(sp):
                sp.dma_start(L[:, :, :].rearrange("p (b n) e -> p b (n e)", b=batches),
                             logits_d.rearrange("b p n -> p b n")).then_inc(s_in, 16)
                sp.dma_start(rev[:, :], rev_d).then_inc(s_in, 16)
                sp.dma_start(pcol[:, :], pcol_d).then_inc(s_in, 16)
                sp.dma_start(ident[:, :], ident_d).then_inc(s_in, 16)
                sp.wait_ge(s_zero, 1)
                sp.dma_start(table[T:T + P, :], zero[:, :]).then_inc(s_st, 16)
                sp.dma_start(out[T:T + P, :], zero[:, 0:D]).then_inc(s_st, 16)
                sp.wait_ge(s_gate, 1)
                sp.dma_start(table[0:T, D:ROW].rearrange("(n p) e -> p n e", p=P), ex[:, :, :]).then_inc(s_st, 16)
                sp.wait_ge(s_drawn, ROUNDS)
                sp.dma_start(both[:, 0, 0:CAP], drawn[0:E, :]).then_inc(s_mv, 16)
                sp.dma_start(both[:, 0, CAP:2 * CAP], drawn[E:2 * E, :]).then_inc(s_mv, 16)
                sp.wait_ge(s_st, 48)

            @block.gpsimd
            def _(pool):
                pool.memset(zero[:, :], 0.0).then_inc(s_zero, 1)

            @block.scalar
            def _(act):
                act.wait_ge(s_shift, 1)
                act.activation(ex[:, :, :], ex[:, :, :], ACT.Exp).then_inc(s_exp, 1)

            @block.vector
            def _(dve):
                link = Links(dve, s_dv, 6 + 1, 0)
                dve.wait_ge(s_in, 64)
                for i in range(NTT + 1):
                    if i < NTT:
                        dve.max(top[:, i, :], L[:, i, :]).then_inc(s_top, 1)
                    if i:
                        dve.wait_ge(s_top, i)
                        ins = dve.match_replace(rest[:, i - 1, :], top[:, i - 1, :], L[:, i - 1, :], -3.0e38)
                link(ins)
                dve.tensor_tensor(sel[:, :, :, :].rearrange("p i h e -> p h i e"),
                                  rest[:, :, :].rearrange("p (h i) e -> p h i e", h=2),
                                  L[:, :, :].rearrange("p (h i) e -> p h i e", h=2), ALU.not_equal).then_inc(s_sel, 1)
                dve.tensor_tensor(ex[:, :, :], L[:, :, :], bcast(top[:, :, 0]), ALU.subtract).then_inc(s_shift, 1)
                for n in range(HT // 4):
                    dve.wait_ge(s_mt, n + 1)
                    dve.tensor_tensor(key[:, 0, n * D:(n + 1) * D], MT[:, n % 2, :], rev[:, n * D:(n + 1) * D],
                                      ALU.mult).then_inc(s_key, 1)
                dve.wait_ge(s_exp, 1)
                link(dve.tensor_reduce(zsum[:, :], ex[:, :, :], AX.X, ALU.add))
                sel_t = sel[:, :, :, :].rearrange("p i h e -> p h i e")
                ex_t = ex[:, :, :].rearrange("p (h i) e -> p h i e", h=2)
                link(dve.tensor_tensor(ex_t, ex_t, sel_t, ALU.mult))
                link(dve.tensor_reduce(den[:, :], ex[:, :, :], AX.X, ALU.add))
                link(dve.scalar_tensor_tensor(den[:, :], zsum[:, :], 1e-20, den[:, :], ALU.mult, ALU.add))
                link(dve.reciprocal(den[:, :], den[:, :]))
                dve.tensor_tensor(ex[:, :, :], ex[:, :, :], bcast(den[:, :]), ALU.mult).then_inc(s_gate, 1)
                dve.wait_ge(s_key, HT // 4)
                for r in range(ROUNDS):
                    v = drawn[:, 8 * r:8 * r + 8]
                    dve.max(v, key[:, r % 2, :]).then_inc(s_drawn, 1)
                    dve.wait_ge(s_drawn, r + 1)
                    if r + 1 < ROUNDS:
                        dve.match_replace(key[:, (r + 1) % 2, :], v, key[:, r % 2, :], 0.0).then_inc(s_key, 1)
                        dve.wait_ge(s_key, HT // 4 + r + 1)
                dve.wait_ge(s_mv, 32)
                for r in range(ROUNDS):
                    v = first[:, 8 * r:8 * r + 8]
                    dve.max(v, both[:, r % 2, :]).then_inc(s_first, 1)
                    dve.wait_ge(s_first, r + 1)
                    if r + 1 < ROUNDS:
                        dve.match_replace(both[:, (r + 1) % 2, :], v, both[:, r % 2, :], 0.0).then_inc(s_key, 1)
                        dve.wait_ge(s_key, HT // 4 + ROUNDS + r)
                dve.wait_ge(s_vt, 1)
                link(dve.tensor_copy(vt[:, :], VT[:, :]))
                dve.tensor_scalar(tmp[:, :], vt[:, :], 0.0, pcol[:, 0:1], ALU.is_equal, ALU.mult).then_inc(s_shift, 1)
                dve.wait_ge(s_shift, 2)
                dve.tensor_tensor(tmp[:, :], tmp[:, :], vt[:, :], ALU.subtract).then_inc(s_shift, 1)
                dve.wait_ge(s_shift, 3)
                dve.tensor_scalar(slots[:, :], tmp[:, :], float(T), None, ALU.add).then_inc(s_shift, 1)
                link.close()

            @block.tensor
            def _(pe):
                pe.wait_ge(s_in, 64)
                pe.wait_ge(s_sel, 1)
                for n in range(HT // 4):
                    if n >= 2:
                        pe.wait_ge(s_key, n - 1)
                    for i in range(4):
                        ins = pe.transpose(MT[:, n % 2, i * P:(i + 1) * P],
                                           sel[:, 4 * n + i, :, :].rearrange("p h e -> p (h e)"), ident[:, :])
                    ins.then_inc(s_mt, 1)
                pe.wait_ge(s_first, ROUNDS)
                pe.transpose(VT[:, :], first[:, :], ident[0:E, 0:E]).then_inc(s_vt, 1)


def experts(nc, w_gate, w_up, w_down, ident_d, table, out, slots):
    RING = 4
    GROUPS = E // RING
    FJ = 2
    FP = FE // FJ
    with ExitStack() as ctx:
        def sb(name, shape, dt=F32):
            return ctx.enter_context(nc.sbuf_tensor(name, shape, dt))

        def pb(name, shape):
            return ctx.enter_context(nc.psum_tensor(name, shape, F32))

        def sem(name):
            return ctx.enter_context(nc.semaphore(name))

        XP = pb("xt_ps", [P, 2, D])
        GU = pb("gu_ps", [P, 2, D])
        HP = pb("ht_ps", [P, D])
        YP = pb("y_ps", [P, 2, D])
        ident = sb("e_ident", [P, P])
        wgu = sb("e_gate_up", [P, RING, 2, KT * FE])
        wd = sb("e_down", [FP, RING, FJ * D])
        xg = sb("e_rows", [P, RING, ROW])
        idx = sb("e_index", [P, RING], I32)
        idx_out = sb("e_index_out", [P, RING], I32)
        xT = sb("e_xT", [P, 2, D])
        sg = sb("e_silu", [P, 2, FE])
        hm = sb("e_hidden", [P, 2, FE])
        hT = sb("e_hiddenT", [FP, 2, FJ * P])
        wt = sb("e_weight", [P, RING])
        ys = sb("e_y", [P, 2, D])

        s_w = [sem(f"e_w{q}") for q in range(RING)]
        s_xg = [sem(f"e_xg{q}") for q in range(RING)]
        s_passed = sem("e_passed")
        s_c, s_idx, s_idxo, s_sc = sem("e_const"), sem("e_idx"), sem("e_idx_out"), sem("e_scattered")
        s_xp, s_xT, s_wt, s_gu, s_sg, s_hm = (sem("e_" + n) for n in ("xp", "xT", "wt", "gu", "sg", "hm"))
        s_hp, s_hT, s_y, s_ys = (sem("e_" + n) for n in ("hp", "hT", "y", "ys"))

        def over_groups(eng, group):
            group(0, True, False)
            with eng.Fori(1, GROUPS - 1) as i:
                group(i, False, False)
            group(GROUPS - 1, False, True)

        with nc.Block() as block:
            @block.sync
            def _(sp):
                sp.dma_start(ident[:, :], ident_d).then_inc(s_c, 16)

                def group(i, first, last):
                    for q in range(RING):
                        n = i * RING + q
                        if not first:
                            sp.wait_ge(s_y, n - RING + 1)
                        for m, d in enumerate((w_gate, w_up)):
                            sp.dma_start(wgu[:, q, m, :], d[bass.ds(n, 1)].rearrange(
                                "o (p k) f -> (o p) (k f)", k=KT)).then_inc(s_w[q], 16)
                        sp.dma_start(wd[:, q, :], w_down[bass.ds(n, 1)].rearrange(
                            "o (p j) n -> (o p) (j n)", j=FJ)).then_inc(s_w[q], 16)

                over_groups(sp, group)

            @block.gpsimd
            def _(pool):
                def gather(n, q, first):
                    if not first:
                        pool.wait_ge(s_ys, n - RING + 1)
                    pool.sem_inc(s_passed, 1)
                    pool.tensor_copy(idx[:, q:q + 1], slots[:, bass.ds(n, 1)]).then_inc(s_idx, 1)
                    pool.wait_ge(s_idx, n + 1)
                    pool.sem_inc(s_passed, 1)
                    pool.indirect_dma_start(xg[:, q, :], None, table, bass.IndirectOffsetOnAxis(idx[:, q:q + 1], 0))\
                        .then_inc(s_xg[q], 16)

                def scatter(n, q, first):
                    if not first:
                        pool.wait_ge(s_sc, 16 * n)
                    pool.sem_inc(s_passed, 1)
                    pool.tensor_copy(idx_out[:, q:q + 1], slots[:, bass.ds(n, 1)]).then_inc(s_idxo, 1)
                    pool.wait_ge(s_idxo, n + 1)
                    pool.wait_ge(s_ys, n + 1)
                    pool.sem_inc(s_passed, 1)
                    pool.indirect_dma_start(out, bass.IndirectOffsetOnAxis(idx_out[:, q:q + 1], 0), ys[:, q % 2, :], None,
                                            compute_op=ALU.add).then_inc(s_sc, 16)

                def group(i, first, last):
                    for q in range(RING):
                        n = i * RING + q
                        if not last:
                            gather(n + RING, q, False)
                        scatter(n, q, first and q == 0)

                for q in range(RING):
                    gather(q, q, True)
                over_groups(pool, group)
                pool.wait_ge(s_sc, 16 * E)

            @block.scalar
            def _(act):
                def x_out(n, q):
                    act.wait_ge(s_xp, n + 1)
                    act.activation(xT[:, q % 2, :], XP[:, q % 2, :], ACT.Copy).then_inc(s_xT, 1)

                def y_out(n, q, first):
                    act.wait_ge(s_y, n + 1)
                    act.wait_ge(s_wt, n + 1)
                    if not first:
                        act.wait_ge(s_sc, 16 * (n - 1))
                    act.activation(ys[:, q % 2, :], YP[:, q % 2, :], ACT.Copy, scale=wt[:, q:q + 1]).then_inc(s_ys, 1)

                def group(i, first, last):
                    for q in range(RING):
                        n = i * RING + q
                        act.wait_ge(s_gu, n + 1)
                        act.activation(sg[:, q % 2, :], GU[:, q % 2, 0:FE], ACT.Silu).then_inc(s_sg, 1)
                        if not (last and q == RING - 1):
                            x_out(n + 1, (q + 1) % RING)
                        if not (first and q == 0):
                            y_out(n - 1, (q - 1) % RING, first and q <= 2)

                x_out(0, 0)
                over_groups(act, group)
                y_out(E - 1, RING - 1, False)

            @block.vector
            def _(dve):
                def group(i, first, last):
                    for q in range(RING):
                        n = i * RING + q
                        dve.wait_ge(s_xg[q], i * 16 + 16)
                        dve.tensor_copy(wt[:, q:q + 1], xg[:, q, bass.ds(n + D, 1)]).then_inc(s_wt, 1)
                        dve.wait_ge(s_sg, n + 1)
                        dve.tensor_tensor(hm[:, q % 2, :], sg[:, q % 2, :], GU[:, q % 2, FE:2 * FE], ALU.mult)\
                           .then_inc(s_hm, 1)
                        dve.wait_ge(s_hp, n + 1)
                        dve.tensor_copy(hT[:, q % 2, :], HP[0:FP, 0:FJ * P]).then_inc(s_hT, 1)

                over_groups(dve, group)

            @block.tensor
            def _(pe):
                pe.wait_ge(s_c, 16)

                def turn_x(n, q, turn):
                    pe.wait_ge(s_xg[q], turn * 16 + 16)
                    for k in range(KT):
                        ins = pe.transpose(XP[:, q % 2, k * P:(k + 1) * P], xg[:, q, k:D:KT], ident[:, :])
                    ins.then_inc(s_xp, 1)

                def down(n, q, first):
                    pe.wait_ge(s_hT, n + 1)
                    if not first:
                        pe.wait_ge(s_ys, n - 1)
                    for j in range(FJ):
                        ins = pe.matmul(YP[:, q % 2, :], hT[:, q % 2, j * P:(j + 1) * P],
                                        wd[:, q, j * D:(j + 1) * D], start=(j == 0), stop=(j == FJ - 1))
                    ins.then_inc(s_y, 1)

                def group(i, first, last):
                    for q in range(RING):
                        n = i * RING + q
                        pe.wait_ge(s_xT, n + 1)
                        pe.wait_ge(s_w[q], i * 48 + 48)
                        for k in range(KT):
                            ins = pe.matmul(GU[:, q % 2, 0:2 * FE].rearrange("p (m f) -> p m f", m=2),
                                            xT[:, q % 2, k * P:(k + 1) * P], wgu[:, q, :, k * FE:(k + 1) * FE],
                                            start=(k == 0), stop=(k == KT - 1))
                        ins.then_inc(s_gu, 1)
                        if not (last and q == RING - 1):
                            turn_x(n + 1, (q + 1) % RING, i + (q == RING - 1))
                        if not (first and q == 0):
                            down(n - 1, (q - 1) % RING, first and q <= 2)
                        pe.wait_ge(s_hm, n + 1)
                        for j in range(FJ):
                            ins = pe.transpose(HP[0:FP, j * P:(j + 1) * P], hm[:, q % 2, j:FE:FJ], ident[:, :])
                        ins.then_inc(s_hp, 1)

                turn_x(0, 0, 0)
                over_groups(pe, group)
                down(E - 1, RING - 1, False)


def transformer(nc, x, wqk, wvT, woT, lam, w1T, w3T, W2T, wr, wf, wc, wo, ln_scale, rwT, w_gate, w_up, w_down,
                ident, mask, had, rev, pcol, out):
    T = x.shape[0]
    batches = T // S
    chunks = T // D

    def scratch(name, shape):
        return nc.dram_tensor(name, shape, F32, kind="Internal").ap()

    w2p = scratch("w2_transformed", (HID, D))
    xt_hi, xt_lo = scratch("xt_hi", (chunks, P, KT, D)), scratch("xt_lo", (chunks, P, KT, D))
    x1, x1b, x2 = scratch("x_attn", (T, D)), scratch("x_half", (T, D)), scratch("x_layer0", (T, D))
    table = scratch("token_table", (T + P, ROW))
    logits = scratch("router_logits", (batches, P, NT * E))

    hadamard_w2(nc, W2T, had, w2p)
    with nc.cleanup_on_exit():
        attention(nc, x, wqk, wvT, woT, lam, ident, mask, xt_hi, xt_lo, x1, batches)
    dense_ffn(nc, w1T, w3T, w2p, xt_hi, xt_lo, x1, x1b, x2, chunks)
    recurrence(nc, wr, wf, wc, wo, ln_scale, rwT, ident, x2, table, logits, out, batches)
    with nc.sbuf_tensor("slots", [P, E], I32) as slots:
        routing(nc, logits, rev, pcol, ident, table, out, slots, batches)
        experts(nc, w_gate, w_up, w_down, ident, table, out, slots)


def by_partition(w):
    return np.ascontiguousarray(w.reshape(-1, P, w.shape[1]).transpose(1, 0, 2))


def kernel(**inputs):
    import concourse.bacc as _bacc
    from concourse.bass_utils import run_bass_kernel_spmd as _run

    a = {k: np.asarray(v) for k, v in inputs.items()}
    f32 = np.float32
    x = a["L0_attn_x"]
    B, _, _ = x.shape
    T = B * S
    wq, wk = a["L0_attn_wq"], a["L0_attn_wk"]

    def two(w, h):
        return [w[DH * h:DH * (h + 1)], w[DH * (h + HEADS):DH * (h + HEADS + 1)]]

    wqk = np.stack([by_partition(np.concatenate(two(wq, h) + two(wk, h), 0).T) for h in range(HEADS)])
    lam = np.stack([a["L0_attn_" + n] for n in ("l_q1", "l_k1", "l_q2", "l_k2")])
    rw = a["L1_ffn_router_w"]

    ident = np.eye(P, dtype=f32)
    query, key = np.arange(P)[:, None], np.arange(2 * P)[None]
    mask = np.concatenate([np.where(key > query + P * t, MASKED, 0.0) for t in range(2)], 1).astype(f32)
    had = np.ones((1, 1), f32)
    while had.shape[0] < P:
        had = np.block([[had, had], [had, -had]])
    rev = np.concatenate([np.tile(T - h * (T // 2) - np.arange(T // 2), (E, 1)) for h in range(2)], 0).astype(f32)
    pcol = np.arange(P, dtype=f32)[:, None]

    arrays = {
        "x": x.reshape(T, D),
        "wqk": wqk,
        "wvT": by_partition(a["L0_attn_wv"].T),
        "woT": by_partition(a["L0_attn_wo"].T),
        "lam": np.broadcast_to(lam, (P,) + lam.shape),
        "w1T": a["L0_ffn_W1"].T,
        "w3T": a["L0_ffn_W3"].T,
        "W2T": a["L0_ffn_W2"].T,
        "wr": by_partition(a["L1_attn_Wr"]),
        "wf": by_partition(a["L1_attn_Wf"]),
        "wc": by_partition(a["L1_attn_Wc"]),
        "wo": by_partition(a["L1_attn_Wo"]),
        "ln_scale": a["L1_attn_ln_scale"].reshape(KT, P).T,
        "rwT": by_partition(np.concatenate([rw, rw], 0).T),
        "w_gate": a["L1_ffn_w_gate"],
        "w_up": a["L1_ffn_w_up"],
        "w_down": a["L1_ffn_w_down"],
        "ident": ident, "mask": mask, "had": had, "rev": rev, "pcol": pcol,
    }
    nc = _bacc.Bacc("TRN2", target_bir_lowering=False, num_devices=1)
    sent, args = {}, {}
    for name, v in arrays.items():
        v = np.ascontiguousarray(v)
        sent[f"in_{name}_dram"] = v
        args[name] = nc.dram_tensor(f"in_{name}_dram", v.shape, mybir.dt.from_np(v.dtype), kind="ExternalInput").ap()
    out = nc.dram_tensor("out_0_dram", (T + P, D), F32, kind="ExternalOutput").ap()
    transformer(nc, out=out, **args)
    r = _run(nc, [sent], core_ids=[0])
    return r.results[0]["out_0_dram"][:T].reshape(B, S, D)
```
